# Optimizing a Trainium2 kernel written in Bass

```python
import numpy as np
import jax
import jax.numpy as jnp

def _softmax(x, axis=-1):
    return jax.nn.softmax(x, axis=axis)

def _gelu(x):
    return jax.nn.gelu(x, approximate=True)

def _silu(x):
    return jax.nn.silu(x)

def _sigmoid(x):
    return jax.nn.sigmoid(x)

def _layernorm(x, axis=-1, eps=1e-05):
    m = jnp.mean(x, axis=axis, keepdims=True)
    v = jnp.var(x, axis=axis, keepdims=True)
    return (x - m) / jnp.sqrt(v + eps)

def _scatter_add(tgt, idx, src, axis=0):
    return tgt.at[idx].add(src)

def _segment_sum(src, seg, n):
    return jax.ops.segment_sum(src, seg, n)
kernel_name = 'mk_gnn_preln_d2_gnn_r8_a8f625'

def setup_inputs(seed: int=0):
    np.random.seed(seed)
    _w = jnp.asarray

    def _rec_inputs():
        import jax
        import jax.numpy as jnp
        _gk = jax.random.key(seed)
        x = -0.0004287 + 1 * jax.random.normal(jax.random.fold_in(_gk, 1), (12500, 160), jnp.float32)
        src = jax.random.randint(jax.random.fold_in(_gk, 2), (200000,), 0, 12500, jnp.int32)
        dst = jnp.minimum((12500 * jax.random.uniform(jax.random.fold_in(_gk, 3), (200000,)) ** 2.0).astype(jnp.int32), 99999)
        _o = jnp.argsort(dst, stable=True)
        src = src[_o]
        dst = dst[_o]
        edge_attr_10 = jax.random.uniform(jax.random.fold_in(_gk, 12), (200000, 10), jnp.float32, 0.0, 1)
        edge_attr_3 = 0.00047201 + 1.00023 * jax.random.normal(jax.random.fold_in(_gk, 13), (200000, 3), jnp.float32)
        edge_attr_4 = 0.000486536 + 0.999406 * jax.random.normal(jax.random.fold_in(_gk, 14), (200000, 4), jnp.float32)
        edge_attr_64 = 0.000279952 + 1.00013 * jax.random.normal(jax.random.fold_in(_gk, 15), (200000, 64), jnp.float32)
        node_vec1 = -0.00786984 + 0.999612 * jax.random.normal(jax.random.fold_in(_gk, 17), (12500, 1), jnp.float32)
        node_vec1_n2 = -0.00786984 + 0.999612 * jax.random.normal(jax.random.fold_in(_gk, 18), (12500, 1), jnp.float32)
        node_vec1_n3 = -0.00786984 + 0.999612 * jax.random.normal(jax.random.fold_in(_gk, 19), (12500, 1), jnp.float32)
        return (x, src, dst, edge_attr_10, edge_attr_3, edge_attr_4, edge_attr_64, node_vec1, node_vec1_n2, node_vec1_n3)
    x, src, dst, edge_attr_10, edge_attr_3, edge_attr_4, edge_attr_64, node_vec1, node_vec1_n2, node_vec1_n3 = _rec_inputs()

    def _L0_gnn_setup():
        import jax, jax.numpy as jnp
        import numpy as np
        N = 3125
        E = 50000
        S = 64
        V = 32
        NB = 10
        H = 100
        WN = 192
        MID = 96
        NUM_NEIGHBORS = 16.0
        C_S = float(np.sin(np.pi / 8.0))
        C_X = float(np.cos(np.pi / 8.0))
        SQRT3 = float(np.sqrt(3.0))

        def fctp_scalar_attr(xs, xv, attr, Ws, Wv):
            s = xs * attr @ Ws
            v = jnp.einsum('nuc,uo->noc', xv * attr[:, :, None], Wv)
            return (s, v)
        key = jax.random.key(seed)
        k = jax.random.split(key, 24)

        def w(i, shape):
            return jax.random.normal(k[i], shape, jnp.float32) / np.sqrt(float(shape[0]))
        return {'node_input': jax.random.normal(k[0], (N, S + 3 * V), jnp.float32), 'node_attr': jax.random.normal(k[1], (N, 1), jnp.float32), 'node_crystal_attr': jax.random.normal(k[2], (N, 1), jnp.float32), 'sym_mask': jax.random.normal(k[3], (N, 1), jnp.float32), 'edge_attr': jax.random.normal(k[4], (E, 4), jnp.float32), 'edge_length_embedded': jax.random.uniform(k[5], (E, NB), dtype=jnp.float32), 'edge_src': jax.random.randint(k[6], (E,), 0, N), 'edge_dst': jax.random.randint(k[7], (E,), 0, N), 'Ws_sc_a': w(8, (S, S)), 'Wv_sc_a': w(9, (V, V)), 'Ws_sc_c': w(10, (S, S)), 'Wv_sc_c': w(11, (V, V)), 'Ws_l1_a': w(12, (S, S)), 'Wv_l1_a': w(13, (V, V)), 'Ws_l1_c': w(14, (S, S)), 'Wv_l1_c': w(15, (V, V)), 'W_fc1': w(16, (NB, H)), 'W_fc2': w(17, (H, WN)), 'Ws_l2_a': w(18, (MID, MID)), 'Wv_l2_a': w(19, (MID, MID)), 'Ws_l2_c': w(20, (MID, MID)), 'Wv_l2_c': w(21, (MID, MID)), 'Ws_l3': w(22, (MID, S)), 'Wv_l3': w(23, (MID, V))}
    _L0_gnn_all = _L0_gnn_setup()
    _L0_gnn_in = {k: v for k, v in _L0_gnn_all.items() if k in ('Ws_sc_a', 'Wv_sc_a', 'Ws_sc_c', 'Wv_sc_c', 'Ws_l1_a', 'Wv_l1_a', 'Ws_l1_c', 'Wv_l1_c', 'W_fc1', 'W_fc2', 'Ws_l2_a', 'Wv_l2_a', 'Ws_l2_c', 'Wv_l2_c', 'Ws_l3', 'Wv_l3')}
    del _L0_gnn_all

    def _L1_gnn_setup():
        import jax, jax.numpy as jnp
        import numpy as np
        N_NODES = 1250
        N_EDGES = 40000
        MUL0, MUL1 = (64, 32)
        EDGE_DIM = 64
        W_NUMEL = 224
        DENOM = 32.0
        SQRT3 = 3.0 ** 0.5
        INV_SQRT3 = 1.0 / SQRT3
        INV_SQRT2 = 2.0 ** (-0.5)

        def _forward(node_feature, edge_attr, edge_feature, W_skip0, W_skip1, W_nl0, W_nl1, W_fc1, W_fc2, W_out_s, W_out_v, edge_index):
            N = node_feature.shape[0]
            E = edge_attr.shape[0]
            s = node_feature[:, :MUL0]
            v = node_feature[:, MUL0:].reshape(N, MUL1, 3)
            skip_s = s @ W_skip0
            skip_v = jnp.einsum('nmi,mk->nki', v, W_skip1)
            s = s @ W_nl0
            v = jnp.einsum('nmi,mk->nki', v, W_nl1)
            rhat = edge_attr / jnp.linalg.norm(edge_attr, axis=-1, keepdims=True)
            sh1 = SQRT3 * rhat
            w = jax.nn.relu(edge_feature @ W_fc1) @ W_fc2
            w0, w1, w2, w3, w4 = jnp.split(w, [64, 128, 160, 192], axis=-1)
            src, dst = (edge_index[0], edge_index[1])
            xs = s[dst]
            xv = v[dst]
            out0a = w0 * xs
            out0b = w3 * (jnp.einsum('emi,ei->em', xv, sh1) * INV_SQRT3)
            out1a = (w1 * xs)[:, :, None] * sh1[:, None, :]
            out1b = w2[:, :, None] * xv
            out1c = w4[:, :, None] * (jnp.cross(xv, sh1[:, None, :]) * INV_SQRT2)
            tp = jnp.concatenate([out0a, out0b, out1a.reshape(E, -1), out1b.reshape(E, -1), out1c.reshape(E, -1)], axis=-1)
            agg = jax.ops.segment_sum(tp, src, num_segments=N) / DENOM
            agg_s = agg[:, :96]
            agg_v = agg[:, 96:].reshape(N, 128, 3)
            out_s = agg_s @ W_out_s + skip_s
            out_v = jnp.einsum('nmi,mk->nki', agg_v, W_out_v) + skip_v
            fs = jax.nn.silu(out_s[:, :MUL0])
            gate = jax.nn.sigmoid(out_s[:, MUL0:MUL0 + 32])
            gv = gate[:, :, None] * out_v
            return jnp.concatenate([fs, gv.reshape(N, -1)], axis=-1)
        key = jax.random.key(seed)
        ks = jax.random.split(key, 12)

        def lin(k, fi, fo):
            return jax.random.normal(k, (fi, fo), jnp.float32) / np.float32(np.sqrt(fi))
        return {'node_feature': jax.random.normal(ks[0], (N_NODES, MUL0 + 3 * MUL1), jnp.float32), 'edge_attr': jax.random.normal(ks[1], (N_EDGES, 3), jnp.float32), 'edge_feature': jax.random.normal(ks[2], (N_EDGES, EDGE_DIM), jnp.float32), 'W_skip0': lin(ks[3], MUL0, 96), 'W_skip1': lin(ks[4], MUL1, 32), 'W_nl0': lin(ks[5], MUL0, MUL0), 'W_nl1': lin(ks[6], MUL1, MUL1), 'W_fc1': lin(ks[7], EDGE_DIM, 64), 'W_fc2': lin(ks[8], 64, W_NUMEL), 'W_out_s': lin(ks[9], 96, 96), 'W_out_v': lin(ks[10], 128, 32), 'edge_index': jax.random.randint(ks[11], (2, N_EDGES), 0, N_NODES)}
    _L1_gnn_all = _L1_gnn_setup()
    _L1_gnn_in = {k: v for k, v in _L1_gnn_all.items() if k in ('W_skip0', 'W_skip1', 'W_nl0', 'W_nl1', 'W_fc1', 'W_fc2', 'W_out_s', 'W_out_v')}
    del _L1_gnn_all
    return {'x': x, 'src': src, 'dst': dst, 'edge_attr_10': edge_attr_10, 'edge_attr_3': edge_attr_3, 'edge_attr_4': edge_attr_4, 'edge_attr_64': edge_attr_64, 'node_vec1': node_vec1, 'node_vec1_n2': node_vec1_n2, 'node_vec1_n3': node_vec1_n3, 'L0_gnn_Ws_sc_a': _L0_gnn_in['Ws_sc_a'], 'L0_gnn_Wv_sc_a': _L0_gnn_in['Wv_sc_a'], 'L0_gnn_Ws_sc_c': _L0_gnn_in['Ws_sc_c'], 'L0_gnn_Wv_sc_c': _L0_gnn_in['Wv_sc_c'], 'L0_gnn_Ws_l1_a': _L0_gnn_in['Ws_l1_a'], 'L0_gnn_Wv_l1_a': _L0_gnn_in['Wv_l1_a'], 'L0_gnn_Ws_l1_c': _L0_gnn_in['Ws_l1_c'], 'L0_gnn_Wv_l1_c': _L0_gnn_in['Wv_l1_c'], 'L0_gnn_W_fc1': _L0_gnn_in['W_fc1'], 'L0_gnn_W_fc2': _L0_gnn_in['W_fc2'], 'L0_gnn_Ws_l2_a': _L0_gnn_in['Ws_l2_a'], 'L0_gnn_Wv_l2_a': _L0_gnn_in['Wv_l2_a'], 'L0_gnn_Ws_l2_c': _L0_gnn_in['Ws_l2_c'], 'L0_gnn_Wv_l2_c': _L0_gnn_in['Wv_l2_c'], 'L0_gnn_Ws_l3': _L0_gnn_in['Ws_l3'], 'L0_gnn_Wv_l3': _L0_gnn_in['Wv_l3'], 'L1_gnn_W_skip0': _L1_gnn_in['W_skip0'], 'L1_gnn_W_skip1': _L1_gnn_in['W_skip1'], 'L1_gnn_W_nl0': _L1_gnn_in['W_nl0'], 'L1_gnn_W_nl1': _L1_gnn_in['W_nl1'], 'L1_gnn_W_fc1': _L1_gnn_in['W_fc1'], 'L1_gnn_W_fc2': _L1_gnn_in['W_fc2'], 'L1_gnn_W_out_s': _L1_gnn_in['W_out_s'], 'L1_gnn_W_out_v': _L1_gnn_in['W_out_v']}

def reference(x, src, dst, edge_attr_10, edge_attr_3, edge_attr_4, edge_attr_64, node_vec1, node_vec1_n2, node_vec1_n3, L0_gnn_Ws_sc_a, L0_gnn_Wv_sc_a, L0_gnn_Ws_sc_c, L0_gnn_Wv_sc_c, L0_gnn_Ws_l1_a, L0_gnn_Wv_l1_a, L0_gnn_Ws_l1_c, L0_gnn_Wv_l1_c, L0_gnn_W_fc1, L0_gnn_W_fc2, L0_gnn_Ws_l2_a, L0_gnn_Wv_l2_a, L0_gnn_Ws_l2_c, L0_gnn_Wv_l2_c, L0_gnn_Ws_l3, L0_gnn_Wv_l3, L1_gnn_W_skip0, L1_gnn_W_skip1, L1_gnn_W_nl0, L1_gnn_W_nl1, L1_gnn_W_fc1, L1_gnn_W_fc2, L1_gnn_W_out_s, L1_gnn_W_out_v):
    import jax
    import jax.numpy as jnp

    def _L0_gnn_ref(node_input, node_attr, node_crystal_attr, sym_mask, edge_attr, edge_length_embedded, edge_src, edge_dst, Ws_sc_a, Wv_sc_a, Ws_sc_c, Wv_sc_c, Ws_l1_a, Wv_l1_a, Ws_l1_c, Wv_l1_c, W_fc1, W_fc2, Ws_l2_a, Wv_l2_a, Ws_l2_c, Wv_l2_c, Ws_l3, Wv_l3):
        import jax, jax.numpy as jnp
        import numpy as np
        N = 3125
        E = 50000
        S = 64
        V = 32
        NB = 10
        H = 100
        WN = 192
        MID = 96
        NUM_NEIGHBORS = 16.0
        C_S = float(np.sin(np.pi / 8.0))
        C_X = float(np.cos(np.pi / 8.0))
        SQRT3 = float(np.sqrt(3.0))

        def fctp_scalar_attr(xs, xv, attr, Ws, Wv):
            s = xs * attr @ Ws
            v = jnp.einsum('nuc,uo->noc', xv * attr[:, :, None], Wv)
            return (s, v)
        n = node_input.shape[0]
        xs = node_input[:, :S]
        xv = node_input[:, S:].reshape(n, V, 3)
        ssa, sva = fctp_scalar_attr(xs, xv, node_attr, Ws_sc_a, Wv_sc_a)
        ssc, svc = fctp_scalar_attr(xs, xv, node_crystal_attr, Ws_sc_c, Wv_sc_c)
        s_s, s_v = (ssa + ssc, sva + svc)
        l1a_s, l1a_v = fctp_scalar_attr(xs, xv, node_attr, Ws_l1_a, Wv_l1_a)
        l1c_s, l1c_v = fctp_scalar_attr(xs, xv, node_crystal_attr, Ws_l1_c, Wv_l1_c)
        x1s, x1v = (l1a_s + l1c_s, l1a_v + l1c_v)
        weight = jax.nn.silu(edge_length_embedded @ W_fc1) @ W_fc2
        w0 = weight[:, :S]
        w1 = weight[:, S:2 * S]
        w2 = weight[:, 2 * S:2 * S + V]
        w3 = weight[:, 2 * S + V:]
        gs = x1s[edge_src]
        gv = x1v[edge_src]
        e_s = edge_attr[:, :1]
        e_v = edge_attr[:, 1:]
        mid0a = w0 * gs * e_s
        mid0b = w3 * (jnp.einsum('euc,ec->eu', gv, e_v) / SQRT3)
        mid1a = w1[:, :, None] * gs[:, :, None] * e_v[:, None, :]
        mid1b = w2[:, :, None] * gv * e_s[:, :, None]
        edge_feat = jnp.concatenate([mid0a, mid0b, mid1a.reshape(-1, 3 * S), mid1b.reshape(-1, 3 * V)], axis=-1)
        agg = jax.ops.segment_sum(edge_feat, edge_dst, num_segments=n) / np.sqrt(NUM_NEIGHBORS)
        m_s = agg[:, :MID]
        m_v = agg[:, MID:].reshape(n, MID, 3)
        l2a_s, l2a_v = fctp_scalar_attr(m_s, m_v, node_attr, Ws_l2_a, Wv_l2_a)
        l2c_s, l2c_v = fctp_scalar_attr(m_s, m_v, node_crystal_attr, Ws_l2_c, Wv_l2_c)
        m_s, m_v = (l2a_s + l2c_s, l2a_v + l2c_v)
        o_s, o_v = fctp_scalar_attr(m_s, m_v, sym_mask, Ws_l3, Wv_l3)
        out_s = C_S * s_s + C_X * o_s
        out_v = C_S * s_v + C_X * o_v
        return jnp.concatenate([out_s, out_v.reshape(n, 3 * V)], axis=-1)

    def _L1_gnn_ref(node_feature, edge_attr, edge_feature, W_skip0, W_skip1, W_nl0, W_nl1, W_fc1, W_fc2, W_out_s, W_out_v, edge_index):
        import jax, jax.numpy as jnp
        import numpy as np
        N_NODES = 1250
        N_EDGES = 40000
        MUL0, MUL1 = (64, 32)
        EDGE_DIM = 64
        W_NUMEL = 224
        DENOM = 32.0
        SQRT3 = 3.0 ** 0.5
        INV_SQRT3 = 1.0 / SQRT3
        INV_SQRT2 = 2.0 ** (-0.5)

        def _forward(node_feature, edge_attr, edge_feature, W_skip0, W_skip1, W_nl0, W_nl1, W_fc1, W_fc2, W_out_s, W_out_v, edge_index):
            N = node_feature.shape[0]
            E = edge_attr.shape[0]
            s = node_feature[:, :MUL0]
            v = node_feature[:, MUL0:].reshape(N, MUL1, 3)
            skip_s = s @ W_skip0
            skip_v = jnp.einsum('nmi,mk->nki', v, W_skip1)
            s = s @ W_nl0
            v = jnp.einsum('nmi,mk->nki', v, W_nl1)
            rhat = edge_attr / jnp.linalg.norm(edge_attr, axis=-1, keepdims=True)
            sh1 = SQRT3 * rhat
            w = jax.nn.relu(edge_feature @ W_fc1) @ W_fc2
            w0, w1, w2, w3, w4 = jnp.split(w, [64, 128, 160, 192], axis=-1)
            src, dst = (edge_index[0], edge_index[1])
            xs = s[dst]
            xv = v[dst]
            out0a = w0 * xs
            out0b = w3 * (jnp.einsum('emi,ei->em', xv, sh1) * INV_SQRT3)
            out1a = (w1 * xs)[:, :, None] * sh1[:, None, :]
            out1b = w2[:, :, None] * xv
            out1c = w4[:, :, None] * (jnp.cross(xv, sh1[:, None, :]) * INV_SQRT2)
            tp = jnp.concatenate([out0a, out0b, out1a.reshape(E, -1), out1b.reshape(E, -1), out1c.reshape(E, -1)], axis=-1)
            agg = jax.ops.segment_sum(tp, src, num_segments=N) / DENOM
            agg_s = agg[:, :96]
            agg_v = agg[:, 96:].reshape(N, 128, 3)
            out_s = agg_s @ W_out_s + skip_s
            out_v = jnp.einsum('nmi,mk->nki', agg_v, W_out_v) + skip_v
            fs = jax.nn.silu(out_s[:, :MUL0])
            gate = jax.nn.sigmoid(out_s[:, MUL0:MUL0 + 32])
            gv = gate[:, :, None] * out_v
            return jnp.concatenate([fs, gv.reshape(N, -1)], axis=-1)
        return _forward(node_feature, edge_attr, edge_feature, W_skip0, W_skip1, W_nl0, W_nl1, W_fc1, W_fc2, W_out_s, W_out_v, edge_index)
    edge_index = jnp.stack([src, dst])
    h = jnp.maximum(_layernorm(x, axis=-1), 0.0)
    x = x + _L0_gnn_ref(h, node_vec1, node_vec1_n2, node_vec1_n3, edge_attr_4, edge_attr_10, src, dst, L0_gnn_Ws_sc_a, L0_gnn_Wv_sc_a, L0_gnn_Ws_sc_c, L0_gnn_Wv_sc_c, L0_gnn_Ws_l1_a, L0_gnn_Wv_l1_a, L0_gnn_Ws_l1_c, L0_gnn_Wv_l1_c, L0_gnn_W_fc1, L0_gnn_W_fc2, L0_gnn_Ws_l2_a, L0_gnn_Wv_l2_a, L0_gnn_Ws_l2_c, L0_gnn_Wv_l2_c, L0_gnn_Ws_l3, L0_gnn_Wv_l3)
    h = jnp.maximum(_layernorm(x, axis=-1), 0.0)
    x = x + _L1_gnn_ref(h, edge_attr_3, edge_attr_64, L1_gnn_W_skip0, L1_gnn_W_skip1, L1_gnn_W_nl0, L1_gnn_W_nl1, L1_gnn_W_fc1, L1_gnn_W_fc2, L1_gnn_W_out_s, L1_gnn_W_out_v, edge_index)
    return x

_drawn_inputs = setup_inputs


def setup_inputs(seed=0):
    import zlib

    import numpy as np

    out = dict(_drawn_inputs(seed))
    spreads = {}
    factors = {}
    for name, (base, spread) in spreads.items():
        noise = np.random.default_rng([zlib.crc32(name.encode()), seed]).standard_normal(out[name].shape)
        drawn = base * np.exp(spread * noise) if base else spread * noise
        out[name] = jnp.asarray(drawn.astype(out[name].dtype))
    for name, factor in factors.items():
        out[name] = (out[name] * factor).astype(out[name].dtype)
    return out
```

```python
import concourse.bass as bass
from concourse import mybir
from contextlib import ExitStack

F32 = mybir.dt.float32
I32 = mybir.dt.int32
BF16 = mybir.dt.bfloat16
ALU = mybir.AluOpType
ACT = mybir.ActivationFunctionType
AXX = mybir.AxisListType.X

P = 128
MS, MV = 64, 32
D = MS + 3 * MV
TILES = 4
G = TILES * P
RANKED = 5
UNROLL = 4
LN_EPS = 1e-5
OUT_OF_BOUNDS = 1 << 20
EA10, EA4, EA3, EA64, SRC, DST, POSB, ROW_A = 0, 10, 14, 17, 81, 82, 83, 84
B_EA3, B_EA64, B_SRC, B_DST, B_POS, B_NODE, ROW_B = 0, 3, 67, 68, 69, 70, 70 + D
H0, WN0, MID0 = 100, 192, 96
AGG0 = MID0 * 4
H1, WN1 = 64, 224
AGG1 = 96 + 3 * 128
C_S = 0.3826834323650898
C_X = 0.9238795325112867


def blocks_of(n_nodes):
    return 2 * (-(-n_nodes // (2 * P)))


def columns_of(n_edges):
    return 2 * RANKED * (-(-(n_edges + G) // (P * 2 * RANKED)))


def groups_of(n_edges, n_blocks):
    return UNROLL * (-(-(n_edges // G + n_blocks) // UNROLL))


class Names:

    def __init__(self, nc, ctx, stage):
        self.nc, self.ctx, self.stage, self.sems = nc, ctx, stage, []
        ctx.callback(self.clear)

    def sb(self, name, shape, dt=F32):
        return self.ctx.enter_context(self.nc.sbuf_tensor(f"{self.stage}_{name}", shape, dt))

    def ps(self, name, cols=512, dt=F32):
        return self.ctx.enter_context(self.nc.psum_tensor(f"{self.stage}_{name}", [P, cols], dt))

    def sem(self, name):
        self.sems.append(self.nc.alloc_semaphore(name=f"{self.stage}_{name}"))
        return self.sems[-1]

    def clear(self):
        self.nc.clear_and_free_semaphores(self.sems)
        self.nc.all_engine_barrier()


def loop_pairs(eng, n, body, peel=1, step=2):
    for k in range(min(peel, n // step)):
        for u in range(step):
            body(step * k + u, u, k)
    if n // step > peel:
        with eng.Fori(peel, n // step) as k:
            for u in range(step):
                body(k * step + u, u, k)


def bcast(ap, dim, count):
    shape = list(ap.shape)
    return ap.unsqueeze(dim).to_broadcast(shape[:dim] + [count] + shape[dim:])


def settle(eng, C):
    eng.sem_inc(C["settled"], 1)


def constants(nc, C):
    ctx = ExitStack()
    with ctx:
        a = Names(nc, ctx, "const")
        done, filled = a.sem("done"), a.sem("filled")
        block = ctx.enter_context(nc.Block())

        @block.gpsimd
        def _(pool):
            pool.memset(C["ident"][:, :], 0.0).then_inc(filled, 1)
            pool.memset(C["before"][:, :], 1.0).then_inc(filled, 1)
            pool.memset(C["not_before"][:, :], 1.0).then_inc(filled, 1)
            pool.memset(C["ones"][:, :], 1.0).then_inc(done, 1)
            pool.wait_ge(filled, 3)
            pool.affine_select(out=C["ident"][:, :], in_=C["ident"][:, :], compare_op=ALU.not_equal, fill=1.0,
                               base=0, pattern=[[-1, P]], channel_multiplier=1).then_inc(done, 1)
            pool.affine_select(out=C["before"][:, :], in_=C["before"][:, :], compare_op=ALU.is_gt, fill=0.0,
                               base=0, pattern=[[1, P]], channel_multiplier=-1).then_inc(done, 1)
            pool.affine_select(out=C["not_before"][:, :], in_=C["not_before"][:, :], compare_op=ALU.is_ge, fill=0.0,
                               base=0, pattern=[[-1, P]], channel_multiplier=1).then_inc(done, 1)
            nb = C["blocks"]
            pool.iota(C["block_ramp"][:, :], [[1, nb]], base=0, channel_multiplier=0,
                      allow_small_or_imprecise_dtypes=True).then_inc(done, 1)
            pool.iota(C["node_ramp"][:, :], [[1, P]], base=0, channel_multiplier=0,
                      allow_small_or_imprecise_dtypes=True).then_inc(done, 1)
            pool.wait_ge(done, 6)


def rank(nc, C, stage, key, cols, nb, pos_dram, count):
    W = RANKED * nb
    n = cols // RANKED
    ctx = ExitStack()
    with ctx:
        a = Names(nc, ctx, stage)
        keys = a.sb("keys", [P, cols], I32)
        of_block = a.sb("of_block", [P, cols], I32)
        blk = a.sb("blk", [P, cols], BF16)
        hot = [a.sb(f"hot{i}", [P, W], BF16) for i in range(2)]
        picked = [a.sb(f"picked{i}", [P, W]) for i in range(2)]
        place = a.sb("place", [P, cols])
        own = a.sb("own", [P, cols])
        padding = a.sb("padding", [P, cols])
        place_i = a.sb("place_i", [P, cols], I32)
        total = a.sb("total", [P, W])
        base = a.sb("base", [P, W])
        end = a.sb("end", [P, nb])
        zeros = a.sb("zeros", [P, nb])
        totals_ps = a.ps("totals")
        ranks_ps = a.ps("ranks")
        loaded, ch, iota_done = a.sem("loaded"), a.sem("chain"), a.sem("iota")
        hot1, summed1 = a.sem("hot_count"), a.sem("summed")
        base_ready, based = a.sem("base_ready"), a.sem("based")
        hot2, ranked, read, advanced = a.sem("hot_rank"), a.sem("ranked"), a.sem("read"), a.sem("advanced")
        reduced, stored = a.sem("reduced"), a.sem("stored")
        block = ctx.enter_context(nc.Block())

        @block.sync
        def _(sp):
            sp.dma_start(keys[:, :], key.rearrange("(p c) -> p c", p=P)).then_inc(loaded, 16)
            sp.wait_ge(stored, 1)
            sp.dma_start(pos_dram.rearrange("(p c) -> p c", p=P), place_i[:, :]).then_inc(loaded, 16)
            sp.wait_ge(loaded, 32)

        @block.gpsimd
        def _(pool):
            pool.iota(own[:, :], [[1, cols]], base=0, channel_multiplier=cols,
                      allow_small_or_imprecise_dtypes=True).then_inc(iota_done, 1)

        @block.tensor
        def _(pe):
            def count_batch(g, u, k):
                pe.wait_ge(hot1, g + 1)
                nc.tensor.matmul(totals_ps[:, 0:W], C["ones"][:, :], hot[u][:, :],
                                 start=before(g, 1), stop=isinstance(g, int) and g == n - 1).then_inc(summed1, 1)
            loop_pairs(pe, n - 2, count_batch)
            for g in (n - 2, n - 1):
                count_batch(g, g % 2, None)
            pe.wait_ge(base_ready, 1)
            nc.tensor.matmul(ranks_ps[:, 0:W], C["ident"][:, :], base[:, :], start=True, stop=True).then_inc(based, 1)

            def rank_batch(g, u, k):
                pe.wait_ge(hot2, g + 1)
                nc.tensor.matmul(ranks_ps[:, 0:W], C["before"][:, :], hot[u][:, :], start=False, stop=True,
                                 skip_group_check=True).then_inc(ranked, 1)
                pe.wait_ge(read, g + 1)
                nc.tensor.matmul(ranks_ps[:, 0:W], C["not_before"][:, :], hot[u][:, :], start=False, stop=True,
                                 skip_group_check=True).then_inc(advanced, 1)
            loop_pairs(pe, n, rank_batch)

        @block.vector
        def _(dve):
            chain = [0]

            def link(ins):
                chain[0] += 1
                ins.then_inc(ch, 1)
                dve.wait_ge(ch, chain[0])

            dve.wait_ge(loaded, 16)
            link(nc.vector.tensor_scalar(of_block[:, :], keys[:, :], 7, None, ALU.logical_shift_right))
            link(nc.vector.tensor_copy(blk[:, :], of_block[:, :]))

            def make_hot(g, u):
                return nc.vector.tensor_tensor(
                    hot[u][:, :].rearrange("p (c b) -> p c b", c=RANKED),
                    bcast(C["block_ramp"][:, :], 1, RANKED),
                    bcast(blk[:, bass.ds(g * RANKED, RANKED)], 2, nb), ALU.is_equal)

            def count_batch(g, u, k):
                if not (isinstance(g, int) and g < 2):
                    dve.wait_ge(summed1, g - 1)
                make_hot(g, u).then_inc(hot1, 1)
            loop_pairs(dve, n, count_batch)

            dve.wait_ge(summed1, n)
            link(nc.vector.tensor_copy(total[:, :], totals_ps[:, 0:W]))
            link(nc.vector.tensor_reduce(count[:, :], total[:, :].rearrange("p (c b) -> p b c", c=RANKED), AXX, ALU.add))
            link(nc.vector.memset(zeros[:, :], 0.0))
            link(nc.vector.tensor_tensor_scan(end[:, :], count[:, :], zeros[:, :], 0.0, ALU.add, ALU.add))
            link(nc.vector.tensor_tensor(base[:, 0:nb], end[:, :], count[:, :], ALU.subtract))
            for c in range(1, RANKED):
                ins = nc.vector.tensor_tensor(base[:, c * nb:(c + 1) * nb], base[:, (c - 1) * nb:c * nb],
                                              total[:, (c - 1) * nb:c * nb], ALU.add)
                if c < RANKED - 1:
                    link(ins)
                else:
                    ins.then_inc(base_ready, 1)

            def rank_batch(g, u, k):
                if not (isinstance(g, int) and g < 2):
                    dve.wait_ge(advanced, g - 1)
                make_hot(g, u).then_inc(hot2, 1)

            def read_batch(g, u, k):
                dve.wait_ge(ranked, g + 1)
                nc.vector.tensor_tensor(picked[u][:, :], ranks_ps[:, 0:W], hot[u][:, :], ALU.mult).then_inc(read, 1)

            def reduce_batch(g, u, k):
                dve.wait_ge(read, g + 1)
                nc.vector.tensor_reduce(place[:, bass.ds(g * RANKED, RANKED)],
                                        picked[u][:, :].rearrange("p (c b) -> p c b", c=RANKED),
                                        AXX, ALU.add).then_inc(reduced, 1)

            dve.wait_ge(based, 1)

            def step(g, u, k):
                if isinstance(g, int) and g == 0:
                    rank_batch(g, u, k)
                read_batch(g, u, k)
                if not (isinstance(g, int) and g == n - 1):
                    rank_batch(g + 1, 1 - u, k)
                reduce_batch(g, u, k)
            loop_pairs(dve, n - 2, step)
            for g in (n - 2, n - 1):
                step(g, g % 2, None)
            dve.wait_ge(iota_done, 1)
            dve.wait_ge(reduced, n)
            link(nc.vector.tensor_scalar(padding[:, :], blk[:, :], float(nb), None, ALU.is_ge))
            link(nc.vector.tensor_tensor(padding[:, :], padding[:, :], own[:, :], ALU.mult))
            nc.vector.tensor_tensor(place_i[:, :], place[:, :], padding[:, :], ALU.add).then_inc(stored, 1)


def group_table(nc, C, stage, count, nb, n_edges, ng, meta_dram, table, last):
    cols = -(-ng // P)
    ctx = ExitStack()
    with ctx:
        a = Names(nc, ctx, stage)
        up = a.sb("up", [P, nb], I32)
        groups_i = a.sb("groups_i", [P, nb], I32)
        groups = a.sb("groups", [P, nb])
        zeros = a.sb("zeros", [P, nb])
        end = a.sb("end", [P, nb])
        start = a.sb("start", [P, nb])
        slack = a.sb("slack", [P, nb])
        g_of = a.sb("g_of", [P, cols])
        junk = a.sb("junk", [P, nb])
        out = a.sb("out", [P, 3, cols])
        ch, iota_done, made, moved = a.sem("chain"), a.sem("iota"), a.sem("made"), a.sem("moved")
        block = ctx.enter_context(nc.Block())

        @block.gpsimd
        def _(pool):
            pool.iota(g_of[:, :], [[P, cols]], base=0, channel_multiplier=1,
                      allow_small_or_imprecise_dtypes=True).then_inc(iota_done, 1)

        @block.vector
        def _(dve):
            chain = [0]

            def link(ins):
                chain[0] += 1
                ins.then_inc(ch, 1)
                dve.wait_ge(ch, chain[0])

            link(nc.vector.tensor_scalar(up[:, :], count[:, :], float(G - 1), None, ALU.add))
            link(nc.vector.tensor_scalar(groups_i[:, :], up[:, :], G.bit_length() - 1, None, ALU.logical_shift_right))
            link(nc.vector.tensor_scalar(groups[:, :], groups_i[:, :], 1.0, None, ALU.max))
            link(nc.vector.memset(zeros[:, :], 0.0))
            link(nc.vector.tensor_tensor_scan(end[:, :], groups[:, :], zeros[:, :], 0.0, ALU.add, ALU.add))
            link(nc.vector.tensor_tensor(start[:, :], end[:, :], groups[:, :], ALU.subtract))
            link(nc.vector.scalar_tensor_tensor(slack[:, :], groups[:, :], float(-G), count[:, :], ALU.mult, ALU.add))
            link(nc.vector.tensor_scalar(last[:, :], end[0:1, :], -1.0, None, ALU.add))
            dve.wait_ge(iota_done, 1)
            for c in range(cols):
                g = g_of[:, c:c + 1]
                link(nc.vector.scalar_tensor_tensor(junk[:, :], end[:, :], g, slack[:, :], ALU.is_le, ALU.mult))
                link(nc.vector.tensor_reduce(out[:, 0, c:c + 1], junk[:, :], AXX, ALU.add))
                link(nc.vector.tensor_scalar(junk[:, :], end[:, :], g, float(P), ALU.is_le, ALU.mult))
                link(nc.vector.tensor_reduce(out[:, 1, c:c + 1], junk[:, :], AXX, ALU.add))
                link(nc.vector.tensor_scalar(junk[:, :], start[:, :], g, None, ALU.is_equal))
                link(nc.vector.tensor_reduce(out[:, 2, c:c + 1], junk[:, :], AXX, ALU.add))
            link(nc.vector.scalar_tensor_tensor(out[:, 0, :], g_of[:, :], float(G), out[:, 0, :], ALU.mult, ALU.add))
            link(nc.vector.tensor_scalar(out[:, 0, :], out[:, 0, :], float(n_edges), None, ALU.min))
            nc.vector.tensor_scalar(out[:, 2, :], out[:, 2, :], -1.0, 1.0, ALU.mult, ALU.add).then_inc(made, 1)

        @block.sync
        def _(sp):
            sp.wait_ge(made, 1)
            with nc.allow_non_contiguous_dma(reason="a table of a few hundred words"):
                for r in range(3):
                    sp.dma_start(meta_dram[r, :].rearrange("(c p) -> p c", p=P), out[:, r, :]).then_inc(moved, 16)
            sp.wait_ge(moved, 48)
            for r in range(3):
                sp.dma_start(table[:, r, :], meta_dram[r:r + 1, 0:ng].to_broadcast([P, ng])).then_inc(moved, 16)
            sp.wait_ge(moved, 96)


def to_destination_order(nc, C, attrs, src, dst, posa, posb, rows_a, cols):
    n = cols // RANKED
    ctx = ExitStack()
    with ctx:
        a = Names(nc, ctx, "pack")
        ids = a.sb("ids", [P, cols, 3], I32)
        place = a.sb("place", [P, cols], I32)
        one = [a.sb(f"one{i}", [P, cols], I32) for i in range(3)]
        row = [a.sb(f"row{i}", [P, RANKED, ROW_A]) for i in range(2)]
        at = [a.sb(f"at{i}", [P, RANKED], I32) for i in range(2)]
        loaded, ids_ready, packed = a.sem("loaded"), a.sem("ids_ready"), a.sem("packed")
        filled = [a.sem(f"filled{i}") for i in range(2)]
        scattered = [a.sem(f"scattered{i}") for i in range(2)]
        block = ctx.enter_context(nc.Block())
        attrs_v = attrs.rearrange("(p c) w -> p c w", p=P)

        @block.sync
        def _(sp):
            for i, x in enumerate((src, dst, posb)):
                sp.dma_start(one[i][:, :], x.rearrange("(p c) -> p c", p=P)).then_inc(loaded, 16)
            sp.dma_start(place[:, :], posa.rearrange("(p c) -> p c", p=P)).then_inc(loaded, 16)

            def load(g, u, k):
                if not (isinstance(g, int) and g < 2):
                    sp.wait_ge(scattered[u], k * (16 * RANKED))
                settle(sp, C)
                sp.dma_start(row[u][:, :, 0:SRC], attrs_v[:, bass.ds(g * RANKED, RANKED), :]).then_inc(filled[u], 16)
            loop_pairs(sp, n, load)

        @block.vector
        def _(dve):
            dve.wait_ge(loaded, 64)
            for i in range(3):
                nc.vector.tensor_copy(ids[:, :, i], one[i][:, :]).then_inc(ids_ready, 1)
            dve.wait_ge(ids_ready, 3)

            def pack(g, u, k):
                if not (isinstance(g, int) and g < 2):
                    dve.wait_ge(scattered[u], k * (16 * RANKED))
                nc.vector.tensor_copy(row[u][:, :, SRC:ROW_A].bitcast(I32), ids[:, bass.ds(g * RANKED, RANKED), :])\
                    .then_inc(packed, 1)
                nc.vector.tensor_copy(at[u][:, :], place[:, bass.ds(g * RANKED, RANKED)]).then_inc(packed, 1)
            loop_pairs(dve, n, pack)

        @block.gpsimd
        def _(pool):
            def scatter(g, u, k):
                pool.wait_ge(filled[u], k * 16 + 16)
                pool.wait_ge(packed, g * 2 + 2)
                settle(pool, C)
                for j in range(RANKED):
                    pool.indirect_dma_start(
                        out=rows_a, out_offset=bass.IndirectOffsetOnAxis(ap=at[u][:, j:j + 1], axis=0),
                        in_=row[u][:, j, :], in_offset=None).then_inc(scattered[u], 16)
            loop_pairs(pool, n, scatter)
            for u in range(2):
                pool.wait_ge(scattered[u], 16 * RANKED * (n // 2))


def before_gnn0(nc, C, x, attr, Wn, nb, x1, base):
    ctx = ExitStack()
    with ctx:
        a = Names(nc, ctx, "node0")
        xin = [a.sb(f"x{i}", [P, D]) for i in range(2)]
        at = [a.sb(f"attr{i}", [P, 3]) for i in range(2)]
        hs = [a.sb(f"h{i}", [P, D]) for i in range(2)]
        hT = [a.sb(f"hT{i}", [P, 2 * P]) for i in range(2)]
        o1 = [a.sb(f"x1_{i}", [P, D]) for i in range(2)]
        ob = [a.sb(f"base{i}", [P, D]) for i in range(2)]
        tmp = [a.sb(f"tmp{i}", [P, 2 * D]) for i in range(2)]
        st, mv, sd, rs = a.sb("st", [P, 6]), a.sb("mv", [P, 2]), a.sb("sd", [P, 1]), a.sb("rs", [P, 1])
        eps = a.sb("eps", [P, 1])
        tps = [a.ps(f"t{i}") for i in range(2)]
        sps = [a.ps(f"s{i}") for i in range(2)]
        vps = [a.ps(f"v{i}") for i in range(2)]
        ld = [a.sem(f"loaded{i}") for i in range(2)]
        stx = [a.sem(f"stored{i}") for i in range(2)]
        zero = a.sb("zero", [P, D])
        zero_ready, zero_out = a.sem("zero_ready"), a.sem("zero_out")
        ch, eps_ready, made_ch = a.sem("chain"), a.sem("eps_ready"), a.sem("mix_chain")
        var, root, h_ready, tr, ev, mm, made = (a.sem(s) for s in
                                                ("var", "root", "h_ready", "transposed", "evacuated", "mixed", "made"))
        block = ctx.enter_context(nc.Block())

        def rows(ap, b):
            return ap[bass.ds(b * P, P), :]

        @block.sync
        def _(sp):
            def step(b, u, k):
                if not (isinstance(b, int) and b < 2):
                    sp.wait_ge(made, b - 1)
                settle(sp, C)
                sp.dma_start(xin[u][:, :], rows(x, b)).then_inc(ld[u], 16)
                sp.dma_start(at[u][:, :], rows(attr, b)).then_inc(ld[u], 16)
            loop_pairs(sp, nb, step)

        @block.vector
        def _(dve):
            nc.vector.memset(eps[:, :], LN_EPS).then_inc(eps_ready, 1)
            nc.vector.memset(zero[:, :], 0.0).then_inc(zero_ready, 1)

            def norm(b, u, k):
                dve.wait_ge(ld[u], k * 32 + 32)
                nc.vector.bn_stats(st[:, :], xin[u][:, :]).then_inc(ch, 1)
                dve.wait_ge(ch, b * 3 + 1)
                settle(dve, C)
                nc.vector.bn_aggr(mv[:, :], st[:, :]).then_inc(var, 1)
                dve.wait_ge(root, b + 1)
                nc.vector.reciprocal(rs[:, :], sd[:, :]).then_inc(ch, 1)
                dve.wait_ge(ch, b * 3 + 2)
                if not (isinstance(b, int) and b < 2):
                    dve.wait_ge(tr, b - 1)
                nc.vector.tensor_scalar(hs[u][:, :], xin[u][:, :], mv[:, 0:1], rs[:, :], ALU.subtract, ALU.mult).then_inc(ch, 1)
                dve.wait_ge(ch, b * 3 + 3)
                nc.vector.tensor_scalar(hs[u][:, :], hs[u][:, :], 0.0, None, ALU.max).then_inc(h_ready, 1)

            def mix(b, u, k):
                dve.wait_ge(mm, b + 1)
                if not (isinstance(b, int) and b < 2):
                    dve.wait_ge(stx[u], k * 32)
                s4 = sps[u][:, 0:4 * MS].rearrange("p (l a f) -> p l a f", l=2, a=2)
                v4 = vps[u][:, 0:4 * 96].rearrange("p (l a f) -> p l a f", l=2, a=2)
                t2 = tmp[u][:, :].rearrange("p (l f) -> p l f", l=2)
                nc.vector.tensor_scalar(t2[:, :, 0:MS], s4[:, :, 0, :], at[u][:, 0:1], None, ALU.mult).then_inc(made_ch, 1)
                nc.vector.tensor_scalar(t2[:, :, MS:D], v4[:, :, 0, :], at[u][:, 0:1], None, ALU.mult).then_inc(made_ch, 1)
                dve.wait_ge(made_ch, b * 4 + 2)
                nc.vector.scalar_tensor_tensor(o1[u][:, 0:MS], s4[:, 0, 1, :], at[u][:, 1:2], t2[:, 0, 0:MS], ALU.mult, ALU.add)
                nc.vector.scalar_tensor_tensor(o1[u][:, MS:D], v4[:, 0, 1, :], at[u][:, 1:2], t2[:, 0, MS:D], ALU.mult, ALU.add)
                nc.vector.scalar_tensor_tensor(ob[u][:, 0:MS], s4[:, 1, 1, :], at[u][:, 1:2], t2[:, 1, 0:MS], ALU.mult, ALU.add).then_inc(made_ch, 1)
                nc.vector.scalar_tensor_tensor(ob[u][:, MS:D], v4[:, 1, 1, :], at[u][:, 1:2], t2[:, 1, MS:D], ALU.mult, ALU.add).then_inc(made_ch, 1)
                dve.wait_ge(made_ch, b * 4 + 4)
                nc.vector.tensor_tensor(ob[u][:, :], ob[u][:, :], xin[u][:, :], ALU.add).then_inc(made, 1)

            def step(b, u, k):
                norm(b, u, k)
                if isinstance(b, int) and b == 0:
                    return
                mix(b - 1, 1 - u, k if u else k - 1)
            loop_pairs(dve, nb, step)
            mix(nb - 1, 1, nb // 2 - 1)

        @block.scalar
        def _(act):
            act.wait_ge(eps_ready, 1)

            def step(b, u, k):
                act.wait_ge(var, b + 1)
                nc.scalar.activation(sd[:, :], mv[:, 1:2], ACT.Sqrt, bias=eps[:, :]).then_inc(root, 1)
                act.wait_ge(tr, b + 1)
                if not (isinstance(b, int) and b < 2):
                    act.wait_ge(mm, b - 1)
                nc.scalar.copy(hT[u][0:MS, 0:P], tps[u][0:MS, 0:P])
                nc.scalar.copy(hT[u][0:96, P:2 * P], tps[u][0:96, P:2 * P]).then_inc(ev, 1)
            loop_pairs(act, nb, step)

        @block.tensor
        def _(pe):
            def step(b, u, k):
                pe.wait_ge(h_ready, b + 1)
                if not (isinstance(b, int) and b < 2):
                    pe.wait_ge(ev, b - 1)
                settle(pe, C)
                nc.tensor.transpose(tps[u][0:MS, 0:P], hs[u][:, 0:MS], C["ident"][:, :])
                nc.tensor.transpose(tps[u][0:96, P:2 * P], hs[u][:, MS:D], C["ident"][:, :]).then_inc(tr, 1)
                pe.wait_ge(ev, b + 1)
                if not (isinstance(b, int) and b < 2):
                    pe.wait_ge(made, b - 1)
                settle(pe, C)
                nc.tensor.matmul(sps[u][:, 0:4 * MS], hT[u][0:MS, 0:P], Wn["s0"][0:MS, :], start=True, stop=True)
                nc.tensor.matmul(vps[u][:, 0:4 * 96], hT[u][0:96, P:2 * P], Wn["v0"][0:96, :], start=True, stop=True).then_inc(mm, 1)
            loop_pairs(pe, nb, step)

        @block.gpsimd
        def _(pool):
            pool.wait_ge(zero_ready, 1)
            pool.dma_start(x1[nb * P:(nb + 1) * P, :], zero[:, :]).then_inc(zero_out, 16)
            pool.wait_ge(zero_out, 16)

            def step(b, u, k):
                pool.wait_ge(made, b + 1)
                settle(pool, C)
                pool.dma_start(rows(x1, b), o1[u][:, :]).then_inc(stx[u], 16)
                pool.dma_start(rows(base, b), ob[u][:, :]).then_inc(stx[u], 16)
            loop_pairs(pool, nb, step)
            for u in range(2):
                pool.wait_ge(stx[u], 32 * (nb // 2))


def prepare_weights(nc, C, Wd, Wn):
    ctx = ExitStack()
    with ctx:
        a = Names(nc, ctx, "weights")
        l2 = {k: a.sb(f"l2{k}", [96, 96]) for k in ("sa", "sc", "va", "vc")}
        l3s, l3v = a.sb("l3s", [96, MS]), a.sb("l3v", [96, MV])
        l2T = a.sb("l2T", [96, 4 * 96])
        tps, mps = a.ps("t"), a.ps("m")
        zeroed, loaded, scaled, tr, ev, mm = (a.sem(s) for s in ("zeroed", "loaded", "scaled", "tr", "ev", "mm"))
        block = ctx.enter_context(nc.Block())
        loads = []
        for i, m in enumerate(("Ws_l1_a", "Ws_l1_c", "Ws_sc_a", "Ws_sc_c")):
            loads.append((Wn["s0"][0:MS, i * MS:(i + 1) * MS], Wd["L0_gnn_" + m][:, :]))
        for i, m in enumerate(("Wv_l1_a", "Wv_l1_c", "Wv_sc_a", "Wv_sc_c")):
            for c in range(3):
                loads.append((Wn["v0"][c * MV:(c + 1) * MV, i * 96 + c * MV:i * 96 + (c + 1) * MV], Wd["L0_gnn_" + m][:, :]))
        loads.append((Wn["fc1_0"][0:10, :], Wd["L0_gnn_W_fc1"][:, :]))
        for to, of, n in ((0, 0, MS), (MS, 2 * MS, MV), (MS + MV, MS, MS), (2 * MS + MV, 2 * MS + MV, MV)):
            loads.append((Wn["fc2_0"][0:H0, to:to + n], Wd["L0_gnn_W_fc2"][:, of:of + n]))
        for k, m in (("sa", "Ws_l2_a"), ("sc", "Ws_l2_c"), ("va", "Wv_l2_a"), ("vc", "Wv_l2_c")):
            loads.append((l2[k][:, :], Wd["L0_gnn_" + m][:, :]))
        loads.append((l3s[:, :], Wd["L0_gnn_Ws_l3"][:, :]))
        loads.append((l3v[:, :], Wd["L0_gnn_Wv_l3"][:, :]))
        loads.append((Wn["s1"][0:MS, 0:MS], Wd["L1_gnn_W_nl0"][:, :]))
        loads.append((Wn["s1"][0:MS, MS:MS + 96], Wd["L1_gnn_W_skip0"][:, :]))
        for i, m in enumerate(("W_nl1", "W_skip1")):
            for c in range(3):
                loads.append((Wn["v1"][c * MV:(c + 1) * MV, i * 96 + c * MV:i * 96 + (c + 1) * MV], Wd["L1_gnn_" + m][:, :]))
        loads.append((Wn["fc1_1"][0:64, :], Wd["L1_gnn_W_fc1"][:, :]))
        loads.append((Wn["fc2_1"][0:H1, :], Wd["L1_gnn_W_fc2"][:, :]))
        loads.append((Wn["outs"][0:96, :], Wd["L1_gnn_W_out_s"][:, :]))
        loads.append((Wn["outv"][:, :], Wd["L1_gnn_W_out_v"][:, :]))

        @block.sync
        def _(sp):
            sp.wait_ge(zeroed, 2)
            for to, of in loads:
                sp.dma_start(to, of).then_inc(loaded, 16)

        @block.vector
        def _(dve):
            nc.vector.memset(Wn["v0"][:, :], 0.0).then_inc(zeroed, 1)
            nc.vector.memset(Wn["v1"][:, :], 0.0).then_inc(zeroed, 1)
            dve.wait_ge(loaded, 16 * len(loads))
            for w, f in ((Wn["s0"][0:MS, 2 * MS:4 * MS], C_S), (Wn["v0"][0:96, 2 * 96:4 * 96], C_S),
                         (Wn["fc2_0"][0:H0, 2 * MS + MV:WN0], 3.0 ** -0.5), (Wn["fc2_1"][0:H1, 160:192], 3.0 ** -0.5),
                         (Wn["fc2_1"][0:H1, 192:224], 2.0 ** -0.5), (Wn["outs"][0:96, :], 1 / 32.0),
                         (Wn["outv"][:, :], 1 / 32.0)):
                nc.vector.tensor_scalar(w, w, f, None, ALU.mult).then_inc(scaled, 1)
            dve.wait_ge(tr, 1)
            nc.vector.tensor_copy(l2T[:, :], tps[0:96, 0:4 * 96]).then_inc(ev, 1)
            dve.wait_ge(mm, 1)
            nc.vector.tensor_scalar(Wn["ps"][0:96, :], mps[0:96, 0:2 * MS], C_X / 4.0, None, ALU.mult).then_inc(scaled, 1)
            nc.vector.tensor_scalar(Wn["pv"][0:96, :], mps[0:96, 2 * MS:2 * MS + 2 * MV], C_X / 4.0, None, ALU.mult).then_inc(scaled, 1)
            dve.wait_ge(scaled, 9)

        @block.tensor
        def _(pe):
            pe.wait_ge(loaded, 16 * len(loads))
            for i, k in enumerate(("sa", "sc", "va", "vc")):
                last = nc.tensor.transpose(tps[0:96, i * 96:(i + 1) * 96], l2[k][:, :], C["ident"][0:96, 0:96])
            last.then_inc(tr, 1)
            pe.wait_ge(ev, 1)
            at = 0
            for i, w, n in ((0, l3s, MS), (1, l3s, MS), (2, l3v, MV), (3, l3v, MV)):
                last = nc.tensor.matmul(mps[0:96, at:at + n], l2T[:, i * 96:(i + 1) * 96], w[:, :], start=True, stop=True)
                at += n
            last.then_inc(mm, 1)


def between(nc, C, agg, last, base, attr, Wn, nb, x2, sv, skip):
    ctx = ExitStack()
    with ctx:
        a = Names(nc, ctx, "node1")
        def two(name, shape):
            return [a.sb(f"{name}{i}", shape) for i in range(2)]
        ag, bs, at, am = two("agg", [P, AGG0]), two("base", [P, D]), two("attr", [P, 3]), two("am", [P, 2])
        mT, hT, hs = two("mT", [P, 4 * P]), two("hT", [P, 2 * P]), two("h", [P, D])
        xo, so, ko = two("x2", [P, D]), two("sv", [P, D]), two("skip", [P, 192])
        st, mv, sd, rs = a.sb("st", [P, 6]), a.sb("mv", [P, 2]), a.sb("sd", [P, 1]), a.sb("rs", [P, 1])
        eps = a.sb("eps", [P, 1])
        mps, ops = [a.ps(f"m{i}") for i in range(2)], [a.ps(f"o{i}") for i in range(2)]
        hps, kps = a.ps("h"), [a.ps(f"k{i}") for i in range(2)]
        ld = [a.sem(f"loaded{i}") for i in range(2)]
        stx = [a.sem(f"stored{i}") for i in range(2)]
        ch, eps_ready, x2_ready = a.sem("chain"), a.sem("eps_ready"), a.sem("x2_ready")
        mtr, mev, mmm, var, root, h_ready, htr, hev, hmm, made = (
            a.sem(s) for s in ("mtr", "mev", "mmm", "var", "root", "h_ready", "htr", "hev", "hmm", "made"))
        block = ctx.enter_context(nc.Block())
        agg_rows = agg.rearrange("g p f -> (g p) f")

        def rows(ap, b):
            return ap[bass.ds(b * P, P), :]

        @block.sync
        def _(sp):
            def step(b, u, k):
                if not (isinstance(b, int) and b < 2):
                    sp.wait_ge(made, b - 1)
                settle(sp, C)
                g = sp.value_load(last[0:1, bass.ds(b, 1)], min_val=0, max_val=agg.shape[0] - 1)
                sp.dma_start(ag[u][:, :], agg_rows[bass.ds(g * P, P), :]).then_inc(ld[u], 16)
                sp.dma_start(bs[u][:, :], rows(base, b)).then_inc(ld[u], 16)
                sp.dma_start(at[u][:, :], rows(attr, b)).then_inc(ld[u], 16)
            loop_pairs(sp, nb, step)

        @block.vector
        def _(dve):
            nc.vector.memset(eps[:, :], LN_EPS).then_inc(eps_ready, 1)

            def step(b, u, k):
                dve.wait_ge(ld[u], k * 48 + 48)
                nc.vector.tensor_scalar(am[u][:, :], at[u][:, 0:2], at[u][:, 2:3], None, ALU.mult).then_inc(ch, 1)
                dve.wait_ge(mmm, b + 1)
                dve.wait_ge(ch, b * 8 + 1)
                if not (isinstance(b, int) and b < 2):
                    dve.wait_ge(stx[u], k * 48)
                s2 = ops[u][:, 0:2 * MS].rearrange("p (a f) -> p a f", a=2)
                v2 = ops[u][:, 2 * MS:2 * MS + 6 * MV].rearrange("p (c a f) -> p a c f", c=3, a=2)
                xv = xo[u][:, MS:D].rearrange("p (c f) -> p c f", c=3)
                bv = bs[u][:, MS:D].rearrange("p (c f) -> p c f", c=3)
                nc.vector.scalar_tensor_tensor(xo[u][:, 0:MS], s2[:, 0, :], am[u][:, 0:1], bs[u][:, 0:MS], ALU.mult, ALU.add).then_inc(ch, 1)
                nc.vector.scalar_tensor_tensor(xv, v2[:, 0, :, :], am[u][:, 0:1], bv, ALU.mult, ALU.add).then_inc(ch, 1)
                dve.wait_ge(ch, b * 8 + 3)
                nc.vector.scalar_tensor_tensor(xo[u][:, 0:MS], s2[:, 1, :], am[u][:, 1:2], xo[u][:, 0:MS], ALU.mult, ALU.add).then_inc(ch, 1)
                nc.vector.scalar_tensor_tensor(xv, v2[:, 1, :, :], am[u][:, 1:2], xv, ALU.mult, ALU.add).then_inc(ch, 1)
                dve.wait_ge(ch, b * 8 + 5)
                nc.vector.bn_stats(st[:, :], xo[u][:, :]).then_inc(ch, 1)
                dve.wait_ge(ch, b * 8 + 6)
                settle(dve, C)
                nc.vector.bn_aggr(mv[:, :], st[:, :]).then_inc(var, 1)
                dve.wait_ge(root, b + 1)
                nc.vector.reciprocal(rs[:, :], sd[:, :]).then_inc(ch, 1)
                dve.wait_ge(ch, b * 8 + 7)
                nc.vector.tensor_scalar(hs[u][:, :], xo[u][:, :], mv[:, 0:1], rs[:, :], ALU.subtract, ALU.mult).then_inc(ch, 1)
                dve.wait_ge(ch, b * 8 + 8)
                nc.vector.tensor_scalar(hs[u][:, :], hs[u][:, :], 0.0, None, ALU.max).then_inc(h_ready, 1)
            loop_pairs(dve, nb, step)

        @block.scalar
        def _(act):
            act.wait_ge(eps_ready, 1)

            def close(b, u, k):
                act.wait_ge(htr, b + 1)
                nc.scalar.copy(hT[u][0:MS, 0:P], hps[0:MS, 0:P])
                nc.scalar.copy(hT[u][0:96, P:2 * P], hps[0:96, P:2 * P]).then_inc(hev, 1)
                act.wait_ge(hmm, b + 1)
                nc.scalar.copy(so[u][:, 0:MS], kps[u][:, 0:MS])
                nc.scalar.copy(ko[u][:, 0:96], kps[u][:, MS:MS + 96])
                nc.scalar.copy(so[u][:, MS:D], kps[u][:, 160:256])
                nc.scalar.copy(ko[u][:, 96:192], kps[u][:, 256:352]).then_inc(made, 1)

            def step(b, u, k):
                act.wait_ge(mtr, b + 1)
                nc.scalar.copy(mT[u][0:96, :], mps[u][0:96, :]).then_inc(mev, 1)
                act.wait_ge(var, b + 1)
                nc.scalar.activation(sd[:, :], mv[:, 1:2], ACT.Sqrt, bias=eps[:, :]).then_inc(root, 1)
                if not (isinstance(b, int) and b < 2):
                    act.wait_ge(stx[u], k * 48)
                close(b, u, k)
            loop_pairs(act, nb, step)

        @block.tensor
        def _(pe):
            def open_(b, u, k):
                pe.wait_ge(ld[u], k * 48 + 48)
                if not (isinstance(b, int) and b < 2):
                    pe.wait_ge(mev, b - 1)
                for c in range(4):
                    last_ = nc.tensor.transpose(mps[u][0:96, c * P:(c + 1) * P], ag[u][:, c * 96:(c + 1) * 96], C["ident"][:, :])
                last_.then_inc(mtr, 1)
                pe.wait_ge(mev, b + 1)
                if not (isinstance(b, int) and b < 2):
                    pe.wait_ge(h_ready, b - 1)
                nc.tensor.matmul(ops[u][:, 0:2 * MS], mT[u][0:96, 0:P], Wn["ps"][0:96, :], start=True, stop=True)
                for c in range(3):
                    last_ = nc.tensor.matmul(ops[u][:, 2 * MS + c * 2 * MV:2 * MS + (c + 1) * 2 * MV],
                                             mT[u][0:96, (c + 1) * P:(c + 2) * P], Wn["pv"][0:96, :], start=True, stop=True)
                last_.then_inc(mmm, 1)

            def close(b, u, k):
                pe.wait_ge(h_ready, b + 1)
                if not (isinstance(b, int) and b < 1):
                    pe.wait_ge(hev, b)
                settle(pe, C)
                nc.tensor.transpose(hps[0:MS, 0:P], hs[u][:, 0:MS], C["ident"][:, :])
                nc.tensor.transpose(hps[0:96, P:2 * P], hs[u][:, MS:D], C["ident"][:, :]).then_inc(htr, 1)
                pe.wait_ge(hev, b + 1)
                if not (isinstance(b, int) and b < 2):
                    pe.wait_ge(made, b - 1)
                settle(pe, C)
                nc.tensor.matmul(kps[u][:, 0:160], hT[u][0:MS, 0:P], Wn["s1"][0:MS, :], start=True, stop=True)
                nc.tensor.matmul(kps[u][:, 160:352], hT[u][0:96, P:2 * P], Wn["v1"][0:96, :], start=True, stop=True).then_inc(hmm, 1)

            def step(b, u, k):
                open_(b, u, k)
                close(b, u, k)
            loop_pairs(pe, nb, step)

        @block.gpsimd
        def _(pool):
            def step(b, u, k):
                pool.wait_ge(made, b + 1)
                settle(pool, C)
                pool.dma_start(rows(x2, b), xo[u][:, :]).then_inc(stx[u], 16)
                pool.dma_start(rows(sv, b), so[u][:, :]).then_inc(stx[u], 16)
                pool.dma_start(rows(skip, b), ko[u][:, :]).then_inc(stx[u], 16)
            loop_pairs(pool, nb, step)
            for u in range(2):
                pool.wait_ge(stx[u], 48 * (nb // 2))


def after_gnn1(nc, C, agg, last, x2, skip, Wn, nb, out):
    ctx = ExitStack()
    with ctx:
        a = Names(nc, ctx, "node2")
        def two(name, shape):
            return [a.sb(f"{name}{i}", shape) for i in range(2)]
        ag, xs, ks = two("agg", [P, AGG1]), two("x2", [P, D]), two("skip", [P, 192])
        mT, pre, sg, tm, ot = two("mT", [P, 4 * P]), two("pre", [P, 192]), two("sg", [P, 96]), two("tm", [P, D]), two("out", [P, D])
        mps, ops = [a.ps(f"m{i}") for i in range(2)], [a.ps(f"o{i}") for i in range(2)]
        ld = [a.sem(f"loaded{i}") for i in range(2)]
        stx = [a.sem(f"stored{i}") for i in range(2)]
        mtr, mev, mmm, pre_ready, sig, ch, made = (a.sem(s) for s in ("mtr", "mev", "mmm", "pre_ready", "sig", "chain", "made"))
        block = ctx.enter_context(nc.Block())
        agg_rows = agg.rearrange("g p f -> (g p) f")

        def rows(ap, b):
            return ap[bass.ds(b * P, P), :]

        @block.sync
        def _(sp):
            def step(b, u, k):
                if not (isinstance(b, int) and b < 2):
                    sp.wait_ge(made, b - 1)
                settle(sp, C)
                g = sp.value_load(last[0:1, bass.ds(b, 1)], min_val=0, max_val=agg.shape[0] - 1)
                sp.dma_start(ag[u][:, :], agg_rows[bass.ds(g * P, P), :]).then_inc(ld[u], 16)
                sp.dma_start(xs[u][:, :], rows(x2, b)).then_inc(ld[u], 16)
                sp.dma_start(ks[u][:, :], rows(skip, b)).then_inc(ld[u], 16)
            loop_pairs(sp, nb, step)

        @block.vector
        def _(dve):
            def step(b, u, k):
                dve.wait_ge(mmm, b + 1)
                nc.vector.tensor_tensor(pre[u][:, :], ops[u][:, 0:192], ks[u][:, :], ALU.add).then_inc(pre_ready, 1)
                dve.wait_ge(sig, b + 1)
                if not (isinstance(b, int) and b < 2):
                    dve.wait_ge(stx[u], k * 16)
                nc.vector.tensor_tensor(tm[u][:, 0:MS], pre[u][:, 0:MS], sg[u][:, 0:MS], ALU.mult).then_inc(ch, 1)
                nc.vector.tensor_tensor(tm[u][:, MS:D].rearrange("p (c f) -> p c f", c=3),
                                        pre[u][:, 96:192].rearrange("p (c f) -> p c f", c=3),
                                        bcast(sg[u][:, MS:96], 1, 3), ALU.mult).then_inc(ch, 1)
                dve.wait_ge(ch, b * 2 + 2)
                nc.vector.tensor_tensor(ot[u][:, :], tm[u][:, :], xs[u][:, :], ALU.add).then_inc(made, 1)
            loop_pairs(dve, nb, step)

        @block.scalar
        def _(act):
            def step(b, u, k):
                act.wait_ge(mtr, b + 1)
                nc.scalar.copy(mT[u][0:96, 0:P], mps[u][0:96, 0:P])
                nc.scalar.copy(mT[u][:, P:4 * P], mps[u][:, P:4 * P]).then_inc(mev, 1)
                act.wait_ge(pre_ready, b + 1)
                nc.scalar.activation(sg[u][:, :], pre[u][:, 0:96], ACT.Sigmoid).then_inc(sig, 1)
            loop_pairs(act, nb, step)

        @block.tensor
        def _(pe):
            def step(b, u, k):
                pe.wait_ge(ld[u], k * 48 + 48)
                if not (isinstance(b, int) and b < 2):
                    pe.wait_ge(mev, b - 1)
                nc.tensor.transpose(mps[u][0:96, 0:P], ag[u][:, 0:96], C["ident"][:, :])
                for c in range(3):
                    last_ = nc.tensor.transpose(mps[u][:, (c + 1) * P:(c + 2) * P], ag[u][:, 96 + c * 128:96 + (c + 1) * 128], C["ident"][:, :])
                last_.then_inc(mtr, 1)
                pe.wait_ge(mev, b + 1)
                if not (isinstance(b, int) and b < 2):
                    pe.wait_ge(pre_ready, b - 1)
                nc.tensor.matmul(ops[u][:, 0:96], mT[u][0:96, 0:P], Wn["outs"][0:96, :], start=True, stop=True)
                for c in range(3):
                    last_ = nc.tensor.matmul(ops[u][:, 96 + c * MV:96 + (c + 1) * MV], mT[u][:, (c + 1) * P:(c + 2) * P],
                                             Wn["outv"][:, :], start=True, stop=True)
                last_.then_inc(mmm, 1)
            loop_pairs(pe, nb, step)

        @block.gpsimd
        def _(pool):
            def step(b, u, k):
                pool.wait_ge(made, b + 1)
                settle(pool, C)
                pool.dma_start(rows(out, b), ot[u][:, :]).then_inc(stx[u], 16)
            loop_pairs(pool, nb, step)
            for u in range(2):
                pool.wait_ge(stx[u], 16 * (nb // 2))


def before(index, n):
    return isinstance(index, int) and index < n


def edges_gnn0(nc, C, rows_a, x1, table, row0, Wn, ng, agg):
    U = UNROLL
    ctx = ExitStack()
    with ctx:
        a = Names(nc, ctx, "edge0")
        row = [a.sb(f"row{i}", [P, TILES, ROW_A]) for i in range(U)]
        src = [a.sb(f"src{i}", [P, TILES], I32) for i in range(U)]
        gath = [a.sb(f"gath{i}", [P, TILES, D]) for i in range(U)]
        eT, hid = a.sb("eT", [16, G]), a.sb("hid", [P, G])
        es = [a.sb(f"es{i}", [P, TILES, 96]) for i in range(2)]
        hot = [a.sb(f"hot{i}", [P, TILES, P]) for i in range(2)]
        msg = [a.sb(f"msg{i}", [P, TILES, AGG0]) for i in range(2)]
        local = a.sb("local", [P, TILES])
        ws = a.sb("ws", [P, TILES, MS])
        dots = a.sb("dots", [P, TILES, 3, MV])
        dot = a.sb("dot", [P, TILES, MV])
        acc = [a.sb(f"acc{i}", [P, AGG0]) for i in range(U)]
        tps, hps = a.ps("t"), a.ps("h")
        wps = [[a.ps(f"w{i}{j}") for j in range(2)] for i in range(2)]
        aps = [a.ps(f"a{i}") for i in range(2)]
        row_in = [a.sem(f"row_in{i}") for i in range(U)]
        gath_in = [a.sem(f"gath_in{i}") for i in range(U)]
        acc_out = [a.sem(f"acc_out{i}") for i in range(U)]
        tr, ev, fc1, act1, w_ready, es_ready = (a.sem(s) for s in ("tr", "ev", "fc1", "act1", "w_ready", "es_ready"))
        src_ready, msg_ready, summed, acc_ready, ch, zeroed = (
            a.sem(s) for s in ("src_ready", "msg_ready", "summed", "acc_ready", "chain", "zeroed"))
        block = ctx.enter_context(nc.Block())
        agg_rows = agg.rearrange("g p f -> (g p) f")

        @block.sync
        def _(sp):
            def store(g, u):
                sp.wait_ge(acc_ready, g + 1)
                settle(sp, C)
                sp.dma_start(agg_rows[bass.ds(g * P, P), :], acc[u][:, :]).then_inc(acc_out[u], 16)

            def step(g, u, k):
                if not before(g, 5):
                    store(g - 5, (u - 5) % U)
                if not before(g, U):
                    sp.wait_ge(msg_ready, g - (U - 1))
                settle(sp, C)
                r = sp.value_load(row0[0:1, bass.ds(g, 1)], min_val=0, max_val=rows_a.shape[0] - G)
                sp.dma_start(row[u][:, :, :].rearrange("p j w -> p (j w)"),
                             rows_a[bass.ds(r, G), :].rearrange("(p j) w -> p (j w)", p=P)).then_inc(row_in[u], 16)
            loop_pairs(sp, ng, step, peel=2, step=U)
            for g in range(ng - 5, ng):
                store(g, g % U)
            for u in range(U):
                sp.wait_ge(acc_out[u], 16 * (ng // U))

        @block.gpsimd
        def _(pool):
            def step(g, u, k):
                pool.wait_ge(row_in[u], k * 16 + 16)
                if not before(g, U):
                    pool.wait_ge(msg_ready, g - (U - 1))
                pool.wait_ge(src_ready, g + 1)
                settle(pool, C)
                for j in range(TILES):
                    pool.indirect_dma_start(
                        out=gath[u][:, j, :], out_offset=None, in_=x1,
                        in_offset=bass.IndirectOffsetOnAxis(ap=src[u][:, j:j + 1], axis=0)).then_inc(gath_in[u], 16)
            loop_pairs(pool, ng, step, peel=1, step=U)

        @block.scalar
        def _(act):
            def scale(g, u2):
                act.wait_ge(w_ready, g + 1)
                if not before(g, 2):
                    act.wait_ge(msg_ready, g - 1)
                for j in range(TILES):
                    w = wps[u2][j // 2][:, (j % 2) * WN0:(j % 2) * WN0 + 96]
                    last_ = nc.scalar.activation(es[u2][:, j, :], w, ACT.Copy, scale=row[scale.slot][:, j, EA4:EA4 + 1])
                last_.then_inc(es_ready, 1)

            def step(g, u, k):
                act.wait_ge(row_in[u], k * 16 + 16)
                if not before(g, U):
                    act.wait_ge(gath_in[u], k * (16 * TILES))
                nc.scalar.copy(src[u][:, :], row[u][:, :, SRC].bitcast(I32)).then_inc(src_ready, 1)
                act.wait_ge(tr, g + 1)
                if not before(g, 1):
                    act.wait_ge(fc1, g)
                nc.scalar.copy(eT[0:10, :], tps[0:10, :]).then_inc(ev, 1)
                if not before(g, 1):
                    scale.slot = (u - 1) % U
                    scale(g - 1, (u - 1) % 2)
                act.wait_ge(fc1, g + 1)
                if not before(g, 1):
                    act.wait_ge(w_ready, g)
                nc.scalar.activation(hid[0:H0, :], hps[0:H0, :], ACT.Silu).then_inc(act1, 1)
            loop_pairs(act, ng, step, peel=1, step=U)
            scale.slot = (ng - 1) % U
            scale(ng - 1, (ng - 1) % 2)

        @block.vector
        def _(dve):
            nc.vector.memset(acc[U - 1][:, :], 0.0).then_inc(zeroed, 1)
            dve.wait_ge(zeroed, 1)

            def add_group(g, u, k):
                dve.wait_ge(summed, g + 1)
                if not before(g, 1):
                    dve.wait_ge(acc_ready, g)
                if not before(g, U):
                    dve.wait_ge(acc_out[u], k * 16)
                nc.vector.scalar_tensor_tensor(acc[u][:, :], acc[(u - 1) % U][:, :], table[:, 2, bass.ds(g, 1)],
                                               aps[u % 2][:, 0:AGG0], ALU.mult, ALU.add).then_inc(acc_ready, 1)

            def step(g, u, k):
                r, v = row[u], u % 2
                CH = 6
                dve.wait_ge(row_in[u], k * 16 + 16)
                if not before(g, 1):
                    dve.wait_ge(ch, g * CH)
                nc.vector.tensor_scalar(local[:, :], r[:, :, DST].bitcast(I32), table[:, 1, bass.ds(g, 1)], None,
                                        ALU.subtract).then_inc(ch, 1)
                dve.wait_ge(ch, g * CH + 1)
                if not before(g, 2):
                    dve.wait_ge(summed, g - 1)
                nc.vector.tensor_tensor(hot[v][:, :, :], bcast(C["node_ramp"][:, :], 1, TILES), bcast(local[:, :], 2, P),
                                        ALU.is_equal)
                if not before(g, 2):
                    add_group(g - 2, (u - 2) % U, k if u >= 2 else k - 1)
                dve.wait_ge(gath_in[u], (k + 1) * (16 * TILES))
                gs = gath[u][:, :, 0:MS]
                gv = gath[u][:, :, MS:D].rearrange("p j (c f) -> p j c f", c=3)
                ev_ = r[:, :, EA4 + 1:EA4 + 4]
                nc.vector.tensor_tensor(dots[:, :, :, :], gv, bcast(ev_, 3, MV), ALU.mult).then_inc(ch, 1)
                dve.wait_ge(es_ready, g + 1)
                for h in range(2):
                    w = wps[v][h][:, 0:2 * WN0].rearrange("p (j f) -> p j f", j=2)
                    i_ = nc.vector.tensor_tensor(ws[:, 2 * h:2 * h + 2, :], w[:, :, 96:160], gs[:, 2 * h:2 * h + 2, :], ALU.mult)
                i_.then_inc(ch, 1)
                dve.wait_ge(ch, g * CH + 2)
                nc.vector.tensor_tensor(dot[:, :, :], dots[:, :, 0, :], dots[:, :, 1, :], ALU.add).then_inc(ch, 1)
                m = msg[v]
                mv_ = m[:, :, 96:AGG0].rearrange("p j (c f) -> p j c f", c=3)
                nc.vector.tensor_tensor(m[:, :, 0:MS], es[v][:, :, 0:MS], gs, ALU.mult)
                dve.wait_ge(ch, g * CH + 4)
                nc.vector.tensor_tensor(dot[:, :, :], dot[:, :, :], dots[:, :, 2, :], ALU.add).then_inc(ch, 1)
                for j in range(TILES):
                    i_ = nc.vector.tensor_tensor(mv_[:, j, :, 0:MS], bcast(ws[:, j, :], 1, 3), bcast(ev_[:, j, :], 2, MS), ALU.mult)
                i_.then_inc(ch, 1)
                dve.wait_ge(ch, g * CH + 5)
                for h in range(2):
                    w = wps[v][h][:, 0:2 * WN0].rearrange("p (j f) -> p j f", j=2)
                    nc.vector.tensor_tensor(m[:, 2 * h:2 * h + 2, MS:96], w[:, :, 160:192], dot[:, 2 * h:2 * h + 2, :], ALU.mult)
                nc.vector.tensor_tensor(mv_[:, :, :, MS:96], bcast(es[v][:, :, MS:96], 2, 3), gv, ALU.mult).then_inc(msg_ready, 1)
            loop_pairs(dve, ng, step, peel=1, step=U)
            for g in (ng - 2, ng - 1):
                add_group(g, g % U, ng // U - 1)

        @block.tensor
        def _(pe):
            def half_sum(g, v, h):
                if h == 0:
                    pe.wait_ge(msg_ready, g + 1)
                    if not before(g, 2):
                        pe.wait_ge(acc_ready, g - 1)
                for j in (2 * h, 2 * h + 1):
                    i_ = nc.tensor.matmul(aps[v][:, 0:AGG0], hot[v][:, j, :], msg[v][:, j, :], start=j == 0, stop=j == TILES - 1)
                if h:
                    i_.then_inc(summed, 1)

            def step(g, u, k):
                v = u % 2
                pe.wait_ge(row_in[u], k * 16 + 16)
                if not before(g, 1):
                    pe.wait_ge(ev, g)
                for j in range(TILES):
                    i_ = nc.tensor.transpose(tps[0:10, j * P:(j + 1) * P], row[u][:, j, EA10:EA10 + 10], C["ident"][:, :])
                i_.then_inc(tr, 1)
                if not before(g, 2):
                    half_sum(g - 2, v, 0)
                pe.wait_ge(ev, g + 1)
                if not before(g, 1):
                    pe.wait_ge(act1, g)
                nc.tensor.matmul(hps[0:H0, :], Wn["fc1_0"][0:10, :], eT[0:10, :], start=True, stop=True).then_inc(fc1, 1)
                if not before(g, 2):
                    half_sum(g - 2, v, 1)
                pe.wait_ge(act1, g + 1)
                for j in range(TILES):
                    i_ = nc.tensor.matmul(wps[v][j // 2][:, (j % 2) * WN0:(j % 2 + 1) * WN0], hid[0:H0, j * P:(j + 1) * P],
                                          Wn["fc2_0"][0:H0, :], start=True, stop=True)
                i_.then_inc(w_ready, 1)
            loop_pairs(pe, ng, step, peel=1, step=U)
            for g in (ng - 2, ng - 1):
                half_sum(g, g % 2, 0)
                half_sum(g, g % 2, 1)


def to_source_order(nc, C, rows_a, sv, table, row0, node0, ng, n_edges, rows_b):
    U = UNROLL
    ctx = ExitStack()
    with ctx:
        a = Names(nc, ctx, "route")
        row = [a.sb(f"row{i}", [P, TILES, ROW_B]) for i in range(U)]
        node = [a.sb(f"node{i}", [P, D]) for i in range(U)]
        at = [a.sb(f"at{i}", [P, TILES], I32) for i in range(U)]
        hot = [a.sb(f"hot{i}", [P, TILES, P]) for i in range(2)]
        hotT = [a.sb(f"hotT{i}", [P, G]) for i in range(2)]
        local, low, high = a.sb("local", [P, TILES]), a.sb("low", [P, TILES]), a.sb("high", [P, TILES])
        pad = a.sb("pad", [G // 8, 8 * ROW_B])
        tps = [a.ps(f"t{i}") for i in range(2)]
        nps = [[a.ps(f"n{i}{j}") for j in range(2)] for i in range(2)]
        row_in = [a.sem(f"row_in{i}") for i in range(U)]
        out_done = [a.sem(f"out_done{i}") for i in range(U)]
        hot_ready, tr, ev, picked, filled, at_ready, ch, padded, pad_out = (
            a.sem(s) for s in ("hot_ready", "tr", "ev", "picked", "filled", "at_ready", "chain", "padded", "pad_out"))
        block = ctx.enter_context(nc.Block())

        @block.sync
        def _(sp):
            sp.wait_ge(padded, 2)
            sp.dma_start(rows_b[n_edges:n_edges + G, :].rearrange("(p j) w -> p (j w)", j=8), pad[:, :]).then_inc(pad_out, 16)

            def step(g, u, k):
                if not before(g, U):
                    sp.wait_ge(out_done[u], k * (16 * TILES))
                    settle(sp, C)
                    sp.wait_ge(picked, g - (U - 1))
                settle(sp, C)
                r = sp.value_load(row0[0:1, bass.ds(g, 1)], min_val=0, max_val=rows_a.shape[0] - G)
                b = sp.value_load(node0[0:1, bass.ds(g, 1)], min_val=0, max_val=sv.shape[0] - P)
                sp.dma_start(row[u][:, :, 0:B_NODE], rows_a[bass.ds(r, G), :].rearrange("(p j) w -> p j w", p=P)[:, :, EA3:ROW_A])\
                    .then_inc(row_in[u], 16)
                sp.dma_start(node[u][:, :], sv[bass.ds(b, P), :]).then_inc(row_in[u], 16)
            loop_pairs(sp, ng, step, peel=1, step=U)
            sp.wait_ge(pad_out, 16)

        @block.vector
        def _(dve):
            nc.vector.memset(pad[:, :], 1.0).then_inc(padded, 1)
            dve.wait_ge(padded, 1)
            nc.vector.memset(pad[:, :].rearrange("p (j w) -> p j w", j=8)[:, :, B_SRC].bitcast(I32), C["blocks"] * P + P)\
                .then_inc(padded, 1)

            def fill(g, u, k):
                dve.wait_ge(picked, g + 1)
                for h in range(2):
                    i_ = nc.vector.tensor_copy(row[u][:, 2 * h:2 * h + 2, B_NODE:ROW_B],
                                               nps[u % 2][h][:, 0:2 * D].rearrange("p (j f) -> p j f", j=2))
                i_.then_inc(filled, 1)

            def step(g, u, k):
                dve.wait_ge(row_in[u], k * 32 + 32)
                if not before(g, 1):
                    dve.wait_ge(ch, g * 4)
                    dve.wait_ge(at_ready, g)
                nc.vector.tensor_scalar(local[:, :], row[u][:, :, B_DST].bitcast(I32), table[:, 1, bass.ds(g, 1)], None,
                                        ALU.subtract).then_inc(ch, 1)
                dve.wait_ge(ch, g * 4 + 1)
                if not before(g, 2):
                    dve.wait_ge(tr, g - 1)
                nc.vector.tensor_tensor(hot[u % 2][:, :, :], bcast(C["node_ramp"][:, :], 1, TILES), bcast(local[:, :], 2, P),
                                        ALU.is_equal).then_inc(hot_ready, 1)
                nc.vector.tensor_scalar(low[:, :], local[:, :], 0.0, float(OUT_OF_BOUNDS), ALU.is_lt, ALU.mult).then_inc(ch, 1)
                nc.vector.tensor_scalar(high[:, :], local[:, :], float(P), float(OUT_OF_BOUNDS), ALU.is_ge, ALU.mult).then_inc(ch, 1)
                dve.wait_ge(ch, g * 4 + 3)
                nc.vector.tensor_tensor(high[:, :], high[:, :], low[:, :], ALU.add).then_inc(ch, 1)
                dve.wait_ge(ch, g * 4 + 4)
                if not before(g, U):
                    dve.wait_ge(out_done[u], k * (16 * TILES))
                nc.vector.tensor_tensor(at[u][:, :], high[:, :], row[u][:, :, B_POS].bitcast(I32), ALU.add).then_inc(at_ready, 1)
                if not before(g, 1):
                    fill(g - 1, (u - 1) % U, k)
            loop_pairs(dve, ng, step, peel=1, step=U)
            fill(ng - 1, (ng - 1) % U, None)

        @block.scalar
        def _(act):
            def step(g, u, k):
                act.wait_ge(tr, g + 1)
                if not before(g, 2):
                    act.wait_ge(picked, g - 1)
                nc.scalar.copy(hotT[u % 2][:, :], tps[u % 2][:, :]).then_inc(ev, 1)
            loop_pairs(act, ng, step, peel=1, step=U)

        @block.tensor
        def _(pe):
            def pick(g, u, k):
                pe.wait_ge(ev, g + 1)
                if not before(g, 2):
                    pe.wait_ge(filled, g - 1)
                pe.wait_ge(row_in[u], (k + 1) * 32)
                for j in range(TILES):
                    i_ = nc.tensor.matmul(nps[u % 2][j // 2][:, (j % 2) * D:(j % 2 + 1) * D], hotT[u % 2][:, j * P:(j + 1) * P],
                                          node[u][:, :], start=True, stop=True)
                i_.then_inc(picked, 1)

            def step(g, u, k):
                pe.wait_ge(hot_ready, g + 1)
                if not before(g, 2):
                    pe.wait_ge(ev, g - 1)
                for j in range(TILES):
                    i_ = nc.tensor.transpose(tps[u % 2][:, j * P:(j + 1) * P], hot[u % 2][:, j, :], C["ident"][:, :])
                i_.then_inc(tr, 1)
                pick(g, u, k)
            loop_pairs(pe, ng, step, peel=1, step=U)

        @block.gpsimd
        def _(pool):
            bound = rows_b.shape[0] - 1

            def step(g, u, k):
                pool.wait_ge(filled, g + 1)
                pool.wait_ge(at_ready, g + 1)
                settle(pool, C)
                for j in range(TILES):
                    pool.indirect_dma_start(
                        out=rows_b, out_offset=bass.IndirectOffsetOnAxis(ap=at[u][:, j:j + 1], axis=0),
                        in_=row[u][:, j, :], in_offset=None, bounds_check=bound, oob_is_err=False).then_inc(out_done[u], 16)
            loop_pairs(pool, ng, step, peel=1, step=U)
            for u in range(U):
                pool.wait_ge(out_done[u], 16 * TILES * (ng // U))


def edges_gnn1(nc, C, rows_b, table, row0, Wn, ng, agg):
    U = UNROLL
    ctx = ExitStack()
    with ctx:
        a = Names(nc, ctx, "edge1")
        row = [a.sb(f"row{i}", [P, TILES, ROW_B]) for i in range(U)]
        fT, hid = a.sb("fT", [64, G]), a.sb("hid", [64, G])
        hot = [a.sb(f"hot{i}", [P, TILES, P]) for i in range(2)]
        msg = [a.sb(f"msg{i}", [P, TILES, AGG1]) for i in range(2)]
        local, sq, n2, n1, rn = (a.sb(s, [P, TILES]) for s in ("local", "sq1", "n2", "n1", "rn"))
        squares = a.sb("squares", [P, TILES, 3])
        sh = [a.sb(f"sh{i}", [P, TILES, 5]) for i in range(2)]
        ws = a.sb("ws", [P, TILES, MS])
        dots = a.sb("dots", [P, TILES, 3, MV])
        dot = a.sb("dot", [P, TILES, MV])
        wv = [a.sb(f"wv{i}", [P, TILES, 5, MV]) for i in range(2)]
        left = [a.sb(f"left{i}", [P, TILES, 3, MV]) for i in range(2)]
        right = [a.sb(f"right{i}", [P, TILES, 3, MV]) for i in range(2)]
        acc = [a.sb(f"acc{i}", [P, AGG1]) for i in range(U)]
        tps, hps = a.ps("t"), a.ps("h")
        wps = [[a.ps(f"w{i}{j}") for j in range(2)] for i in range(2)]
        aps = [a.ps(f"a{i}") for i in range(2)]
        row_in = [a.sem(f"row_in{i}") for i in range(U)]
        acc_out = [a.sem(f"acc_out{i}") for i in range(U)]
        tr, ev, fc1, act1, w_ready = (a.sem(s) for s in ("tr", "ev", "fc1", "act1", "w_ready"))
        n2_ready, root, wv_ready, crossed, msg_ready, summed, acc_ready, ch, zeroed, pch = (
            a.sem(s) for s in ("n2_ready", "root", "wv_ready", "crossed", "msg_ready", "summed", "acc_ready", "chain", "zeroed", "pool_chain"))
        block = ctx.enter_context(nc.Block())
        agg_rows = agg.rearrange("g p f -> (g p) f")

        @block.sync
        def _(sp):
            def store(g, u):
                sp.wait_ge(acc_ready, g + 1)
                settle(sp, C)
                sp.dma_start(agg_rows[bass.ds(g * P, P), :], acc[u][:, :]).then_inc(acc_out[u], 16)

            def step(g, u, k):
                if not before(g, 5):
                    store(g - 5, (u - 5) % U)
                if not before(g, U):
                    sp.wait_ge(msg_ready, g - (U - 1))
                settle(sp, C)
                r = sp.value_load(row0[0:1, bass.ds(g, 1)], min_val=0, max_val=rows_b.shape[0] - G)
                sp.dma_start(row[u][:, :, :].rearrange("p j w -> p (j w)"),
                             rows_b[bass.ds(r, G), :].rearrange("(p j) w -> p (j w)", p=P)).then_inc(row_in[u], 16)
            loop_pairs(sp, ng, step, peel=2, step=U)
            for g in range(ng - 5, ng):
                store(g, g % U)
            for u in range(U):
                sp.wait_ge(acc_out[u], 16 * (ng // U))

        @block.scalar
        def _(act):
            def step(g, u, k):
                act.wait_ge(tr, g + 1)
                if not before(g, 1):
                    act.wait_ge(fc1, g)
                nc.scalar.copy(fT[:, :], tps[0:64, :]).then_inc(ev, 1)
                act.wait_ge(n2_ready, g + 1)
                nc.scalar.activation(n1[:, :], n2[:, :], ACT.Sqrt, scale=1 / 3.0).then_inc(root, 1)
                act.wait_ge(fc1, g + 1)
                if not before(g, 1):
                    act.wait_ge(w_ready, g)
                nc.scalar.activation(hid[:, :], hps[0:64, :], ACT.Relu).then_inc(act1, 1)
            loop_pairs(act, ng, step, peel=1, step=U)

        @block.gpsimd
        def _(pool):
            def step(g, u, k):
                v = u % 2
                pool.wait_ge(wv_ready, g + 1)
                settle(pool, C)
                nc.gpsimd.tensor_tensor(left[v][:, :, :, :], wv[v][:, :, 1:4, :], bcast(sh[v][:, :, 2:5], 3, MV), ALU.mult)
                nc.gpsimd.tensor_tensor(right[v][:, :, :, :], wv[v][:, :, 2:5, :], bcast(sh[v][:, :, 1:4], 3, MV), ALU.mult).then_inc(pch, 1)
                pool.wait_ge(pch, g + 1)
                settle(pool, C)
                if not before(g, 2):
                    pool.wait_ge(summed, g - 1)
                settle(pool, C)
                nc.gpsimd.tensor_tensor(msg[v][:, :, 96:AGG1].rearrange("p j (c f) -> p j c f", c=3)[:, :, :, 96:128],
                                        left[v][:, :, :, :], right[v][:, :, :, :], ALU.subtract).then_inc(crossed, 1)
            loop_pairs(pool, ng, step, peel=1, step=U)

        @block.vector
        def _(dve):
            nc.vector.memset(acc[U - 1][:, :], 0.0).then_inc(zeroed, 1)
            dve.wait_ge(zeroed, 1)

            def add_group(g, u, k):
                dve.wait_ge(summed, g + 1)
                if not before(g, 1):
                    dve.wait_ge(acc_ready, g)
                if not before(g, U):
                    dve.wait_ge(acc_out[u], k * 16)
                nc.vector.scalar_tensor_tensor(acc[u][:, :], acc[(u - 1) % U][:, :], table[:, 2, bass.ds(g, 1)],
                                               aps[u % 2][:, 0:AGG1], ALU.mult, ALU.add).then_inc(acc_ready, 1)

            def step(g, u, k):
                r, v = row[u], u % 2
                CH = 10
                xs = r[:, :, B_NODE:B_NODE + MS]
                xv = r[:, :, B_NODE + MS:ROW_B].rearrange("p j (c f) -> p j c f", c=3)
                m = msg[v]
                mv_ = m[:, :, 96:AGG1].rearrange("p j (c f) -> p j c f", c=3)

                def w(h, lo, n):
                    return wps[v][h][:, 0:2 * WN1].rearrange("p (j f) -> p j f", j=2)[:, :, lo:lo + n]
                dve.wait_ge(row_in[u], k * 16 + 16)
                if not before(g, 1):
                    dve.wait_ge(ch, g * CH)
                    dve.wait_ge(msg_ready, g)
                nc.vector.tensor_tensor(squares[:, :, :], r[:, :, B_EA3:B_EA3 + 3], r[:, :, B_EA3:B_EA3 + 3], ALU.mult).then_inc(ch, 1)
                nc.vector.tensor_scalar(local[:, :], r[:, :, B_SRC].bitcast(I32), table[:, 1, bass.ds(g, 1)], None,
                                        ALU.subtract).then_inc(ch, 1)
                dve.wait_ge(ch, g * CH + 1)
                nc.vector.tensor_reduce(n2[:, :], squares[:, :, :], AXX, ALU.add).then_inc(n2_ready, 1)
                dve.wait_ge(ch, g * CH + 2)
                if not before(g, 2):
                    dve.wait_ge(summed, g - 1)
                nc.vector.tensor_tensor(hot[v][:, :, :], bcast(C["node_ramp"][:, :], 1, TILES), bcast(local[:, :], 2, P),
                                        ALU.is_equal)
                if not before(g, 2):
                    add_group(g - 2, (u - 2) % U, k if u >= 2 else k - 1)
                dve.wait_ge(root, g + 1)
                nc.vector.reciprocal(rn[:, :], n1[:, :]).then_inc(ch, 1)
                dve.wait_ge(w_ready, g + 1)
                if not before(g, 2):
                    dve.wait_ge(crossed, g - 1)
                for h in range(2):
                    j2 = slice(2 * h, 2 * h + 2)
                    nc.vector.tensor_tensor(wv[v][:, j2, 0:3, :], bcast(w(h, 192, MV), 2, 3), xv[:, j2, :, :], ALU.mult)
                dve.wait_ge(ch, g * CH + 3)
                nc.vector.tensor_tensor(sh[v][:, :, 0:3], r[:, :, B_EA3:B_EA3 + 3], bcast(rn[:, :], 2, 3), ALU.mult).then_inc(ch, 1)
                for h in range(2):
                    j2 = slice(2 * h, 2 * h + 2)
                    i_ = nc.vector.tensor_tensor(wv[v][:, j2, 3:5, :], bcast(w(h, 192, MV), 2, 2), xv[:, j2, 0:2, :], ALU.mult)
                dve.wait_ge(ch, g * CH + 4)
                nc.vector.tensor_copy(sh[v][:, :, 3:5], sh[v][:, :, 0:2]).then_inc(wv_ready, 1)
                s_ = sh[v][:, :, 0:3]
                nc.vector.tensor_tensor(dots[:, :, :, :], xv, bcast(s_, 3, MV), ALU.mult).then_inc(ch, 1)
                for h in range(2):
                    j2 = slice(2 * h, 2 * h + 2)
                    i_ = nc.vector.tensor_tensor(ws[:, j2, :], w(h, MS, MS), xs[:, j2, :], ALU.mult)
                i_.then_inc(ch, 1)
                dve.wait_ge(ch, g * CH + 5)
                nc.vector.tensor_tensor(dot[:, :, :], dots[:, :, 0, :], dots[:, :, 1, :], ALU.add).then_inc(ch, 1)
                for h in range(2):
                    j2 = slice(2 * h, 2 * h + 2)
                    i_ = nc.vector.tensor_tensor(m[:, j2, 0:MS], w(h, 0, MS), xs[:, j2, :], ALU.mult)
                dve.wait_ge(ch, g * CH + 7)
                nc.vector.tensor_tensor(dot[:, :, :], dot[:, :, :], dots[:, :, 2, :], ALU.add).then_inc(ch, 1)
                for j in range(TILES):
                    i_ = nc.vector.tensor_tensor(mv_[:, j, :, 0:MS], bcast(ws[:, j, :], 1, 3), bcast(s_[:, j, :], 2, MS), ALU.mult)
                i_.then_inc(ch, 1)
                for h in range(2):
                    j2 = slice(2 * h, 2 * h + 2)
                    i_ = nc.vector.tensor_tensor(mv_[:, j2, :, MS:96], bcast(w(h, 128, MV), 2, 3), xv[:, j2, :, :], ALU.mult)
                i_.then_inc(ch, 1)
                dve.wait_ge(ch, g * CH + 8)
                for h in range(2):
                    j2 = slice(2 * h, 2 * h + 2)
                    i_ = nc.vector.tensor_tensor(m[:, j2, MS:96], w(h, 160, MV), dot[:, j2, :], ALU.mult)
                i_.then_inc(msg_ready, 1)
            loop_pairs(dve, ng, step, peel=1, step=U)
            for g in (ng - 2, ng - 1):
                add_group(g, g % U, ng // U - 1)

        @block.tensor
        def _(pe):
            def half_sum(g, v, h):
                if h == 0:
                    pe.wait_ge(msg_ready, g + 1)
                    pe.wait_ge(crossed, g + 1)
                    if not before(g, 2):
                        pe.wait_ge(acc_ready, g - 1)
                for j in (2 * h, 2 * h + 1):
                    i_ = nc.tensor.matmul(aps[v][:, 0:AGG1], hot[v][:, j, :], msg[v][:, j, :], start=j == 0, stop=j == TILES - 1)
                if h:
                    i_.then_inc(summed, 1)

            def step(g, u, k):
                v = u % 2
                pe.wait_ge(row_in[u], k * 16 + 16)
                if not before(g, 1):
                    pe.wait_ge(ev, g)
                settle(pe, C)
                for j in range(TILES):
                    i_ = nc.tensor.transpose(tps[0:64, j * P:(j + 1) * P], row[u][:, j, B_EA64:B_EA64 + 64], C["ident"][:, :])
                i_.then_inc(tr, 1)
                if not before(g, 2):
                    half_sum(g - 2, v, 0)
                pe.wait_ge(ev, g + 1)
                if not before(g, 1):
                    pe.wait_ge(act1, g)
                settle(pe, C)
                nc.tensor.matmul(hps[0:64, :], Wn["fc1_1"][0:64, :], fT[:, :], start=True, stop=True).then_inc(fc1, 1)
                if not before(g, 2):
                    half_sum(g - 2, v, 1)
                pe.wait_ge(act1, g + 1)
                for j in range(TILES):
                    i_ = nc.tensor.matmul(wps[v][j // 2][:, (j % 2) * WN1:(j % 2 + 1) * WN1], hid[:, j * P:(j + 1) * P],
                                          Wn["fc2_1"][0:H1, :], start=True, stop=True)
                i_.then_inc(w_ready, 1)
            loop_pairs(pe, ng, step, peel=1, step=U)
            for g in (ng - 2, ng - 1):
                half_sum(g, g % 2, 0)
                half_sum(g, g % 2, 1)


def table_ints(nc, stage, table, row0, node0):
    ctx = ExitStack()
    with ctx:
        done = Names(nc, ctx, stage).sem("ints")
        block = ctx.enter_context(nc.Block())

        @block.vector
        def _(dve):
            top = float(node0_limit[0])
            nc.vector.tensor_copy(row0[:, :], table[0:1, 0, :]).then_inc(done, 1)
            nc.vector.tensor_scalar(node0[:, :], table[0:1, 1, :], top, None, ALU.min).then_inc(done, 1)
            dve.wait_ge(done, 2)


node0_limit = [0]


def program(nc, n_nodes, n_edges, A, Wd, out):
    nb, cols = blocks_of(n_nodes), columns_of(n_edges)
    ng = groups_of(n_edges, nb)
    e_pad = P * cols
    node0_limit[0] = (nb - 1) * P

    def dram(name, shape, dt=F32):
        return nc.dram_tensor(name, shape, dt, kind="Internal").ap()
    pos_a, pos_b = dram("place_by_destination", [e_pad], I32), dram("place_by_source", [e_pad], I32)
    rows_a, rows_b = dram("rows_by_destination", [e_pad, ROW_A]), dram("rows_by_source", [e_pad, ROW_B])
    x1 = dram("x1", [(nb + 1) * P, D])
    base, x2, sv = (dram(s, [nb * P, D]) for s in ("base", "x2", "sv"))
    skip = dram("skip", [nb * P, 192])
    agg0, agg1 = dram("agg0", [ng, P, AGG0]), dram("agg1", [ng, P, AGG1])
    meta = dram("meta", [2, 3, P * (-(-ng // P))])
    ctx = ExitStack()
    with ctx:
        a = Names(nc, ctx, "all")
        C = {"blocks": nb, "ident": a.sb("ident", [P, P]), "before": a.sb("before", [P, P], BF16),
             "not_before": a.sb("not_before", [P, P], BF16), "ones": a.sb("ones", [P, P], BF16),
             "block_ramp": a.sb("block_ramp", [P, nb], BF16), "node_ramp": a.sb("node_ramp", [P, P])}
        Wn = {k: a.sb(k, [P, n]) for k, n in (("s0", 4 * MS), ("v0", 4 * 96), ("fc1_0", H0), ("fc2_0", WN0), ("ps", 2 * MS),
                                             ("pv", 2 * MV), ("s1", MS + 96), ("v1", 192), ("fc1_1", 64), ("fc2_1", WN1),
                                             ("outs", 96), ("outv", MV))}
        count = a.sb("count", [P, nb])
        tables = [a.sb(f"table{i}", [P, 3, ng]) for i in range(2)]
        row0 = [a.sb(f"row0_{i}", [1, ng], I32) for i in range(2)]
        node0 = [a.sb(f"node0_{i}", [1, ng], I32) for i in range(2)]
        last = [a.sb(f"last{i}", [1, nb], I32) for i in range(2)]
        C["settled"] = a.sem("settled")
        constants(nc, C)
        prepare_weights(nc, C, Wd, Wn)
        rank(nc, C, "rank_src", A["src"], cols, nb, pos_b, count)
        group_table(nc, C, "groups_src", count, nb, n_edges, ng, meta[1], tables[1], last[1])
        table_ints(nc, "src", tables[1], row0[1], node0[1])
        rank(nc, C, "rank_dst", A["dst"], cols, nb, pos_a, count)
        group_table(nc, C, "groups_dst", count, nb, n_edges, ng, meta[0], tables[0], last[0])
        table_ints(nc, "dst", tables[0], row0[0], node0[0])
        to_destination_order(nc, C, A["attrs"], A["src"], A["dst"], pos_a, pos_b, rows_a, cols)
        before_gnn0(nc, C, A["x"], A["attr"], Wn, nb, x1, base)
        edges_gnn0(nc, C, rows_a, x1, tables[0], row0[0], Wn, ng, agg0)
        between(nc, C, agg0, last[0], base, A["attr"], Wn, nb, x2, sv, skip)
        to_source_order(nc, C, rows_a, sv, tables[0], row0[0], node0[0], ng, n_edges, rows_b)
        edges_gnn1(nc, C, rows_b, tables[1], row0[1], Wn, ng, agg1)
        after_gnn1(nc, C, agg1, last[1], x2, skip, Wn, nb, out)


WEIGHTS = ["L0_gnn_" + s for s in ("Ws_sc_a", "Wv_sc_a", "Ws_sc_c", "Wv_sc_c", "Ws_l1_a", "Wv_l1_a", "Ws_l1_c", "Wv_l1_c",
                                   "W_fc1", "W_fc2", "Ws_l2_a", "Wv_l2_a", "Ws_l2_c", "Wv_l2_c", "Ws_l3", "Wv_l3")] \
    + ["L1_gnn_" + s for s in ("W_skip0", "W_skip1", "W_nl0", "W_nl1", "W_fc1", "W_fc2", "W_out_s", "W_out_v")]


def kernel(**inputs):
    import numpy as np
    import concourse.bacc as bacc
    from concourse.bass_utils import run_bass_kernel_spmd

    n, e = inputs["x"].shape[0], inputs["src"].shape[0]
    nb, e_pad = blocks_of(n), P * columns_of(e)

    def padded(a, rows, value):
        return np.concatenate([a, np.full((rows - a.shape[0],) + a.shape[1:], value, a.dtype)])

    x = np.asarray(inputs["x"])
    x = np.concatenate([x[:, :MS], x[:, MS:].reshape(n, MV, 3).transpose(0, 2, 1).reshape(n, 3 * MV)], axis=1)
    attrs = np.concatenate([np.asarray(inputs[s]) for s in ("edge_attr_10", "edge_attr_4", "edge_attr_3", "edge_attr_64")], axis=1)
    attr = np.concatenate([np.asarray(inputs[s]) for s in ("node_vec1", "node_vec1_n2", "node_vec1_n3")], axis=1)
    arrays = {"x": padded(x, nb * P, 0), "attr": padded(attr, nb * P, 0), "attrs": padded(attrs, e_pad, 1),
              "src": padded(np.asarray(inputs["src"]), e_pad, nb * P),
              "dst": padded(np.asarray(inputs["dst"]), e_pad, (nb + 1) * P)}
    for s in WEIGHTS:
        arrays[s] = np.asarray(inputs[s])
    nc = bacc.Bacc("TRN2", target_bir_lowering=False, num_devices=1)
    aps = {s: nc.dram_tensor("in_" + s, v.shape, mybir.dt.from_np(v.dtype), kind="ExternalInput").ap() for s, v in arrays.items()}
    out = nc.dram_tensor("out", (nb * P, D), F32, kind="ExternalOutput").ap()
    program(nc, n, e, aps, aps, out)
    r = run_bass_kernel_spmd(nc, [{"in_" + s: np.ascontiguousarray(v) for s, v in arrays.items()}], core_ids=[0])
    y = r.results[0]["out"][:n]
    return np.concatenate([y[:, :MS], y[:, MS:].reshape(n, 3, MV).transpose(0, 2, 1).reshape(n, 3 * MV)], axis=1)
```

```python
import concourse.bass as bass
from concourse import mybir
from contextlib import ExitStack

F32 = mybir.dt.float32
I32 = mybir.dt.int32
BF16 = mybir.dt.bfloat16
ALU = mybir.AluOpType
ACT = mybir.ActivationFunctionType
AXX = mybir.AxisListType.X

P = 128
MS, MV = 64, 32
D = MS + 3 * MV
G = 2 * P
TILES = 4
RANKED = 5
UNROLL = 4
LONG_UNROLL = 8
SPREAD = 2
LN_EPS = 1e-5
OUT_OF_BOUNDS = 1 << 20
EA10, EA4, ATTR0 = 0, 10, 14
EA3, EA64, ATTR1 = 0, 3, 67
SRC, DST, PLACE = 0, 1, 2
B_SRC, B_NODE, ROW_B = ATTR1, ATTR1 + 1, ATTR1 + 1 + D
W_STRIDE = 256
H0, WN0, MID0 = 100, 192, 96
AGG0 = MID0 * 4
H1, WN1 = 64, 224
AGG1 = 96 + 3 * 128
C_S = 0.3826834323650898
C_X = 0.9238795325112867


def blocks_of(n_nodes):
    return 2 * (-(-n_nodes // (2 * P)))


def columns_of(n_edges):
    return 2 * RANKED * (-(-(n_edges + G) // (P * 2 * RANKED)))


def groups_of(n_edges, n_blocks):
    return 2 * LONG_UNROLL * (-(-(n_edges // G + n_blocks) // (2 * LONG_UNROLL)))


def shifted(i, u, k, by, step=UNROLL):
    return i + by, (u + by) % step, k + (u + by) // step


class Names:

    def __init__(self, nc, ctx, stage):
        self.nc, self.ctx, self.stage, self.sems = nc, ctx, stage, []
        ctx.callback(self.clear)

    def sb(self, name, shape, dt=F32):
        return self.ctx.enter_context(self.nc.sbuf_tensor(f"{self.stage}_{name}", shape, dt))

    def ps(self, name, cols=512, dt=F32):
        return self.ctx.enter_context(self.nc.psum_tensor(f"{self.stage}_{name}", [P, cols], dt))

    def sem(self, name):
        self.sems.append(self.nc.alloc_semaphore(name=f"{self.stage}_{name}"))
        return self.sems[-1]

    def clear(self):
        self.nc.clear_and_free_semaphores(self.sems)
        self.nc.all_engine_barrier()


def loop_pairs(eng, n, body, peel=1, step=2):
    for k in range(min(peel, n // step)):
        for u in range(step):
            body(step * k + u, u, k)
    if n // step > peel:
        with eng.Fori(peel, n // step) as k:
            for u in range(step):
                body(k * step + u, u, k)


def loop_blocks(eng, n, body, step=LONG_UNROLL):
    m = (n - 1) // step * step
    loop_pairs(eng, m, body, step=step)
    for b in range(m, n):
        body(b, b % step, b // step)


def is_last(b, nb):
    return isinstance(b, int) and b == nb - 1


def times(u, nb):
    return (nb - u + LONG_UNROLL - 1) // LONG_UNROLL


def bcast(ap, dim, count):
    shape = list(ap.shape)
    return ap.unsqueeze(dim).to_broadcast(shape[:dim] + [count] + shape[dim:])


def idle(C, *engines):
    for engine in engines:
        @engine
        def _(eng):
            settle(eng, C)


def either(eng, flag, yes, no):
    taken = eng.value_load(flag[0:1, 0:1], min_val=0, max_val=1)
    with eng.If(taken != 0):
        yes()
    with eng.Else():
        no()


def settle(eng, C):
    eng.sem_inc(C["settled"], 1)


def constants(nc, C):
    ctx = ExitStack()
    with ctx:
        a = Names(nc, ctx, "const")
        done, filled = a.sem("done"), a.sem("filled")
        block = ctx.enter_context(nc.Block())

        @block.gpsimd
        def _(pool):
            pool.memset(C["ident"][:, :], 0.0).then_inc(filled, 1)
            pool.memset(C["before"][:, :], 1.0).then_inc(filled, 1)
            pool.memset(C["not_before"][:, :], 1.0).then_inc(filled, 1)
            pool.memset(C["ones"][:, :], 1.0).then_inc(done, 1)
            pool.memset(C["ones_f32"][:, :], 1.0).then_inc(done, 1)
            pool.wait_ge(filled, 3)
            pool.affine_select(out=C["ident"][:, :], in_=C["ident"][:, :], compare_op=ALU.not_equal, fill=1.0,
                               base=0, pattern=[[-1, P]], channel_multiplier=1).then_inc(done, 1)
            pool.affine_select(out=C["before"][:, :], in_=C["before"][:, :], compare_op=ALU.is_gt, fill=0.0,
                               base=0, pattern=[[1, P]], channel_multiplier=-1).then_inc(done, 1)
            pool.affine_select(out=C["not_before"][:, :], in_=C["not_before"][:, :], compare_op=ALU.is_ge, fill=0.0,
                               base=0, pattern=[[-1, P]], channel_multiplier=1).then_inc(done, 1)
            nb = C["blocks"]
            pool.iota(C["block_ramp"][:, :], [[1, nb]], base=0, channel_multiplier=0,
                      allow_small_or_imprecise_dtypes=True).then_inc(done, 1)
            pool.iota(C["node_ramp"][:, :], [[1, P]], base=0, channel_multiplier=0,
                      allow_small_or_imprecise_dtypes=True).then_inc(done, 1)
            pool.wait_ge(done, 7)


def make_hot(nc, C, hot, blk, g, nb):
    return nc.vector.tensor_tensor(hot[:, :].rearrange("p (c b) -> p c b", c=RANKED), bcast(C["block_ramp"][:, :], 1, RANKED),
                             bcast(blk[:, bass.ds(g * RANKED, RANKED)], 2, nb), ALU.is_equal)


def count_both(nc, C, src, dst, cols, nb, totals, counts, unsorted):
    W = RANKED * nb
    n = cols // RANKED
    e_pad = P * cols
    ctx = ExitStack()
    with ctx:
        a = Names(nc, ctx, "count")
        keys = [a.sb(f"keys{i}", [P, cols], I32) for i in range(2)]
        after = a.sb("after", [P, cols], I32)
        of_block = [a.sb(f"of_block{i}", [P, cols], I32) for i in range(2)]
        after_block = a.sb("after_block", [P, cols], I32)
        blk = [a.sb(f"blk{i}", [P, cols], BF16) for i in range(2)]
        falls = a.sb("falls", [P, cols])
        fall = a.sb("fall", [P, 1])
        hot = [[a.sb(f"hot{i}_{u}", [P, W], BF16) for u in range(2)] for i in range(2)]
        totals_ps = [[a.ps(f"totals{i}_{u}") for u in range(2)] for i in range(2)]
        fall_ps = a.ps("falls_sum")
        loaded, ch, last_ready, fall_ready, fall_summed = (
            a.sem(s) for s in ("loaded", "chain", "last_ready", "fall_ready", "fall_summed"))
        hot_ready = [a.sem(f"hot_ready{i}") for i in range(2)]
        summed = [a.sem(f"summed{i}") for i in range(2)]
        block = ctx.enter_context(nc.Block())

        @block.sync
        def _(sp):
            for i, key in enumerate((src, dst)):
                sp.dma_start(keys[i][:, :], key.rearrange("(p c) -> p c", p=P)).then_inc(loaded, 16)
            sp.wait_ge(last_ready, 1)
            flat = dst[1:1 + (P - 1) * cols].rearrange("(p c) -> p c", p=P - 1)
            sp.dma_start(after[0:P - 1, :], flat).then_inc(loaded, 16)
            sp.dma_start(after[P - 1:P, 0:cols - 1], dst[1 + (P - 1) * cols:e_pad].rearrange("(p c) -> p c", p=1))\
                .then_inc(loaded, 16)

        @block.tensor
        def _(pe):
            def count_batch(g, u, k):
                for i in range(2):
                    pe.wait_ge(hot_ready[i], g + 1)
                    nc.tensor.matmul(totals_ps[i][u][:, 0:W], C["ones"][:, :], hot[i][u][:, :],
                                     start=before(g, 2), stop=isinstance(g, int) and g >= n - 2).then_inc(summed[i], 1)
            loop_pairs(pe, n - 2, count_batch)
            for g in (n - 2, n - 1):
                count_batch(g, g % 2, None)
            pe.wait_ge(fall_ready, 1)
            nc.tensor.matmul(fall_ps[:, 0:1], C["ones_f32"][:, :], fall[:, :], start=True, stop=True).then_inc(fall_summed, 1)

        @block.vector
        def _(dve):
            chain = [0]

            def link(ins):
                chain[0] += 1
                ins.then_inc(ch, 1)
                dve.wait_ge(ch, chain[0])

            nc.vector.memset(after[:, cols - 1:cols], (nb + 1) * P).then_inc(last_ready, 1)
            dve.wait_ge(loaded, 64)
            link(nc.vector.tensor_scalar(of_block[1][:, :], keys[1][:, :], 7, None, ALU.logical_shift_right))
            link(nc.vector.tensor_scalar(of_block[0][:, :], keys[0][:, :], 7, None, ALU.logical_shift_right))
            link(nc.vector.tensor_copy(blk[1][:, :], of_block[1][:, :]))
            link(nc.vector.tensor_scalar(after_block[:, :], after[:, :], 7, None, ALU.logical_shift_right))
            link(nc.vector.tensor_copy(blk[0][:, :], of_block[0][:, :]))

            def count_batch(g, u, k):
                for i in range(2):
                    if not before(g, 2):
                        dve.wait_ge(summed[i], g - 1)
                    make_hot(nc, C, hot[i][u], blk[i], g, nb).then_inc(hot_ready[i], 1)
            loop_pairs(dve, n, count_batch)
            link(nc.vector.tensor_tensor(falls[:, :], of_block[1][:, :], after_block[:, :], ALU.is_gt))
            nc.vector.tensor_reduce(fall[:, :], falls[:, :], AXX, ALU.add).then_inc(fall_ready, 1)
            for i in range(2):
                dve.wait_ge(summed[i], n)
                for u in range(2):
                    link(nc.vector.tensor_copy(totals[i][:, u * W:(u + 1) * W], totals_ps[i][u][:, 0:W]))
                link(nc.vector.tensor_reduce(counts[i][:, :], totals[i][:, :].rearrange("p (c b) -> p b c", c=2 * RANKED), AXX, ALU.add))
            dve.wait_ge(fall_summed, 1)
            link(nc.vector.tensor_scalar(unsorted[:, :], fall_ps[0:1, 0:1], 1.0, None, ALU.min))


def rank(nc, C, stage, key, cols, nb, pos_dram, total, count):
    W = RANKED * nb
    n = cols // RANKED
    ctx = ExitStack()
    with ctx:
        a = Names(nc, ctx, stage)
        keys = a.sb("keys", [P, cols], I32)
        of_block = a.sb("of_block", [P, cols], I32)
        blk = a.sb("blk", [P, cols], BF16)
        hot = [a.sb(f"hot{i}", [P, W], BF16) for i in range(4)]
        picked = [a.sb(f"picked{i}", [P, W]) for i in range(4)]
        place = a.sb("place", [P, cols])
        own = a.sb("own", [P, cols])
        padding = a.sb("padding", [P, cols])
        place_i = a.sb("place_i", [P, cols], I32)
        base = a.sb("base", [P, 2 * W])
        end = a.sb("end", [P, nb])
        zeros = a.sb("zeros", [P, nb])
        ranks_ps = [a.ps(f"ranks{i}") for i in range(2)]
        loaded, ch, iota_done = a.sem("loaded"), a.sem("chain"), a.sem("iota")
        base_ready, based = a.sem("base_ready"), a.sem("based")
        hot_ready, ranked, read, advanced = a.sem("hot_ready"), a.sem("ranked"), a.sem("read"), a.sem("advanced")
        reduced, stored = a.sem("reduced"), a.sem("stored")
        block = ctx.enter_context(nc.Block())

        @block.sync
        def _(sp):
            sp.dma_start(keys[:, :], key.rearrange("(p c) -> p c", p=P)).then_inc(loaded, 16)
            sp.wait_ge(stored, 1)
            sp.dma_start(pos_dram.rearrange("(p c) -> p c", p=P), place_i[:, :]).then_inc(loaded, 16)
            sp.wait_ge(loaded, 32)

        @block.gpsimd
        def _(pool):
            pool.iota(own[:, :], [[1, cols]], base=0, channel_multiplier=cols,
                      allow_small_or_imprecise_dtypes=True).then_inc(iota_done, 1)

        @block.tensor
        def _(pe):
            pe.wait_ge(base_ready, 1)
            for v in range(2):
                nc.tensor.matmul(ranks_ps[v][:, 0:W], C["ident"][:, :], base[:, v * W:(v + 1) * W], start=True, stop=True)\
                    .then_inc(based, 1)

            def advance(g, u, k):
                pe.wait_ge(read, g + 1)
                nc.tensor.matmul(ranks_ps[u % 2][:, 0:W], C["not_before"][:, :], hot[u][:, :], start=False, stop=True,
                                 skip_group_check=True).then_inc(advanced, 1)

            def rank_batch(g, u, k):
                if not before(g, 2):
                    advance(*shifted(g, u, k, -2))
                pe.wait_ge(hot_ready, g + 1)
                nc.tensor.matmul(ranks_ps[u % 2][:, 0:W], C["before"][:, :], hot[u][:, :], start=False, stop=True,
                                 skip_group_check=True).then_inc(ranked, 1)
            loop_blocks(pe, n, rank_batch, UNROLL)

        @block.scalar
        def _(act):
            def reduce_batch(g, u, k):
                act.wait_ge(read, g + 1)
                for c in range(RANKED):
                    last_ = nc.scalar.activation(picked[u][:, c * nb:(c + 1) * nb], picked[u][:, c * nb:(c + 1) * nb], ACT.Copy,
                                                 accum_out=place[:, bass.ds(g * RANKED + c, 1)])
                last_.then_inc(reduced, 1)
            loop_blocks(act, n, reduce_batch, UNROLL)

        @block.vector
        def _(dve):
            chain = [0]

            def link(ins):
                chain[0] += 1
                ins.then_inc(ch, 1)
                dve.wait_ge(ch, chain[0])

            dve.wait_ge(loaded, 16)
            link(nc.vector.tensor_scalar(of_block[:, :], keys[:, :], 7, None, ALU.logical_shift_right))
            link(nc.vector.tensor_copy(blk[:, :], of_block[:, :]))
            link(nc.vector.memset(zeros[:, :], 0.0))
            link(nc.vector.tensor_tensor_scan(end[:, :], count[:, :], zeros[:, :], 0.0, ALU.add, ALU.add))
            link(nc.vector.tensor_tensor(base[:, 0:nb], end[:, :], count[:, :], ALU.subtract))
            for c in range(1, 2 * RANKED):
                ins = nc.vector.tensor_tensor(base[:, c * nb:(c + 1) * nb], base[:, (c - 1) * nb:c * nb],
                                              total[:, (c - 1) * nb:c * nb], ALU.add)
                if c < 2 * RANKED - 1:
                    link(ins)
                else:
                    ins.then_inc(base_ready, 1)
            dve.wait_ge(based, 2)

            def hot_batch(g, u, k):
                if not before(g, 4):
                    dve.wait_ge(advanced, g - 3)
                make_hot(nc, C, hot[u], blk, g, nb).then_inc(hot_ready, 1)

            def step(g, u, k):
                dve.wait_ge(ranked, g + 1)
                if not before(g, 4):
                    dve.wait_ge(reduced, g - 3)
                nc.vector.tensor_tensor(picked[u][:, :], ranks_ps[u % 2][:, 0:W], hot[u][:, :], ALU.mult).then_inc(read, 1)
                if not (isinstance(g, int) and g >= n - 2):
                    hot_batch(*shifted(g, u, k, 2))
            hot_batch(0, 0, 0)
            hot_batch(1, 1, 0)
            loop_blocks(dve, n, step, UNROLL)
            dve.wait_ge(iota_done, 1)
            dve.wait_ge(reduced, n)
            link(nc.vector.tensor_scalar(padding[:, :], blk[:, :], float(nb), None, ALU.is_ge))
            link(nc.vector.tensor_tensor(padding[:, :], padding[:, :], own[:, :], ALU.mult))
            nc.vector.tensor_tensor(place_i[:, :], place[:, :], padding[:, :], ALU.add).then_inc(stored, 1)


def group_table(nc, C, stage, count, nb, n_edges, ng, meta_dram, table, last):
    cols = -(-ng // P)
    ctx = ExitStack()
    with ctx:
        a = Names(nc, ctx, stage)
        up = a.sb("up", [P, nb], I32)
        groups_i = a.sb("groups_i", [P, nb], I32)
        groups = a.sb("groups", [P, nb])
        zeros = a.sb("zeros", [P, nb])
        end = a.sb("end", [P, nb])
        start = a.sb("start", [P, nb])
        slack = a.sb("slack", [P, nb])
        g_of = a.sb("g_of", [P, cols])
        junk = a.sb("junk", [P, nb])
        out = a.sb("out", [P, 3, cols])
        ch, iota_done, made, moved = a.sem("chain"), a.sem("iota"), a.sem("made"), a.sem("moved")
        block = ctx.enter_context(nc.Block())

        @block.gpsimd
        def _(pool):
            pool.iota(g_of[:, :], [[P, cols]], base=0, channel_multiplier=1,
                      allow_small_or_imprecise_dtypes=True).then_inc(iota_done, 1)

        @block.vector
        def _(dve):
            chain = [0]

            def link(ins):
                chain[0] += 1
                ins.then_inc(ch, 1)
                dve.wait_ge(ch, chain[0])

            link(nc.vector.tensor_scalar(up[:, :], count[:, :], float(G - 1), None, ALU.add))
            link(nc.vector.tensor_scalar(groups_i[:, :], up[:, :], G.bit_length() - 1, None, ALU.logical_shift_right))
            link(nc.vector.tensor_scalar(groups[:, :], groups_i[:, :], 1.0, None, ALU.max))
            link(nc.vector.memset(zeros[:, :], 0.0))
            link(nc.vector.tensor_tensor_scan(end[:, :], groups[:, :], zeros[:, :], 0.0, ALU.add, ALU.add))
            link(nc.vector.tensor_tensor(start[:, :], end[:, :], groups[:, :], ALU.subtract))
            link(nc.vector.scalar_tensor_tensor(slack[:, :], groups[:, :], float(-G), count[:, :], ALU.mult, ALU.add))
            link(nc.vector.tensor_scalar(last[:, :], end[0:1, :], -1.0, None, ALU.add))
            dve.wait_ge(iota_done, 1)
            for c in range(cols):
                g = g_of[:, c:c + 1]
                link(nc.vector.scalar_tensor_tensor(junk[:, :], end[:, :], g, slack[:, :], ALU.is_le, ALU.mult))
                link(nc.vector.tensor_reduce(out[:, 0, c:c + 1], junk[:, :], AXX, ALU.add))
                link(nc.vector.tensor_scalar(junk[:, :], end[:, :], g, float(P), ALU.is_le, ALU.mult))
                link(nc.vector.tensor_reduce(out[:, 1, c:c + 1], junk[:, :], AXX, ALU.add))
                link(nc.vector.tensor_scalar(junk[:, :], start[:, :], g, None, ALU.is_equal))
                link(nc.vector.tensor_reduce(out[:, 2, c:c + 1], junk[:, :], AXX, ALU.add))
            link(nc.vector.scalar_tensor_tensor(out[:, 0, :], g_of[:, :], float(G), out[:, 0, :], ALU.mult, ALU.add))
            link(nc.vector.tensor_scalar(out[:, 0, :], out[:, 0, :], float(n_edges), None, ALU.min))
            nc.vector.tensor_scalar(out[:, 2, :], out[:, 2, :], -1.0, 1.0, ALU.mult, ALU.add).then_inc(made, 1)

        @block.sync
        def _(sp):
            sp.wait_ge(made, 1)
            with nc.allow_non_contiguous_dma(reason="a table of a few hundred words"):
                for r in range(3):
                    sp.dma_start(meta_dram[r, :].rearrange("(c p) -> p c", p=P), out[:, r, :]).then_inc(moved, 16)
            sp.wait_ge(moved, 48)
            for r in range(3):
                sp.dma_start(table[:, r, :], meta_dram[r:r + 1, 0:ng].to_broadcast([P, ng])).then_inc(moved, 16)
            sp.wait_ge(moved, 96)


def ids_in_order(nc, C, A, posb, ids_a, cols):
    ctx = ExitStack()
    with ctx:
        a = Names(nc, ctx, "ids")
        ids = a.sb("ids", [P, cols, 3], I32)
        one = [a.sb(f"one{i}", [P, cols], I32) for i in range(3)]
        loaded, ids_ready, stored = a.sem("loaded"), a.sem("ids_ready"), a.sem("stored")
        block = ctx.enter_context(nc.Block())
        idle(C, block.scalar, block.tensor, block.gpsimd)

        @block.sync
        def _(sp):
            for i, x in enumerate((A["src"], A["dst"], posb)):
                sp.dma_start(one[i][:, :], x.rearrange("(p c) -> p c", p=P)).then_inc(loaded, 16)
            sp.wait_ge(ids_ready, 3)
            sp.dma_start(ids_a.rearrange("(p c) w -> p c w", p=P), ids[:, :, :]).then_inc(stored, 16)
            sp.wait_ge(stored, 16)

        @block.vector
        def _(dve):
            dve.wait_ge(loaded, 48)
            for i in range(3):
                nc.vector.tensor_copy(ids[:, :, i], one[i][:, :]).then_inc(ids_ready, 1)


def to_destination_order(nc, C, A, posa, posb, attr0_a, attr1_a, ids_a, cols):
    n = cols // RANKED
    ctx = ExitStack()
    with ctx:
        a = Names(nc, ctx, "pack")
        place = a.sb("place", [P, cols], I32)
        ids = a.sb("ids", [P, cols, 3], I32)
        one = [a.sb(f"one{i}", [P, cols], I32) for i in range(3)]
        r0 = [a.sb(f"r0_{i}", [P, RANKED, ATTR0]) for i in range(2)]
        r1 = [a.sb(f"r1_{i}", [P, RANKED, ATTR1]) for i in range(2)]
        r2 = [a.sb(f"r2_{i}", [P, RANKED, 3], I32) for i in range(2)]
        at = [a.sb(f"at{i}", [P, RANKED], I32) for i in range(2)]
        loaded, ids_ready, packed = a.sem("loaded"), a.sem("ids_ready"), a.sem("packed")
        filled = [a.sem(f"filled{i}") for i in range(2)]
        scattered = [a.sem(f"scattered{i}") for i in range(2)]
        block = ctx.enter_context(nc.Block())
        idle(C, block.scalar, block.tensor)

        def columns(ap, g):
            return ap.rearrange("(p c) w -> p c w", p=P)[:, bass.ds(g * RANKED, RANKED), :]

        @block.sync
        def _(sp):
            for i, x in enumerate((A["src"], A["dst"], posb)):
                sp.dma_start(one[i][:, :], x.rearrange("(p c) -> p c", p=P)).then_inc(loaded, 16)
            sp.dma_start(place[:, :], posa.rearrange("(p c) -> p c", p=P)).then_inc(loaded, 16)

            def load(g, u, k):
                if not before(g, 2):
                    sp.wait_ge(scattered[u], k * (48 * RANKED))
                    settle(sp, C)
                sp.dma_start(r0[u][:, :, :], columns(A["attr0"], g)).then_inc(filled[u], 16)
                sp.dma_start(r1[u][:, :, :], columns(A["attr1"], g)).then_inc(filled[u], 16)
            loop_pairs(sp, n, load)

        @block.vector
        def _(dve):
            dve.wait_ge(loaded, 64)
            for i in range(3):
                nc.vector.tensor_copy(ids[:, :, i], one[i][:, :]).then_inc(ids_ready, 1)
            dve.wait_ge(ids_ready, 3)

            def pack(g, u, k):
                if not before(g, 2):
                    dve.wait_ge(scattered[u], k * (48 * RANKED))
                nc.vector.tensor_copy(r2[u][:, :, :], ids[:, bass.ds(g * RANKED, RANKED), :]).then_inc(packed, 1)
                nc.vector.tensor_copy(at[u][:, :], place[:, bass.ds(g * RANKED, RANKED)]).then_inc(packed, 1)
            loop_pairs(dve, n, pack)

        @block.gpsimd
        def _(pool):
            def scatter(g, u, k):
                pool.wait_ge(filled[u], k * 32 + 32)
                pool.wait_ge(packed, g * 2 + 2)
                settle(pool, C)
                for j in range(RANKED):
                    for out, row in ((attr0_a, r0), (attr1_a, r1), (ids_a, r2)):
                        pool.indirect_dma_start(
                            out=out, out_offset=bass.IndirectOffsetOnAxis(ap=at[u][:, j:j + 1], axis=0),
                            in_=row[u][:, j, :], in_offset=None).then_inc(scattered[u], 16)
            loop_pairs(pool, n, scatter)
            for u in range(2):
                pool.wait_ge(scattered[u], 48 * RANKED * (n // 2))


def before_gnn0(nc, C, x, attr, Wn, nb, x1, base):
    U = LONG_UNROLL
    ctx = ExitStack()
    with ctx:
        a = Names(nc, ctx, "node0")
        xin = [a.sb(f"x{i}", [P, D]) for i in range(U)]
        at = [a.sb(f"attr{i}", [P, 3]) for i in range(U)]
        hs = [a.sb(f"h{i}", [P, D]) for i in range(2)]
        hT = [a.sb(f"hT{i}", [P, 2 * P]) for i in range(2)]
        o1 = [a.sb(f"x1_{i}", [P, D]) for i in range(U)]
        ob = [a.sb(f"base{i}", [P, D]) for i in range(U)]
        tmp = [a.sb(f"tmp{i}", [P, 2 * D]) for i in range(2)]
        st, rs = a.sb("st", [P, 6]), a.sb("rs", [P, 1])
        mv = [a.sb(f"mv{i}", [P, 2]) for i in range(2)]
        sd = [a.sb(f"sd{i}", [P, 1]) for i in range(2)]
        eps = a.sb("eps", [P, 1])
        tps = [a.ps(f"t{i}") for i in range(2)]
        sps = [a.ps(f"s{i}") for i in range(2)]
        vps = [a.ps(f"v{i}") for i in range(2)]
        ld = [a.sem(f"loaded{i}") for i in range(U)]
        stx = [a.sem(f"stored{i}") for i in range(U)]
        zero = a.sb("zero", [P, D])
        zero_ready, zero_out, eps_ready = a.sem("zero_ready"), a.sem("zero_out"), a.sem("eps_ready")
        stats_ready, var, root, inverse, h_ready, tr, ev, mm, halves, sums, made = (
            a.sem(s) for s in ("stats_ready", "var", "root", "inverse", "h_ready", "transposed", "evacuated", "mixed",
                               "halves", "sums", "made"))
        block = ctx.enter_context(nc.Block())

        def rows(ap, b):
            return ap[bass.ds(b * P, P), :]

        @block.sync
        def _(sp):
            def step(b, u, k):
                if not before(b, U):
                    sp.wait_ge(made, b - (U - 1))
                settle(sp, C)
                sp.dma_start(xin[u][:, :], rows(x, b)).then_inc(ld[u], 16)
                sp.dma_start(at[u][:, :], rows(attr, b)).then_inc(ld[u], 16)
            loop_blocks(sp, nb, step)

        @block.vector
        def _(dve):
            nc.vector.memset(eps[:, :], LN_EPS).then_inc(eps_ready, 1)
            nc.vector.memset(zero[:, :], 0.0).then_inc(zero_ready, 1)

            def stats(b, u, k):
                dve.wait_ge(ld[u], k * 32 + 32)
                if not before(b, 1):
                    dve.wait_ge(var, b)
                if not before(b, 2):
                    dve.wait_ge(h_ready, b - 1)
                nc.vector.bn_stats(st[:, :], xin[u][:, :]).then_inc(stats_ready, 1)
                dve.wait_ge(stats_ready, b + 1)
                settle(dve, C)
                nc.vector.bn_aggr(mv[u % 2][:, :], st[:, :]).then_inc(var, 1)

            def norm(b, u, k):
                dve.wait_ge(root, b + 1)
                if not before(b, 1):
                    dve.wait_ge(h_ready, b)
                nc.vector.reciprocal(rs[:, :], sd[u % 2][:, :]).then_inc(inverse, 1)
                dve.wait_ge(inverse, b + 1)
                if not before(b, 2):
                    dve.wait_ge(tr, b - 1)
                nc.vector.tensor_scalar(hs[u % 2][:, :], xin[u][:, :], mv[u % 2][:, 0:1], rs[:, :], ALU.subtract, ALU.mult)\
                    .then_inc(h_ready, 1)

            def mix(b, u, k):
                v = u % 2
                dve.wait_ge(mm, b + 1)
                if not before(b, 2):
                    dve.wait_ge(made, b - 1)
                s4 = sps[v][:, 0:4 * MS].rearrange("p (l a f) -> p l a f", l=2, a=2)
                v4 = vps[v][:, 0:4 * 96].rearrange("p (l a f) -> p l a f", l=2, a=2)
                t2 = tmp[v][:, :].rearrange("p (l f) -> p l f", l=2)
                nc.vector.tensor_scalar(t2[:, :, 0:MS], s4[:, :, 0, :], at[u][:, 0:1], None, ALU.mult)
                nc.vector.tensor_scalar(t2[:, :, MS:D], v4[:, :, 0, :], at[u][:, 0:1], None, ALU.mult).then_inc(halves, 1)
                dve.wait_ge(halves, b + 1)
                if not before(b, U):
                    dve.wait_ge(stx[u], k * 32)
                nc.vector.scalar_tensor_tensor(ob[u][:, 0:MS], s4[:, 1, 1, :], at[u][:, 1:2], t2[:, 1, 0:MS], ALU.mult, ALU.add)
                nc.vector.scalar_tensor_tensor(ob[u][:, MS:D], v4[:, 1, 1, :], at[u][:, 1:2], t2[:, 1, MS:D], ALU.mult, ALU.add)\
                    .then_inc(sums, 1)
                nc.vector.scalar_tensor_tensor(o1[u][:, 0:MS], s4[:, 0, 1, :], at[u][:, 1:2], t2[:, 0, 0:MS], ALU.mult, ALU.add)
                nc.vector.scalar_tensor_tensor(o1[u][:, MS:D], v4[:, 0, 1, :], at[u][:, 1:2], t2[:, 0, MS:D], ALU.mult, ALU.add)
                dve.wait_ge(sums, b + 1)
                nc.vector.tensor_tensor(ob[u][:, :], ob[u][:, :], xin[u][:, :], ALU.add).then_inc(made, 1)

            def step(b, u, k):
                if not is_last(b, nb):
                    stats(*shifted(b, u, k, 1, U))
                norm(b, u, k)
                if not before(b, 2):
                    mix(*shifted(b, u, k, -2, U))
            stats(0, 0, 0)
            loop_blocks(dve, nb, step)
            for b in (nb - 2, nb - 1):
                mix(b, b % U, b // U)

        @block.scalar
        def _(act):
            act.wait_ge(eps_ready, 1)

            def deviation(b, u, k):
                act.wait_ge(var, b + 1)
                if not before(b, 2):
                    act.wait_ge(inverse, b - 1)
                nc.scalar.activation(sd[u % 2][:, :], mv[u % 2][:, 1:2], ACT.Sqrt, bias=eps[:, :]).then_inc(root, 1)

            def step(b, u, k):
                if not is_last(b, nb):
                    deviation(*shifted(b, u, k, 1, U))
                act.wait_ge(tr, b + 1)
                if not before(b, 2):
                    act.wait_ge(mm, b - 1)
                nc.scalar.activation(hT[u % 2][0:96, :], tps[u % 2][0:96, 0:2 * P], ACT.Relu).then_inc(ev, 1)
            deviation(0, 0, 0)
            loop_blocks(act, nb, step)

        @block.tensor
        def _(pe):
            def transpose_h(b, u, k):
                v = u % 2
                pe.wait_ge(h_ready, b + 1)
                if not before(b, 2):
                    pe.wait_ge(ev, b - 1)
                settle(pe, C)
                nc.tensor.transpose(tps[v][0:96, 0:P], hs[v][:, 0:96], C["ident"][:, :])
                nc.tensor.transpose(tps[v][0:96, P:2 * P], hs[v][:, MS:D], C["ident"][:, :]).then_inc(tr, 1)

            def mix(b, u, k):
                v = u % 2
                pe.wait_ge(ev, b + 1)
                if not before(b, 2):
                    pe.wait_ge(made, b - 1)
                settle(pe, C)
                nc.tensor.matmul(sps[v][:, 0:4 * MS], hT[v][0:MS, 0:P], Wn["s0"][0:MS, :], start=True, stop=True)
                nc.tensor.matmul(vps[v][:, 0:4 * 96], hT[v][0:96, P:2 * P], Wn["v0"][0:96, :], start=True, stop=True).then_inc(mm, 1)

            def step(b, u, k):
                transpose_h(b, u, k)
                if not before(b, 1):
                    mix(*shifted(b, u, k, -1, U))
            loop_blocks(pe, nb, step)
            mix(nb - 1, (nb - 1) % U, (nb - 1) // U)

        @block.gpsimd
        def _(pool):
            pool.wait_ge(zero_ready, 1)
            pool.dma_start(x1[nb * P:(nb + 1) * P, :], zero[:, :]).then_inc(zero_out, 16)
            pool.wait_ge(zero_out, 16)

            def step(b, u, k):
                pool.wait_ge(made, b + 1)
                settle(pool, C)
                pool.dma_start(rows(x1, b), o1[u][:, :]).then_inc(stx[u], 16)
                pool.dma_start(rows(base, b), ob[u][:, :]).then_inc(stx[u], 16)
            loop_blocks(pool, nb, step)
            for u in range(U):
                pool.wait_ge(stx[u], 32 * times(u, nb))


def prepare_weights(nc, C, Wd, Wn):
    ctx = ExitStack()
    with ctx:
        a = Names(nc, ctx, "weights")
        l2 = {k: a.sb(f"l2{k}", [96, 96]) for k in ("sa", "sc", "va", "vc")}
        l3s, l3v = a.sb("l3s", [96, MS]), a.sb("l3v", [96, MV])
        l2T = a.sb("l2T", [96, 4 * 96])
        tps, mps = a.ps("t"), a.ps("m")
        zeroed, loaded, scaled, tr, ev, mm = (a.sem(s) for s in ("zeroed", "loaded", "scaled", "tr", "ev", "mm"))
        block = ctx.enter_context(nc.Block())
        loads = []
        for i, m in enumerate(("Ws_l1_a", "Ws_l1_c", "Ws_sc_a", "Ws_sc_c")):
            loads.append((Wn["s0"][0:MS, i * MS:(i + 1) * MS], Wd["L0_gnn_" + m][:, :]))
        for i, m in enumerate(("Wv_l1_a", "Wv_l1_c", "Wv_sc_a", "Wv_sc_c")):
            for c in range(3):
                loads.append((Wn["v0"][c * MV:(c + 1) * MV, i * 96 + c * MV:i * 96 + (c + 1) * MV], Wd["L0_gnn_" + m][:, :]))
        for j in range(TILES):
            loads.append((Wn["fc1_0"][j * ATTR0:j * ATTR0 + 10, j * H0:(j + 1) * H0], Wd["L0_gnn_W_fc1"][:, :]))
        for j in range(2):
            loads.append((Wn["fc1_1"][j * 64:(j + 1) * 64, j * 64:(j + 1) * 64], Wd["L1_gnn_W_fc1"][:, :]))
            loads.append((Wn["fc2_1"][j * 64:(j + 1) * 64, j * WN1:(j + 1) * WN1], Wd["L1_gnn_W_fc2"][:, :]))
        for to, of, n in ((0, 0, MS), (MS, 2 * MS, MV), (MS + MV, MS, MS), (2 * MS + MV, 2 * MS + MV, MV)):
            loads.append((Wn["fc2_0"][0:H0, to:to + n], Wd["L0_gnn_W_fc2"][:, of:of + n]))
        for k, m in (("sa", "Ws_l2_a"), ("sc", "Ws_l2_c"), ("va", "Wv_l2_a"), ("vc", "Wv_l2_c")):
            loads.append((l2[k][:, :], Wd["L0_gnn_" + m][:, :]))
        loads.append((l3s[:, :], Wd["L0_gnn_Ws_l3"][:, :]))
        loads.append((l3v[:, :], Wd["L0_gnn_Wv_l3"][:, :]))
        loads.append((Wn["s1"][0:MS, 0:MS], Wd["L1_gnn_W_nl0"][:, :]))
        loads.append((Wn["s1"][0:MS, MS:MS + 96], Wd["L1_gnn_W_skip0"][:, :]))
        for i, m in enumerate(("W_nl1", "W_skip1")):
            for c in range(3):
                loads.append((Wn["v1"][c * MV:(c + 1) * MV, i * 96 + c * MV:i * 96 + (c + 1) * MV], Wd["L1_gnn_" + m][:, :]))
        loads.append((Wn["outs"][0:96, :], Wd["L1_gnn_W_out_s"][:, :]))
        loads.append((Wn["outv"][:, :], Wd["L1_gnn_W_out_v"][:, :]))

        @block.sync
        def _(sp):
            sp.wait_ge(zeroed, 5)
            for to, of in loads:
                sp.dma_start(to, of).then_inc(loaded, 16)

        @block.vector
        def _(dve):
            for k in ("v0", "v1", "fc1_0", "fc1_1", "fc2_1"):
                nc.vector.memset(Wn[k][:, :], 0.0).then_inc(zeroed, 1)
            dve.wait_ge(loaded, 16 * len(loads))
            for w, f in ((Wn["s0"][0:MS, 2 * MS:4 * MS], C_S), (Wn["v0"][0:96, 2 * 96:4 * 96], C_S),
                         (Wn["fc2_0"][0:H0, 2 * MS + MV:WN0], 3.0 ** -0.5), (Wn["fc2_1"][:, 160:192], 3.0 ** -0.5),
                         (Wn["fc2_1"][:, 192:224], 2.0 ** -0.5), (Wn["fc2_1"][:, WN1 + 160:WN1 + 192], 3.0 ** -0.5),
                         (Wn["fc2_1"][:, WN1 + 192:WN1 + 224], 2.0 ** -0.5), (Wn["outs"][0:96, :], 1 / 32.0),
                         (Wn["outv"][:, :], 1 / 32.0)):
                nc.vector.tensor_scalar(w, w, f, None, ALU.mult).then_inc(scaled, 1)
            dve.wait_ge(tr, 1)
            nc.vector.tensor_copy(l2T[:, :], tps[0:96, 0:4 * 96]).then_inc(ev, 1)
            dve.wait_ge(mm, 1)
            nc.vector.tensor_scalar(Wn["ps"][0:96, :], mps[0:96, 0:2 * MS], C_X / 4.0, None, ALU.mult).then_inc(scaled, 1)
            nc.vector.tensor_scalar(Wn["pv"][0:96, :], mps[0:96, 2 * MS:2 * MS + 2 * MV], C_X / 4.0, None, ALU.mult).then_inc(scaled, 1)
            dve.wait_ge(scaled, 11)

        @block.tensor
        def _(pe):
            pe.wait_ge(loaded, 16 * len(loads))
            for i, k in enumerate(("sa", "sc", "va", "vc")):
                last = nc.tensor.transpose(tps[0:96, i * 96:(i + 1) * 96], l2[k][:, :], C["ident"][0:96, 0:96])
            last.then_inc(tr, 1)
            pe.wait_ge(ev, 1)
            at = 0
            for i, w, n in ((0, l3s, MS), (1, l3s, MS), (2, l3v, MV), (3, l3v, MV)):
                last = nc.tensor.matmul(mps[0:96, at:at + n], l2T[:, i * 96:(i + 1) * 96], w[:, :], start=True, stop=True)
                at += n
            last.then_inc(mm, 1)


def between(nc, C, agg, last, base, attr, Wn, nb, x2, sv, skip):
    U = LONG_UNROLL
    ctx = ExitStack()
    with ctx:
        a = Names(nc, ctx, "node1")
        def several(n, name, shape):
            return [a.sb(f"{name}{i}", shape) for i in range(n)]
        ag, bs, at = several(U, "agg", [P, AGG0]), several(U, "base", [P, D]), several(U, "attr", [P, 3])
        mT, hT, hs = several(2, "mT", [P, 4 * P]), several(2, "hT", [P, 2 * P]), several(2, "h", [P, D])
        xo, so, ko = several(U, "x2", [P, D]), several(U, "sv", [P, D]), several(U, "skip", [P, 192])
        mv, sd = several(2, "mv", [P, 2]), several(2, "sd", [P, 1])
        am, st, rs, eps = a.sb("am", [P, 2]), a.sb("st", [P, 6]), a.sb("rs", [P, 1]), a.sb("eps", [P, 1])
        mps, ops = [a.ps(f"m{i}") for i in range(2)], [a.ps(f"o{i}") for i in range(2)]
        hps, kps = a.ps("h"), [a.ps(f"k{i}") for i in range(2)]
        ld = [a.sem(f"loaded{i}") for i in range(U)]
        stx = [a.sem(f"stored{i}") for i in range(U)]
        eps_ready, masked, first, x2_ready, stats_ready, inverse = (
            a.sem(s) for s in ("eps_ready", "masked", "first", "x2_ready", "stats_ready", "inverse"))
        mtr, mev, mmm, var, root, h_ready, htr, hev, hmm, made = (
            a.sem(s) for s in ("mtr", "mev", "mmm", "var", "root", "h_ready", "htr", "hev", "hmm", "made"))
        block = ctx.enter_context(nc.Block())
        agg_rows = agg.rearrange("g p f -> (g p) f")

        def rows(ap, b):
            return ap[bass.ds(b * P, P), :]

        @block.sync
        def _(sp):
            def step(b, u, k):
                if not before(b, U):
                    sp.wait_ge(var, b - (U - 1))
                settle(sp, C)
                g = sp.value_load(last[0:1, bass.ds(b, 1)], min_val=0, max_val=agg.shape[0] - 1)
                sp.dma_start(ag[u][:, :], agg_rows[bass.ds(g * P, P), :]).then_inc(ld[u], 16)
                sp.dma_start(bs[u][:, :], rows(base, b)).then_inc(ld[u], 16)
                sp.dma_start(at[u][:, :], rows(attr, b)).then_inc(ld[u], 16)
            loop_blocks(sp, nb, step)

        @block.vector
        def _(dve):
            nc.vector.memset(eps[:, :], LN_EPS).then_inc(eps_ready, 1)

            def norm(b, u, k):
                dve.wait_ge(root, b + 1)
                if not before(b, 1):
                    dve.wait_ge(h_ready, b)
                nc.vector.reciprocal(rs[:, :], sd[u % 2][:, :]).then_inc(inverse, 1)
                dve.wait_ge(inverse, b + 1)
                if not before(b, 2):
                    dve.wait_ge(htr, b - 1)
                nc.vector.tensor_scalar(hs[u % 2][:, :], xo[u][:, :], mv[u % 2][:, 0:1], rs[:, :], ALU.subtract, ALU.mult)\
                    .then_inc(h_ready, 1)

            def combine(b, u, k):
                v = u % 2
                dve.wait_ge(ld[u], k * 48 + 48)
                if not before(b, 1):
                    dve.wait_ge(x2_ready, b)
                nc.vector.tensor_scalar(am[:, :], at[u][:, 0:2], at[u][:, 2:3], None, ALU.mult).then_inc(masked, 1)
                dve.wait_ge(mmm, b + 1)
                dve.wait_ge(masked, b + 1)
                if not before(b, U):
                    dve.wait_ge(stx[u], k * 48)
                s2 = ops[v][:, 0:2 * MS].rearrange("p (a f) -> p a f", a=2)
                v2 = ops[v][:, 2 * MS:2 * MS + 6 * MV].rearrange("p (c a f) -> p a c f", c=3, a=2)
                xv = xo[u][:, MS:D].rearrange("p (c f) -> p c f", c=3)
                bv = bs[u][:, MS:D].rearrange("p (c f) -> p c f", c=3)
                nc.vector.scalar_tensor_tensor(xo[u][:, 0:MS], s2[:, 0, :], am[:, 0:1], bs[u][:, 0:MS], ALU.mult, ALU.add)
                nc.vector.scalar_tensor_tensor(xv, v2[:, 0, :, :], am[:, 0:1], bv, ALU.mult, ALU.add).then_inc(first, 1)
                dve.wait_ge(first, b + 1)
                nc.vector.scalar_tensor_tensor(xo[u][:, 0:MS], s2[:, 1, :], am[:, 1:2], xo[u][:, 0:MS], ALU.mult, ALU.add)
                nc.vector.scalar_tensor_tensor(xv, v2[:, 1, :, :], am[:, 1:2], xv, ALU.mult, ALU.add).then_inc(x2_ready, 1)
                dve.wait_ge(x2_ready, b + 1)
                nc.vector.bn_stats(st[:, :], xo[u][:, :]).then_inc(stats_ready, 1)
                dve.wait_ge(stats_ready, b + 1)
                settle(dve, C)
                nc.vector.bn_aggr(mv[v][:, :], st[:, :]).then_inc(var, 1)

            def step(b, u, k):
                if not before(b, 1):
                    norm(*shifted(b, u, k, -1, U))
                combine(b, u, k)
            loop_blocks(dve, nb, step)
            norm(nb - 1, (nb - 1) % U, (nb - 1) // U)

        @block.scalar
        def _(act):
            act.wait_ge(eps_ready, 1)

            def take_sums(b, u, k):
                act.wait_ge(mtr, b + 1)
                if not before(b, 2):
                    act.wait_ge(mmm, b - 1)
                nc.scalar.copy(mT[u % 2][0:96, :], mps[u % 2][0:96, :]).then_inc(mev, 1)

            def take_h(b, u, k):
                act.wait_ge(htr, b + 1)
                if not before(b, 2):
                    act.wait_ge(hmm, b - 1)
                nc.scalar.activation(hT[u % 2][0:96, :], hps[0:96, 0:2 * P], ACT.Relu).then_inc(hev, 1)

            def outputs(b, u, k):
                act.wait_ge(hmm, b + 1)
                if not before(b, U):
                    act.wait_ge(stx[u], k * 48)
                nc.scalar.copy(so[u][:, :], kps[u % 2][:, 0:D])
                nc.scalar.copy(ko[u][:, :], kps[u % 2][:, D:D + 192]).then_inc(made, 1)

            def deviation(b, u, k):
                act.wait_ge(var, b + 1)
                if not before(b, 2):
                    act.wait_ge(inverse, b - 1)
                nc.scalar.activation(sd[u % 2][:, :], mv[u % 2][:, 1:2], ACT.Sqrt, bias=eps[:, :]).then_inc(root, 1)

            def step(b, u, k):
                if not is_last(b, nb):
                    take_sums(*shifted(b, u, k, 1, U))
                if not before(b, 1):
                    take_h(*shifted(b, u, k, -1, U))
                if not before(b, 2):
                    outputs(*shifted(b, u, k, -2, U))
                deviation(b, u, k)
            take_sums(0, 0, 0)
            loop_blocks(act, nb, step)
            take_h(nb - 1, (nb - 1) % U, (nb - 1) // U)
            for b in (nb - 2, nb - 1):
                outputs(b, b % U, b // U)

        @block.tensor
        def _(pe):
            def transpose_sums(b, u, k):
                pe.wait_ge(ld[u], k * 48 + 48)
                if not before(b, 2):
                    pe.wait_ge(mev, b - 1)
                for c in range(4):
                    last_ = nc.tensor.transpose(mps[u % 2][0:96, c * P:(c + 1) * P], ag[u][:, c * 96:(c + 1) * 96], C["ident"][:, :])
                last_.then_inc(mtr, 1)

            def mix_sums(b, u, k):
                v = u % 2
                pe.wait_ge(mev, b + 1)
                if not before(b, 2):
                    pe.wait_ge(x2_ready, b - 1)
                nc.tensor.matmul(ops[v][:, 0:2 * MS], mT[v][0:96, 0:P], Wn["ps"][0:96, :], start=True, stop=True)
                for c in range(3):
                    last_ = nc.tensor.matmul(ops[v][:, 2 * MS + c * 2 * MV:2 * MS + (c + 1) * 2 * MV],
                                             mT[v][0:96, (c + 1) * P:(c + 2) * P], Wn["pv"][0:96, :], start=True, stop=True)
                last_.then_inc(mmm, 1)

            def transpose_h(b, u, k):
                pe.wait_ge(h_ready, b + 1)
                if not before(b, 1):
                    pe.wait_ge(hev, b)
                settle(pe, C)
                nc.tensor.transpose(hps[0:96, 0:P], hs[u % 2][:, 0:96], C["ident"][:, :])
                nc.tensor.transpose(hps[0:96, P:2 * P], hs[u % 2][:, MS:D], C["ident"][:, :]).then_inc(htr, 1)

            def mix_h(b, u, k):
                v = u % 2
                pe.wait_ge(hev, b + 1)
                if not before(b, 2):
                    pe.wait_ge(made, b - 1)
                settle(pe, C)
                nc.tensor.matmul(kps[v][:, 0:MS], hT[v][0:MS, 0:P], Wn["s1"][0:MS, 0:MS], start=True, stop=True)
                nc.tensor.matmul(kps[v][:, MS:D], hT[v][0:96, P:2 * P], Wn["v1"][0:96, 0:96], start=True, stop=True)
                nc.tensor.matmul(kps[v][:, D:D + 96], hT[v][0:MS, 0:P], Wn["s1"][0:MS, MS:MS + 96], start=True, stop=True)
                nc.tensor.matmul(kps[v][:, D + 96:D + 192], hT[v][0:96, P:2 * P], Wn["v1"][0:96, 96:192], start=True, stop=True)\
                    .then_inc(hmm, 1)

            def step(b, u, k):
                if not is_last(b, nb):
                    transpose_sums(*shifted(b, u, k, 1, U))
                mix_sums(b, u, k)
                if not before(b, 1):
                    transpose_h(*shifted(b, u, k, -1, U))
                if not before(b, 2):
                    mix_h(*shifted(b, u, k, -2, U))
            transpose_sums(0, 0, 0)
            loop_blocks(pe, nb, step)
            transpose_h(nb - 1, (nb - 1) % U, (nb - 1) // U)
            for b in (nb - 2, nb - 1):
                mix_h(b, b % U, b // U)

        @block.gpsimd
        def _(pool):
            def step(b, u, k):
                pool.wait_ge(made, b + 1)
                settle(pool, C)
                pool.dma_start(rows(x2, b), xo[u][:, :]).then_inc(stx[u], 16)
                pool.dma_start(rows(sv, b), so[u][:, :]).then_inc(stx[u], 16)
                pool.dma_start(rows(skip, b), ko[u][:, :]).then_inc(stx[u], 16)
            loop_blocks(pool, nb, step)
            for u in range(U):
                pool.wait_ge(stx[u], 48 * times(u, nb))


def after_gnn1(nc, C, agg, last, x2, skip, Wn, nb, out):
    U = LONG_UNROLL
    ctx = ExitStack()
    with ctx:
        a = Names(nc, ctx, "node2")
        def several(n, name, shape):
            return [a.sb(f"{name}{i}", shape) for i in range(n)]
        ag, xs, ks = several(U, "agg", [P, AGG1]), several(U, "x2", [P, D]), several(U, "skip", [P, 192])
        mT, pre, sg = several(2, "mT", [P, 4 * P]), several(2, "pre", [P, 192]), several(2, "sg", [P, 96])
        tm, ot = several(2, "tm", [P, D]), several(U, "out", [P, D])
        mps, ops = [a.ps(f"m{i}") for i in range(2)], [a.ps(f"o{i}") for i in range(2)]
        ld = [a.sem(f"loaded{i}") for i in range(U)]
        stx = [a.sem(f"stored{i}") for i in range(U)]
        mtr, mev, mmm, pre_ready, sig, gated, made = (
            a.sem(s) for s in ("mtr", "mev", "mmm", "pre_ready", "sig", "gated", "made"))
        block = ctx.enter_context(nc.Block())
        agg_rows = agg.rearrange("g p f -> (g p) f")

        def rows(ap, b):
            return ap[bass.ds(b * P, P), :]

        @block.sync
        def _(sp):
            def step(b, u, k):
                if not before(b, U):
                    sp.wait_ge(made, b - (U - 1))
                settle(sp, C)
                g = sp.value_load(last[0:1, bass.ds(b, 1)], min_val=0, max_val=agg.shape[0] - 1)
                sp.dma_start(ag[u][:, :], agg_rows[bass.ds(g * P, P), :]).then_inc(ld[u], 16)
                sp.dma_start(xs[u][:, :], rows(x2, b)).then_inc(ld[u], 16)
                sp.dma_start(ks[u][:, :], rows(skip, b)).then_inc(ld[u], 16)
            loop_blocks(sp, nb, step)

        @block.vector
        def _(dve):
            def add_skip(b, u, k):
                dve.wait_ge(mmm, b + 1)
                if not before(b, 2):
                    dve.wait_ge(gated, b - 1)
                nc.vector.tensor_tensor(pre[u % 2][:, :], ops[u % 2][:, 0:192], ks[u][:, :], ALU.add).then_inc(pre_ready, 1)

            def close(b, u, k):
                v = u % 2
                dve.wait_ge(sig, b + 1)
                if not before(b, 2):
                    dve.wait_ge(made, b - 1)
                nc.vector.tensor_tensor(tm[v][:, 0:MS], pre[v][:, 0:MS], sg[v][:, 0:MS], ALU.mult)
                nc.vector.tensor_tensor(tm[v][:, MS:D].rearrange("p (c f) -> p c f", c=3),
                                        pre[v][:, 96:192].rearrange("p (c f) -> p c f", c=3),
                                        bcast(sg[v][:, MS:96], 1, 3), ALU.mult).then_inc(gated, 1)
                dve.wait_ge(gated, b + 1)
                if not before(b, U):
                    dve.wait_ge(stx[u], k * 16)
                nc.vector.tensor_tensor(ot[u][:, :], tm[v][:, :], xs[u][:, :], ALU.add).then_inc(made, 1)

            def step(b, u, k):
                add_skip(b, u, k)
                if not before(b, 1):
                    close(*shifted(b, u, k, -1, U))
            loop_blocks(dve, nb, step)
            close(nb - 1, (nb - 1) % U, (nb - 1) // U)

        @block.scalar
        def _(act):
            def take_sums(b, u, k):
                v = u % 2
                act.wait_ge(mtr, b + 1)
                if not before(b, 2):
                    act.wait_ge(mmm, b - 1)
                nc.scalar.copy(mT[v][0:96, 0:P], mps[v][0:96, 0:P])
                nc.scalar.copy(mT[v][:, P:4 * P], mps[v][:, P:4 * P]).then_inc(mev, 1)

            def step(b, u, k):
                if not is_last(b, nb):
                    take_sums(*shifted(b, u, k, 1, U))
                act.wait_ge(pre_ready, b + 1)
                if not before(b, 2):
                    act.wait_ge(gated, b - 1)
                nc.scalar.activation(sg[u % 2][:, :], pre[u % 2][:, 0:96], ACT.Sigmoid).then_inc(sig, 1)
            take_sums(0, 0, 0)
            loop_blocks(act, nb, step)

        @block.tensor
        def _(pe):
            def transpose_sums(b, u, k):
                v = u % 2
                pe.wait_ge(ld[u], k * 48 + 48)
                if not before(b, 2):
                    pe.wait_ge(mev, b - 1)
                nc.tensor.transpose(mps[v][0:96, 0:P], ag[u][:, 0:96], C["ident"][:, :])
                for c in range(3):
                    last_ = nc.tensor.transpose(mps[v][:, (c + 1) * P:(c + 2) * P], ag[u][:, 96 + c * 128:96 + (c + 1) * 128],
                                                C["ident"][:, :])
                last_.then_inc(mtr, 1)

            def step(b, u, k):
                v = u % 2
                if not is_last(b, nb):
                    transpose_sums(*shifted(b, u, k, 1, U))
                pe.wait_ge(mev, b + 1)
                if not before(b, 2):
                    pe.wait_ge(pre_ready, b - 1)
                nc.tensor.matmul(ops[v][:, 0:96], mT[v][0:96, 0:P], Wn["outs"][0:96, :], start=True, stop=True)
                for c in range(3):
                    last_ = nc.tensor.matmul(ops[v][:, 96 + c * MV:96 + (c + 1) * MV], mT[v][:, (c + 1) * P:(c + 2) * P],
                                             Wn["outv"][:, :], start=True, stop=True)
                last_.then_inc(mmm, 1)
            transpose_sums(0, 0, 0)
            loop_blocks(pe, nb, step)

        @block.gpsimd
        def _(pool):
            def step(b, u, k):
                pool.wait_ge(made, b + 1)
                settle(pool, C)
                pool.dma_start(rows(out, b), ot[u][:, :]).then_inc(stx[u], 16)
            loop_blocks(pool, nb, step)
            for u in range(U):
                pool.wait_ge(stx[u], 16 * times(u, nb))


def before(index, n):
    return isinstance(index, int) and index < n


def group_pair(ap, first):
    return ap[bass.ds(first, G), :].rearrange("(p j) w -> p j w", p=P)


def edges_gnn0(nc, C, unsorted, attr0, attr0_a, ids_a, x1, table, row0, Wn, ng, agg):
    U = UNROLL
    n = ng // 2
    ctx = ExitStack()
    with ctx:
        a = Names(nc, ctx, "edge0")
        attr = [a.sb(f"attr{i}", [P, TILES, ATTR0]) for i in range(U)]
        ids = [a.sb(f"ids{i}", [P, TILES, 3], I32) for i in range(U)]
        src = [a.sb(f"src{i}", [P, TILES], I32) for i in range(U)]
        gath = [a.sb(f"gath{i}", [P, TILES, D]) for i in range(U)]
        eT, hid = a.sb("eT", [TILES * ATTR0, P]), a.sb("hid", [P, TILES * P])
        es = [a.sb(f"es{i}", [P, TILES, 96]) for i in range(2)]
        hot = [a.sb(f"hot{i}", [P, TILES, P]) for i in range(2)]
        msg = [a.sb(f"msg{i}", [P, TILES, AGG0]) for i in range(2)]
        local = a.sb("local", [P, TILES])
        ws = [a.sb(f"ws{i}", [P, TILES, MS]) for i in range(2)]
        dots = a.sb("dots", [P, TILES, 3, MV])
        dot = a.sb("dot", [P, TILES, MV])
        acc = [a.sb(f"acc{i}", [P, 2, AGG0]) for i in range(U)]
        tps, hps = a.ps("t"), a.ps("h")
        wps = [a.ps(f"w{i}", TILES * W_STRIDE) for i in range(2)]
        aps = [a.ps(f"a{i}") for i in range(2)]
        in_ = [a.sem(f"in{i}") for i in range(U)]
        gath_in = [a.sem(f"gath_in{i}") for i in range(U)]
        acc_out = [a.sem(f"acc_out{i}") for i in range(U)]
        tr, ev, fc1, act1, w_ready, es_ready = (a.sem(s) for s in ("tr", "ev", "fc1", "act1", "w_ready", "es_ready"))
        ws_ready, spread_ready = a.sem("ws_ready"), a.sem("spread_ready")
        src_ready, msg_ready, summed, acc_ready, ch, zeroed = (
            a.sem(s) for s in ("src_ready", "msg_ready", "summed", "acc_ready", "chain", "zeroed"))
        block = ctx.enter_context(nc.Block())

        @block.sync
        def _(sp):
            def store(i, u):
                sp.wait_ge(acc_ready, i * 2 + 2)
                settle(sp, C)
                sp.dma_start(agg[bass.ds(i * 2, 2), :, :].rearrange("g p f -> p g f"), acc[u][:, :, :]).then_inc(acc_out[u], 16)

            def run(attributes):
                def step(i, u, k):
                    if not before(i, 5):
                        store(i - 5, (u - 5) % U)
                    if not before(i, U):
                        sp.wait_ge(msg_ready, i - (U - 1))
                        sp.wait_ge(spread_ready, i - (U - 1))
                        settle(sp, C)
                    for h in range(2):
                        r = sp.value_load(row0[0:1, bass.ds(i * 2 + h, 1)], min_val=0, max_val=attributes.shape[0] - G)
                        sp.dma_start(ids[u][:, 2 * h:2 * h + 2, :], group_pair(ids_a, r)).then_inc(in_[u], 16)
                        sp.dma_start(attr[u][:, 2 * h:2 * h + 2, :], group_pair(attributes, r)).then_inc(in_[u], 16)
                loop_pairs(sp, n, step, peel=2, step=U)
            either(sp, unsorted, lambda: run(attr0_a), lambda: run(attr0))
            for i in range(n - 5, n):
                store(i, i % U)
            for u in range(U):
                sp.wait_ge(acc_out[u], 16 * (n // U))

        @block.gpsimd
        def _(pool):
            def step(i, u, k):
                if not before(i, U):
                    pool.wait_ge(msg_ready, i - (U - 1))
                pool.wait_ge(src_ready, i + 1)
                settle(pool, C)
                for j in range(TILES):
                    pool.indirect_dma_start(
                        out=gath[u][:, j, :], out_offset=None, in_=x1,
                        in_offset=bass.IndirectOffsetOnAxis(ap=src[u][:, j:j + 1], axis=0)).then_inc(gath_in[u], 16)
            loop_pairs(pool, n, step, peel=1, step=U)

        @block.scalar
        def _(act):
            def scale(i, u):
                act.wait_ge(w_ready, i + 1)
                if not before(i, 2):
                    act.wait_ge(msg_ready, i - 1)
                for j in range(TILES):
                    last_ = nc.scalar.activation(es[u % 2][:, j, :], wps[u % 2][:, j * W_STRIDE:j * W_STRIDE + 96], ACT.Copy,
                                                 scale=attr[u][:, j, EA4:EA4 + 1])
                last_.then_inc(es_ready, 1)

            def spread(i, u):
                act.wait_ge(ws_ready, i + 1)
                if not before(i, 2):
                    act.wait_ge(summed, i * 2 - 2)
                for j in range(TILES):
                    for c in range(SPREAD):
                        last_ = nc.scalar.activation(msg[u % 2][:, j, 96 * (c + 1):96 * (c + 1) + MS], ws[u % 2][:, j, :], ACT.Copy,
                                                     scale=attr[u][:, j, EA4 + 1 + c:EA4 + 2 + c])
                last_.then_inc(spread_ready, 1)

            def step(i, u, k):
                act.wait_ge(in_[u], k * 64 + 64)
                if not before(i, U):
                    act.wait_ge(gath_in[u], k * (16 * TILES))
                nc.scalar.copy(src[u][:, :], ids[u][:, :, SRC]).then_inc(src_ready, 1)
                act.wait_ge(tr, i + 1)
                if not before(i, 1):
                    act.wait_ge(fc1, i)
                nc.scalar.copy(eT[:, :], tps[0:TILES * ATTR0, 0:P]).then_inc(ev, 1)
                if not before(i, 1):
                    scale(i - 1, (u - 1) % U)
                act.wait_ge(fc1, i + 1)
                if not before(i, 1):
                    act.wait_ge(w_ready, i)
                nc.scalar.activation(hid[0:H0, :], hps[0:H0, :], ACT.Silu).then_inc(act1, 1)
                if not before(i, 1):
                    spread(i - 1, (u - 1) % U)
            loop_pairs(act, n, step, peel=1, step=U)
            scale(n - 1, (n - 1) % U)
            spread(n - 1, (n - 1) % U)

        @block.vector
        def _(dve):
            nc.vector.memset(acc[U - 1][:, :, :], 0.0).then_inc(zeroed, 1)
            dve.wait_ge(zeroed, 1)

            def add_groups(i, u, k):
                if not before(i, U):
                    dve.wait_ge(acc_out[u], k * 16)
                for h in range(2):
                    dve.wait_ge(summed, i * 2 + h + 1)
                    if not (before(i, 1) and h == 0):
                        dve.wait_ge(acc_ready, i * 2 + h)
                    prev = acc[u][:, 0, :] if h else acc[(u - 1) % U][:, 1, :]
                    nc.vector.scalar_tensor_tensor(acc[u][:, h, :], prev, table[:, 2, bass.ds(i * 2 + h, 1)],
                                                   aps[h][:, 0:AGG0], ALU.mult, ALU.add).then_inc(acc_ready, 1)

            def step(i, u, k):
                v = u % 2
                CH = 4
                dve.wait_ge(in_[u], k * 64 + 64)
                if not before(i, 1):
                    dve.wait_ge(ch, i * CH)
                nc.vector.tensor_tensor(local[:, :].rearrange("p (h j) -> p h j", h=2),
                                        ids[u][:, :, DST].rearrange("p (h j) -> p h j", h=2),
                                        bcast(table[:, 1, bass.ds(i * 2, 2)], 2, 2), ALU.subtract).then_inc(ch, 1)
                dve.wait_ge(ch, i * CH + 1)
                if not before(i, 2):
                    dve.wait_ge(summed, i * 2 - 2)
                nc.vector.tensor_tensor(hot[v][:, :, :], bcast(C["node_ramp"][:, :], 1, TILES), bcast(local[:, :], 2, P),
                                        ALU.is_equal)
                if not before(i, 2):
                    add_groups(i - 2, (u - 2) % U, k if u >= 2 else k - 1)
                dve.wait_ge(gath_in[u], (k + 1) * (16 * TILES))
                gs = gath[u][:, :, 0:MS]
                gv = gath[u][:, :, MS:D].rearrange("p j (c f) -> p j c f", c=3)
                ev_ = attr[u][:, :, EA4 + 1:EA4 + 4]
                w = wps[v][:, :].rearrange("p (j f) -> p j f", j=TILES)
                m = msg[v]
                mv_ = m[:, :, 96:AGG0].rearrange("p j (c f) -> p j c f", c=3)
                nc.vector.tensor_tensor(dots[:, :, :, :], gv, bcast(ev_, 3, MV), ALU.mult).then_inc(ch, 1)
                dve.wait_ge(es_ready, i + 1)
                if not before(i, 2):
                    dve.wait_ge(spread_ready, i - 1)
                nc.vector.tensor_tensor(ws[v][:, :, :], w[:, :, 96:160], gs, ALU.mult).then_inc(ws_ready, 1)
                dve.wait_ge(ch, i * CH + 2)
                nc.vector.tensor_tensor(dot[:, :, :], dots[:, :, 0, :], dots[:, :, 1, :], ALU.add).then_inc(ch, 1)
                nc.vector.tensor_tensor(m[:, :, 0:MS], es[v][:, :, 0:MS], gs, ALU.mult)
                dve.wait_ge(ch, i * CH + 3)
                nc.vector.tensor_tensor(dot[:, :, :], dot[:, :, :], dots[:, :, 2, :], ALU.add).then_inc(ch, 1)
                dve.wait_ge(ws_ready, i + 1)
                nc.vector.tensor_tensor(mv_[:, :, SPREAD:3, 0:MS], bcast(ws[v][:, :, :], 2, 3 - SPREAD),
                                        bcast(ev_[:, :, SPREAD:3], 3, MS), ALU.mult)
                dve.wait_ge(ch, i * CH + 4)
                nc.vector.tensor_tensor(m[:, :, MS:96], w[:, :, 160:192], dot[:, :, :], ALU.mult)
                nc.vector.tensor_tensor(mv_[:, :, :, MS:96], bcast(es[v][:, :, MS:96], 2, 3), gv, ALU.mult).then_inc(msg_ready, 1)
            loop_pairs(dve, n, step, peel=1, step=U)
            for i in (n - 2, n - 1):
                add_groups(i, i % U, n // U - 1)

        @block.tensor
        def _(pe):
            def group_sum(i, v, h):
                if h == 0:
                    pe.wait_ge(msg_ready, i + 1)
                    pe.wait_ge(spread_ready, i + 1)
                if not before(i, 1):
                    pe.wait_ge(acc_ready, i * 2 + (h - 1))
                for j in range(2):
                    last_ = nc.tensor.matmul(aps[h][:, 0:AGG0], hot[v][:, 2 * h + j, :], msg[v][:, 2 * h + j, :],
                                             start=j == 0, stop=j == 1)
                last_.then_inc(summed, 1)

            def step(i, u, k):
                v = u % 2
                pe.wait_ge(in_[u], k * 64 + 64)
                if not before(i, 1):
                    pe.wait_ge(ev, i)
                pe.sem_inc(C["settled"], 1)
                nc.tensor.transpose(tps[0:TILES * ATTR0, 0:P], attr[u][:, :, :].rearrange("p j w -> p (j w)"),
                                    C["ident"][:, :]).then_inc(tr, 1)
                if not before(i, 2):
                    group_sum(i - 2, v, 0)
                pe.wait_ge(ev, i + 1)
                if not before(i, 1):
                    pe.wait_ge(act1, i)
                settle(pe, C)
                for j in range(TILES):
                    last_ = nc.tensor.matmul(hps[0:H0, j * P:(j + 1) * P], Wn["fc1_0"][0:TILES * ATTR0, j * H0:(j + 1) * H0],
                                             eT[:, :], start=True, stop=True)
                last_.then_inc(fc1, 1)
                if not before(i, 2):
                    group_sum(i - 2, v, 1)
                pe.wait_ge(act1, i + 1)
                for j in range(TILES):
                    last_ = nc.tensor.matmul(wps[v][:, j * W_STRIDE:j * W_STRIDE + WN0], hid[0:H0, j * P:(j + 1) * P],
                                             Wn["fc2_0"][0:H0, :], start=True, stop=True)
                last_.then_inc(w_ready, 1)
            loop_pairs(pe, n, step, peel=1, step=U)
            for i in (n - 2, n - 1):
                for h in range(2):
                    group_sum(i, i % 2, h)


def to_source_order(nc, C, unsorted, attr1, attr1_a, ids_a, sv, table, row0, node0, ng, n_edges, rows_b):
    U = LONG_UNROLL
    n = ng // 2
    ctx = ExitStack()
    with ctx:
        a = Names(nc, ctx, "route")
        row = [a.sb(f"row{i}", [P, TILES, ROW_B]) for i in range(U)]
        ids = [a.sb(f"ids{i}", [P, TILES, 3], I32) for i in range(U)]
        node = [a.sb(f"node{i}", [P, 2, D]) for i in range(U)]
        at = [a.sb(f"at{i}", [P, TILES], I32) for i in range(U)]
        hot = [a.sb(f"hot{i}", [P, TILES, P]) for i in range(2)]
        hotT = [a.sb(f"hotT{i}", [P, TILES * P]) for i in range(2)]
        local, low, high = a.sb("local", [P, TILES]), a.sb("low", [P, TILES]), a.sb("high", [P, TILES])
        pad = a.sb("pad", [G // 8, 8 * ROW_B])
        tps = [a.ps(f"t{i}") for i in range(2)]
        nps = [a.ps(f"n{i}", TILES * W_STRIDE) for i in range(2)]
        in_ = [a.sem(f"in{i}") for i in range(U)]
        out_done = [a.sem(f"out_done{i}") for i in range(U)]
        hot_ready, tr, ev, picked, filled, at_ready, ch, padded, pad_out = (
            a.sem(s) for s in ("hot_ready", "tr", "ev", "picked", "filled", "at_ready", "chain", "padded", "pad_out"))
        block = ctx.enter_context(nc.Block())

        def load(eng, attributes, h, i, u, k):
            if not before(i, U):
                eng.wait_ge(out_done[u], k * (16 * TILES))
                settle(eng, C)
            r = eng.value_load(row0[0:1, bass.ds(i * 2 + h, 1)], min_val=0, max_val=attributes.shape[0] - G)
            eng.dma_start(ids[u][:, 2 * h:2 * h + 2, :], group_pair(ids_a, r)).then_inc(in_[u], 16)
            eng.dma_start(row[u][:, 2 * h:2 * h + 2, 0:ATTR1], group_pair(attributes, r)).then_inc(in_[u], 16)
            b = eng.value_load(node0[0:1, bass.ds(i * 2 + h, 1)], min_val=0, max_val=sv.shape[0] - P)
            eng.dma_start(node[u][:, h, :], sv[bass.ds(b, P), :]).then_inc(in_[u], 16)

        @block.sync
        def _(sp):
            sp.wait_ge(padded, 2)
            sp.dma_start(rows_b[n_edges:n_edges + G, :].rearrange("(p j) w -> p (j w)", j=8), pad[:, :]).then_inc(pad_out, 16)

            def run(attributes):
                loop_pairs(sp, n, lambda i, u, k: load(sp, attributes, 0, i, u, k), peel=1, step=U)
            either(sp, unsorted, lambda: run(attr1_a), lambda: run(attr1))
            sp.wait_ge(pad_out, 16)

        @block.vector
        def _(dve):
            nc.vector.memset(pad[:, :], 1.0).then_inc(padded, 1)
            dve.wait_ge(padded, 1)
            nc.vector.memset(pad[:, :].rearrange("p (j w) -> p j w", j=8)[:, :, B_SRC].bitcast(I32), C["blocks"] * P + P)\
                .then_inc(padded, 1)

            def fill(i, u):
                dve.wait_ge(picked, i + 1)
                nc.vector.tensor_copy(row[u][:, :, B_NODE:ROW_B],
                                      nps[u % 2][:, :].rearrange("p (j f) -> p j f", j=TILES)[:, :, 0:D]).then_inc(filled, 1)

            def step(i, u, k):
                dve.wait_ge(in_[u], k * 96 + 96)
                if not before(i, 1):
                    dve.wait_ge(ch, i * 4)
                    dve.wait_ge(at_ready, i)
                nc.vector.tensor_tensor(local[:, :].rearrange("p (h j) -> p h j", h=2),
                                        ids[u][:, :, DST].rearrange("p (h j) -> p h j", h=2),
                                        bcast(table[:, 1, bass.ds(i * 2, 2)], 2, 2), ALU.subtract).then_inc(ch, 1)
                dve.wait_ge(ch, i * 4 + 1)
                if not before(i, 2):
                    dve.wait_ge(tr, i - 1)
                nc.vector.tensor_tensor(hot[u % 2][:, :, :], bcast(C["node_ramp"][:, :], 1, TILES), bcast(local[:, :], 2, P),
                                        ALU.is_equal).then_inc(hot_ready, 1)
                nc.vector.tensor_scalar(low[:, :], local[:, :], 0.0, float(OUT_OF_BOUNDS), ALU.is_lt, ALU.mult).then_inc(ch, 1)
                nc.vector.tensor_scalar(high[:, :], local[:, :], float(P), float(OUT_OF_BOUNDS), ALU.is_ge, ALU.mult).then_inc(ch, 1)
                dve.wait_ge(ch, i * 4 + 3)
                nc.vector.tensor_tensor(high[:, :], high[:, :], low[:, :], ALU.add).then_inc(ch, 1)
                if not before(i, 1):
                    fill(i - 1, (u - 1) % U)
                dve.wait_ge(ch, i * 4 + 4)
                if not before(i, U):
                    dve.wait_ge(out_done[u], k * (16 * TILES))
                nc.vector.tensor_tensor(at[u][:, :], high[:, :], ids[u][:, :, PLACE], ALU.add).then_inc(at_ready, 1)
            loop_pairs(dve, n, step, peel=1, step=U)
            fill(n - 1, (n - 1) % U)

        @block.scalar
        def _(act):
            def run(attributes):
                def step(i, u, k):
                    if not (isinstance(i, int) and i >= n - 3):
                        load(act, attributes, 1, *shifted(i, u, k, 3, U))
                    act.wait_ge(in_[u], k * 96 + 96)
                    nc.scalar.copy(row[u][:, :, B_SRC].bitcast(I32), ids[u][:, :, SRC])
                    act.wait_ge(tr, i + 1)
                    if not before(i, 2):
                        act.wait_ge(picked, i - 1)
                    nc.scalar.copy(hotT[u % 2][:, :], tps[u % 2][:, :]).then_inc(ev, 1)
                for i in range(3):
                    load(act, attributes, 1, i, i, 0)
                loop_pairs(act, n - U, step, peel=1, step=U)
                for u in range(U):
                    step(n - U + u, u, n // U - 1)
            either(act, unsorted, lambda: run(attr1_a), lambda: run(attr1))

        @block.tensor
        def _(pe):
            def step(i, u, k):
                pe.wait_ge(hot_ready, i + 1)
                if not before(i, 2):
                    pe.wait_ge(ev, i - 1)
                for j in range(TILES):
                    last_ = nc.tensor.transpose(tps[u % 2][:, j * P:(j + 1) * P], hot[u % 2][:, j, :], C["ident"][:, :])
                last_.then_inc(tr, 1)
                pe.wait_ge(ev, i + 1)
                if not before(i, 2):
                    pe.wait_ge(filled, i - 1)
                pe.wait_ge(in_[u], k * 96 + 96)
                for j in range(TILES):
                    last_ = nc.tensor.matmul(nps[u % 2][:, j * W_STRIDE:j * W_STRIDE + D], hotT[u % 2][:, j * P:(j + 1) * P],
                                             node[u][:, j // 2, :], start=True, stop=True)
                last_.then_inc(picked, 1)
            loop_pairs(pe, n, step, peel=1, step=U)

        @block.gpsimd
        def _(pool):
            bound = rows_b.shape[0] - 1

            def step(i, u, k):
                pool.wait_ge(filled, i + 1)
                pool.wait_ge(at_ready, i + 1)
                settle(pool, C)
                for j in range(TILES):
                    pool.indirect_dma_start(
                        out=rows_b, out_offset=bass.IndirectOffsetOnAxis(ap=at[u][:, j:j + 1], axis=0),
                        in_=row[u][:, j, :], in_offset=None, bounds_check=bound, oob_is_err=False).then_inc(out_done[u], 16)
            loop_pairs(pool, n, step, peel=1, step=U)
            for u in range(U):
                pool.wait_ge(out_done[u], 16 * TILES * (n // U))


def edges_gnn1(nc, C, rows_b, table, row0, Wn, ng, agg):
    U = UNROLL
    n = ng // 2
    ctx = ExitStack()
    with ctx:
        a = Names(nc, ctx, "edge1")
        row = [a.sb(f"row{i}", [P, TILES, ROW_B]) for i in range(U)]
        feat = [a.sb(f"feat{i}", [P, TILES * 64]) for i in range(2)]
        fT, hid = a.sb("fT", [P, 2 * P]), a.sb("hid", [P, 2 * P])
        hot = [a.sb(f"hot{i}", [P, TILES, P]) for i in range(2)]
        msg = [a.sb(f"msg{i}", [P, TILES, AGG1]) for i in range(2)]
        n2, n1, rn = (a.sb(s, [P, TILES]) for s in ("n2", "n1", "rn"))
        local = [a.sb(f"local{i}", [P, TILES]) for i in range(2)]
        squares = a.sb("squares", [P, TILES, 3])
        sh = [a.sb(f"sh{i}", [P, TILES, 5]) for i in range(2)]
        ws = [a.sb(f"ws{i}", [P, TILES, MS]) for i in range(2)]
        dots, part = a.sb("dots", [P, TILES, 3, MV]), a.sb("part", [P, TILES, MV])
        dot = [a.sb(f"dot{i}", [P, TILES, MV]) for i in range(2)]
        wv = [a.sb(f"wv{i}", [P, TILES, 5, MV]) for i in range(2)]
        left, right = a.sb("left", [P, TILES, 3, MV]), a.sb("right", [P, TILES, 3, MV])
        acc = [a.sb(f"acc{i}", [P, 2, AGG1]) for i in range(U)]
        tps, hps = a.ps("t"), a.ps("h")
        wps = [a.ps(f"w{i}", TILES * W_STRIDE) for i in range(2)]
        aps = [a.ps(f"a{i}") for i in range(2)]
        in_ = [a.sem(f"in{i}") for i in range(U)]
        acc_out = [a.sem(f"acc_out{i}") for i in range(U)]
        feat_ready, tr, ev, fc1, act1, w_ready = (a.sem(s) for s in ("feat_ready", "tr", "ev", "fc1", "act1", "w_ready"))
        local_ready, squared, n2_ready, root, inverse, scaled, sh_ready = (
            a.sem(s) for s in ("local_ready", "squared", "n2_ready", "root", "inverse", "scaled", "sh_ready"))
        dots_ready, part_ready, dot_ready, wv_ready, both_ready, crossed = (
            a.sem(s) for s in ("dots_ready", "part_ready", "dot_ready", "wv_ready", "both_ready", "crossed"))
        ws_ready, spread_ready, msg_ready, summed, acc_ready, zeroed = (
            a.sem(s) for s in ("ws_ready", "spread_ready", "msg_ready", "summed", "acc_ready", "zeroed"))
        block = ctx.enter_context(nc.Block())

        def vectors(u):
            return row[u][:, :, B_NODE + MS:ROW_B].rearrange("p j (c f) -> p j c f", c=3)

        @block.sync
        def _(sp):
            def store(i, u):
                sp.wait_ge(acc_ready, i * 2 + 2)
                settle(sp, C)
                sp.dma_start(agg[bass.ds(i * 2, 2), :, :].rearrange("g p f -> p g f"), acc[u][:, :, :]).then_inc(acc_out[u], 16)

            def step(i, u, k):
                if not before(i, 5):
                    store(i - 5, (u - 5) % U)
                if not before(i, U):
                    sp.wait_ge(msg_ready, i - (U - 1))
                    settle(sp, C)
                for h in range(2):
                    r = sp.value_load(row0[0:1, bass.ds(i * 2 + h, 1)], min_val=0, max_val=rows_b.shape[0] - G)
                    sp.dma_start(row[u][:, 2 * h:2 * h + 2, :], group_pair(rows_b, r)).then_inc(in_[u], 16)
            loop_pairs(sp, n, step, peel=2, step=U)
            for i in range(n - 5, n):
                store(i, i % U)
            for u in range(U):
                sp.wait_ge(acc_out[u], 16 * (n // U))

        def vector_message(v):
            return msg[v][:, :, 96:AGG1].rearrange("p j (c f) -> p j c f", c=3)

        @block.scalar
        def _(act):
            def features(i, u, k):
                act.wait_ge(in_[u], k * 32 + 32)
                if not before(i, 2):
                    act.wait_ge(tr, i - 1)
                nc.scalar.copy(feat[u % 2][:, :].rearrange("p (j f) -> p j f", j=TILES), row[u][:, :, EA64:EA64 + 64])\
                    .then_inc(feat_ready, 1)

            def length(i, u, k):
                act.wait_ge(n2_ready, i + 1)
                nc.scalar.activation(n1[:, :], n2[:, :], ACT.Sqrt, scale=1 / 3.0).then_inc(root, 1)

            def spread(i, u, k):
                act.wait_ge(ws_ready, i + 1)
                act.wait_ge(sh_ready, i + 1)
                if not before(i, 2):
                    act.wait_ge(summed, i * 2 - 2)
                for j in range(TILES):
                    for c in range(SPREAD):
                        last_ = nc.scalar.activation(vector_message(u % 2)[:, j, c, 0:MS], ws[u % 2][:, j, :], ACT.Copy,
                                                     scale=sh[u % 2][:, j, c:c + 1])
                last_.then_inc(spread_ready, 1)

            def step(i, u, k):
                act.wait_ge(tr, i + 1)
                if not before(i, 1):
                    act.wait_ge(fc1, i)
                nc.scalar.copy(fT[:, :], tps[:, 0:2 * P]).then_inc(ev, 1)
                if not before(i, 1):
                    spread(*shifted(i, u, k, -1))
                act.wait_ge(fc1, i + 1)
                if not before(i, 1):
                    act.wait_ge(w_ready, i)
                nc.scalar.activation(hid[:, :], hps[:, 0:2 * P], ACT.Relu).then_inc(act1, 1)
                if not (isinstance(i, int) and i == n - 1):
                    features(*shifted(i, u, k, 1))
                    length(*shifted(i, u, k, 1))
            features(0, 0, 0)
            length(0, 0, 0)
            loop_pairs(act, n - U, step, peel=1, step=U)
            for u in range(U):
                step(n - U + u, u, n // U - 1)
            spread(n - 1, U - 1, n // U - 1)

        @block.gpsimd
        def _(pool):
            def step(i, u, k):
                v = u % 2
                pool.wait_ge(sh_ready, i + 1)
                if not before(i, 1):
                    pool.wait_ge(dot_ready, i)
                settle(pool, C)
                nc.gpsimd.tensor_tensor(dots[:, :, :, :], vectors(u), bcast(sh[v][:, :, 0:3], 3, MV), ALU.mult).then_inc(dots_ready, 1)
                pool.wait_ge(dots_ready, i + 1)
                settle(pool, C)
                nc.gpsimd.tensor_tensor(part[:, :, :], dots[:, :, 0, :], dots[:, :, 1, :], ALU.add).then_inc(part_ready, 1)
                if not before(i, 2):
                    pool.wait_ge(msg_ready, i - 1)
                pool.wait_ge(part_ready, i + 1)
                settle(pool, C)
                nc.gpsimd.tensor_tensor(dot[v][:, :, :], part[:, :, :], dots[:, :, 2, :], ALU.add).then_inc(dot_ready, 1)
                pool.wait_ge(wv_ready, i + 1)
                if not before(i, 1):
                    pool.wait_ge(crossed, i)
                settle(pool, C)
                nc.gpsimd.tensor_tensor(left[:, :, :, :], wv[v][:, :, 1:4, :], bcast(sh[v][:, :, 2:5], 3, MV), ALU.mult)
                nc.gpsimd.tensor_tensor(right[:, :, :, :], wv[v][:, :, 2:5, :], bcast(sh[v][:, :, 1:4], 3, MV), ALU.mult)\
                    .then_inc(both_ready, 1)
                if not before(i, 2):
                    pool.wait_ge(summed, i * 2 - 2)
                pool.wait_ge(both_ready, i + 1)
                nc.gpsimd.tensor_tensor(vector_message(v)[:, :, :, 96:128], left[:, :, :, :], right[:, :, :, :], ALU.subtract)\
                    .then_inc(crossed, 1)
            loop_pairs(pool, n, step, peel=1, step=U)

        @block.vector
        def _(dve):
            nc.vector.memset(acc[U - 1][:, :, :], 0.0).then_inc(zeroed, 1)
            dve.wait_ge(zeroed, 1)

            def add_groups(i, u, k):
                if not before(i, U):
                    dve.wait_ge(acc_out[u], k * 16)
                for h in range(2):
                    dve.wait_ge(summed, i * 2 + h + 1)
                    if not (before(i, 1) and h == 0):
                        dve.wait_ge(acc_ready, i * 2 + h)
                    prev = acc[u][:, 0, :] if h else acc[(u - 1) % U][:, 1, :]
                    nc.vector.scalar_tensor_tensor(acc[u][:, h, :], prev, table[:, 2, bass.ds(i * 2 + h, 1)],
                                                   aps[h][:, 0:AGG1], ALU.mult, ALU.add).then_inc(acc_ready, 1)

            def lengths(i, u, k):
                r = row[u]
                dve.wait_ge(in_[u], k * 32 + 32)
                nc.vector.tensor_tensor(local[u % 2][:, :].rearrange("p (h j) -> p h j", h=2),
                                        r[:, :, B_SRC].bitcast(I32).rearrange("p (h j) -> p h j", h=2),
                                        bcast(table[:, 1, bass.ds(i * 2, 2)], 2, 2), ALU.subtract).then_inc(local_ready, 1)
                if not before(i, 1):
                    dve.wait_ge(n2_ready, i)
                    dve.wait_ge(root, i)
                nc.vector.tensor_tensor(squares[:, :, :], r[:, :, EA3:EA3 + 3], r[:, :, EA3:EA3 + 3], ALU.mult).then_inc(squared, 1)
                dve.wait_ge(squared, i + 1)
                nc.vector.tensor_reduce(n2[:, :], squares[:, :, :], AXX, ALU.add).then_inc(n2_ready, 1)

            def inverse_length(i, u, k):
                dve.wait_ge(root, i + 1)
                if not before(i, 1):
                    dve.wait_ge(scaled, i)
                nc.vector.reciprocal(rn[:, :], n1[:, :]).then_inc(inverse, 1)

            def direction(i, u, k):
                if not before(i, 2):
                    dve.wait_ge(crossed, i - 1)
                    dve.wait_ge(spread_ready, i - 1)
                dve.wait_ge(inverse, i + 1)
                nc.vector.tensor_tensor(sh[u % 2][:, :, 0:3], row[u][:, :, EA3:EA3 + 3], bcast(rn[:, :], 2, 3), ALU.mult)\
                    .then_inc(scaled, 1)

            def wrap(i, u, k):
                dve.wait_ge(scaled, i + 1)
                nc.vector.tensor_copy(sh[u % 2][:, :, 3:5], sh[u % 2][:, :, 0:2]).then_inc(sh_ready, 1)

            def step(i, u, k):
                v = u % 2
                xs = row[u][:, :, B_NODE:B_NODE + MS]
                xv = vectors(u)
                m, mv_ = msg[v], vector_message(v)
                more = not (isinstance(i, int) and i == n - 1)

                def w(lo, width):
                    return wps[v][:, :].rearrange("p (j f) -> p j f", j=TILES)[:, :, lo:lo + width]
                if more:
                    lengths(*shifted(i, u, k, 1))
                if not before(i, 2):
                    add_groups(*shifted(i, u, k, -2))
                dve.wait_ge(local_ready, i + 1)
                nc.vector.tensor_tensor(hot[v][:, :, :], bcast(C["node_ramp"][:, :], 1, TILES), bcast(local[v][:, :], 2, P),
                                        ALU.is_equal)
                dve.wait_ge(w_ready, i + 1)
                if not before(i, 2):
                    dve.wait_ge(crossed, i - 1)
                nc.vector.tensor_tensor(wv[v][:, :, 0:3, :], bcast(w(192, MV), 2, 3), xv, ALU.mult)
                nc.vector.tensor_tensor(wv[v][:, :, 3:5, :], bcast(w(192, MV), 2, 2), xv[:, :, 0:2, :], ALU.mult).then_inc(wv_ready, 1)
                if not before(i, 2):
                    dve.wait_ge(spread_ready, i - 1)
                nc.vector.tensor_tensor(ws[v][:, :, :], w(MS, MS), xs, ALU.mult).then_inc(ws_ready, 1)
                if more:
                    inverse_length(*shifted(i, u, k, 1))
                nc.vector.tensor_tensor(m[:, :, 0:MS], w(0, MS), xs, ALU.mult)
                if more:
                    direction(*shifted(i, u, k, 1))
                dve.wait_ge(ws_ready, i + 1)
                nc.vector.tensor_tensor(mv_[:, :, SPREAD:3, 0:MS], bcast(ws[v][:, :, :], 2, 3 - SPREAD),
                                        bcast(sh[v][:, :, SPREAD:3], 3, MS), ALU.mult)
                if more:
                    wrap(*shifted(i, u, k, 1))
                nc.vector.tensor_tensor(mv_[:, :, :, MS:96], bcast(w(128, MV), 2, 3), xv, ALU.mult)
                dve.wait_ge(dot_ready, i + 1)
                nc.vector.tensor_tensor(m[:, :, MS:96], w(160, MV), dot[v][:, :, :], ALU.mult).then_inc(msg_ready, 1)
            for ahead in (lengths, inverse_length, direction, wrap):
                ahead(0, 0, 0)
            loop_pairs(dve, n - U, step, peel=1, step=U)
            for u in range(U):
                step(n - U + u, u, n // U - 1)
            for i in (n - 2, n - 1):
                add_groups(i, i % U, n // U - 1)

        @block.tensor
        def _(pe):
            def group_sum(i, v, h):
                if h == 0:
                    pe.wait_ge(msg_ready, i + 1)
                    pe.wait_ge(crossed, i + 1)
                    pe.wait_ge(spread_ready, i + 1)
                if not before(i, 1):
                    pe.wait_ge(acc_ready, i * 2 + (h - 1))
                for j in range(2):
                    last_ = nc.tensor.matmul(aps[h][:, 0:AGG1], hot[v][:, 2 * h + j, :], msg[v][:, 2 * h + j, :],
                                             start=j == 0, stop=j == 1)
                last_.then_inc(summed, 1)

            def step(i, u, k):
                v = u % 2
                pe.wait_ge(feat_ready, i + 1)
                if not before(i, 1):
                    pe.wait_ge(ev, i)
                settle(pe, C)
                for j in range(2):
                    last_ = nc.tensor.transpose(tps[:, j * P:(j + 1) * P], feat[v][:, j * P:(j + 1) * P],
                                                C["ident"][:, :])
                last_.then_inc(tr, 1)
                if not before(i, 2):
                    group_sum(i - 2, v, 0)
                pe.wait_ge(ev, i + 1)
                if not before(i, 1):
                    pe.wait_ge(act1, i)
                nc.tensor.matmul(hps[:, 0:2 * P], Wn["fc1_1"][:, :], fT[:, :], start=True, stop=True).then_inc(fc1, 1)
                if not before(i, 2):
                    group_sum(i - 2, v, 1)
                pe.wait_ge(act1, i + 1)
                for j in range(TILES):
                    last_ = nc.tensor.matmul(wps[v][:, j * W_STRIDE:j * W_STRIDE + WN1], hid[:, (j // 2) * P:(j // 2 + 1) * P],
                                             Wn["fc2_1"][:, (j % 2) * WN1:(j % 2 + 1) * WN1], start=True, stop=True)
                last_.then_inc(w_ready, 1)
            loop_pairs(pe, n, step, peel=1, step=U)
            for i in (n - 2, n - 1):
                for h in range(2):
                    group_sum(i, i % 2, h)


def table_ints(nc, stage, table, row0, node0):
    ctx = ExitStack()
    with ctx:
        done = Names(nc, ctx, stage).sem("ints")
        block = ctx.enter_context(nc.Block())

        @block.vector
        def _(dve):
            top = float(node0_limit[0])
            nc.vector.tensor_copy(row0[:, :], table[0:1, 0, :]).then_inc(done, 1)
            nc.vector.tensor_scalar(node0[:, :], table[0:1, 1, :], top, None, ALU.min).then_inc(done, 1)
            dve.wait_ge(done, 2)


node0_limit = [0]


def program(nc, n_nodes, n_edges, A, Wd, out):
    nb, cols = blocks_of(n_nodes), columns_of(n_edges)
    ng = groups_of(n_edges, nb)
    e_pad = P * cols
    node0_limit[0] = (nb - 1) * P

    def dram(name, shape, dt=F32):
        return nc.dram_tensor(name, shape, dt, kind="Internal").ap()
    pos_a, pos_b = dram("place_by_destination", [e_pad], I32), dram("place_by_source", [e_pad], I32)
    attr0_a, attr1_a = dram("attr0_by_destination", [e_pad, ATTR0]), dram("attr1_by_destination", [e_pad, ATTR1])
    ids_a, rows_b = dram("ids_by_destination", [e_pad, 3], I32), dram("rows_by_source", [e_pad, ROW_B])
    x1 = dram("x1", [(nb + 1) * P, D])
    base, x2, sv = (dram(s, [nb * P, D]) for s in ("base", "x2", "sv"))
    skip = dram("skip", [nb * P, 192])
    agg0, agg1 = dram("agg0", [ng, P, AGG0]), dram("agg1", [ng, P, AGG1])
    meta = dram("meta", [2, 3, P * (-(-ng // P))])
    ctx = ExitStack()
    with ctx:
        a = Names(nc, ctx, "all")
        C = {"blocks": nb, "ident": a.sb("ident", [P, P]), "before": a.sb("before", [P, P], BF16),
             "not_before": a.sb("not_before", [P, P], BF16), "ones": a.sb("ones", [P, P], BF16), "ones_f32": a.sb("ones_f32", [P, P]),
             "block_ramp": a.sb("block_ramp", [P, nb], BF16), "node_ramp": a.sb("node_ramp", [P, P])}
        Wn = {k: a.sb(k, [P, n]) for k, n in (("s0", 4 * MS), ("v0", 4 * 96), ("fc1_0", TILES * H0), ("fc2_0", WN0), ("ps", 2 * MS),
                                             ("pv", 2 * MV), ("s1", MS + 96), ("v1", 192), ("fc1_1", P), ("fc2_1", 2 * WN1),
                                             ("outs", 96), ("outv", MV))}
        counts = [a.sb(f"count{i}", [P, nb]) for i in range(2)]
        totals = [a.sb(f"total{i}", [P, 2 * RANKED * nb]) for i in range(2)]
        unsorted = a.sb("unsorted", [1, 1], I32)
        tables = [a.sb(f"table{i}", [P, 3, ng]) for i in range(2)]
        row0 = [a.sb(f"row0_{i}", [1, ng], I32) for i in range(2)]
        node0 = [a.sb(f"node0_{i}", [1, ng], I32) for i in range(2)]
        last = [a.sb(f"last{i}", [1, nb], I32) for i in range(2)]
        C["settled"] = a.sem("settled")
        constants(nc, C)
        prepare_weights(nc, C, Wd, Wn)
        count_both(nc, C, A["src"], A["dst"], cols, nb, totals, counts, unsorted)
        for i, name in ((1, "src"), (0, "dst")):
            group_table(nc, C, f"groups_{name}", counts[1 - i], nb, n_edges, ng, meta[i], tables[i], last[i])
            table_ints(nc, name, tables[i], row0[i], node0[i])
        rank(nc, C, "rank_src", A["src"], cols, nb, pos_b, totals[0], counts[0])
        taken = nc.values_load(unsorted[0:1, 0:1], min_val=0, max_val=1)
        with nc.If(taken != 0):
            rank(nc, C, "rank_dst", A["dst"], cols, nb, pos_a, totals[1], counts[1])
            to_destination_order(nc, C, A, pos_a, pos_b, attr0_a, attr1_a, ids_a, cols)
        with nc.Else():
            ids_in_order(nc, C, A, pos_b, ids_a, cols)
        before_gnn0(nc, C, A["x"], A["attr"], Wn, nb, x1, base)
        edges_gnn0(nc, C, unsorted, A["attr0"], attr0_a, ids_a, x1, tables[0], row0[0], Wn, ng, agg0)
        between(nc, C, agg0, last[0], base, A["attr"], Wn, nb, x2, sv, skip)
        to_source_order(nc, C, unsorted, A["attr1"], attr1_a, ids_a, sv, tables[0], row0[0], node0[0], ng, n_edges, rows_b)
        edges_gnn1(nc, C, rows_b, tables[1], row0[1], Wn, ng, agg1)
        after_gnn1(nc, C, agg1, last[1], x2, skip, Wn, nb, out)


WEIGHTS = ["L0_gnn_" + s for s in ("Ws_sc_a", "Wv_sc_a", "Ws_sc_c", "Wv_sc_c", "Ws_l1_a", "Wv_l1_a", "Ws_l1_c", "Wv_l1_c",
                                   "W_fc1", "W_fc2", "Ws_l2_a", "Wv_l2_a", "Ws_l2_c", "Wv_l2_c", "Ws_l3", "Wv_l3")] \
    + ["L1_gnn_" + s for s in ("W_skip0", "W_skip1", "W_nl0", "W_nl1", "W_fc1", "W_fc2", "W_out_s", "W_out_v")]


def kernel(**inputs):
    import numpy as np
    import concourse.bacc as bacc
    from concourse.bass_utils import run_bass_kernel_spmd

    n, e = inputs["x"].shape[0], inputs["src"].shape[0]
    nb, e_pad = blocks_of(n), P * columns_of(e)

    def padded(a, rows, value):
        return np.concatenate([a, np.full((rows - a.shape[0],) + a.shape[1:], value, a.dtype)])

    x = np.asarray(inputs["x"])
    x = np.concatenate([x[:, :MS], x[:, MS:].reshape(n, MV, 3).transpose(0, 2, 1).reshape(n, 3 * MV)], axis=1)
    attr0 = np.concatenate([np.asarray(inputs[s]) for s in ("edge_attr_10", "edge_attr_4")], axis=1)
    attr1 = np.concatenate([np.asarray(inputs[s]) for s in ("edge_attr_3", "edge_attr_64")], axis=1)
    attr = np.concatenate([np.asarray(inputs[s]) for s in ("node_vec1", "node_vec1_n2", "node_vec1_n3")], axis=1)
    arrays = {"x": padded(x, nb * P, 0), "attr": padded(attr, nb * P, 0), "attr0": padded(attr0, e_pad, 1), "attr1": padded(attr1, e_pad, 1),
              "src": padded(np.asarray(inputs["src"]), e_pad, nb * P),
              "dst": padded(np.asarray(inputs["dst"]), e_pad, (nb + 1) * P)}
    for s in WEIGHTS:
        arrays[s] = np.asarray(inputs[s])
    nc = bacc.Bacc("TRN2", target_bir_lowering=False, num_devices=1)
    aps = {s: nc.dram_tensor("in_" + s, v.shape, mybir.dt.from_np(v.dtype), kind="ExternalInput").ap() for s, v in arrays.items()}
    out = nc.dram_tensor("out", (nb * P, D), F32, kind="ExternalOutput").ap()
    program(nc, n, e, aps, aps, out)
    r = run_bass_kernel_spmd(nc, [{"in_" + s: np.ascontiguousarray(v) for s, v in arrays.items()}], core_ids=[0])
    y = r.results[0]["out"][:n]
    return np.concatenate([y[:, :MS], y[:, MS:].reshape(n, 3, MV).transpose(0, 2, 1).reshape(n, 3 * MV)], axis=1)
```

```python
import concourse.bass as bass
from concourse import mybir
from contextlib import ExitStack

F32 = mybir.dt.float32
I32 = mybir.dt.int32
BF16 = mybir.dt.bfloat16
ALU = mybir.AluOpType
ACT = mybir.ActivationFunctionType
AXX = mybir.AxisListType.X

P = 128
MS, MV = 64, 32
D = MS + 3 * MV
G = 2 * P
TILES = 4
RANKED = 5
UNROLL = 4
LONG_UNROLL = 8
SPREAD0, SPREAD1 = 1, 2
LN_EPS = 1e-5
OUT_OF_BOUNDS = 1 << 20
EA4, ATTR0 = 10, 14
EA3, EA64, ATTR1 = 0, 3, 67
SRC, DST, PLACE = 0, 1, 2
B_SH, B_HID, B_SRC, B_NODE, ROW_B = 0, 5, 5 + 64, 5 + 64 + 1, 5 + 64 + 1 + D
W_STRIDE = 256
MIXED = 96 + D + 96
H0, WN0, MID0 = 100, 192, 96
AGG0 = MID0 * 4
WN1 = 224
AGG1 = 96 + 3 * 128
C_S = 0.3826834323650898
C_X = 0.9238795325112867


def blocks_of(n_nodes):
    return 2 * (-(-n_nodes // (2 * P)))


def columns_of(n_edges):
    return 2 * RANKED * (-(-(n_edges + G) // (P * 2 * RANKED)))


def groups_of(n_edges, n_blocks):
    return 2 * LONG_UNROLL * (-(-(n_edges // G + n_blocks) // (2 * LONG_UNROLL)))


def shifted(i, u, k, by, step=UNROLL):
    return i + by, (u + by) % step, k + (u + by) // step


class Names:

    def __init__(self, nc, ctx, stage):
        self.nc, self.ctx, self.stage, self.sems = nc, ctx, stage, []
        ctx.callback(self.clear)

    def sb(self, name, shape, dt=F32):
        return self.ctx.enter_context(self.nc.sbuf_tensor(f"{self.stage}_{name}", shape, dt))

    def ps(self, name, cols=512, dt=F32):
        return self.ctx.enter_context(self.nc.psum_tensor(f"{self.stage}_{name}", [P, cols], dt))

    def sem(self, name):
        self.sems.append(self.nc.alloc_semaphore(name=f"{self.stage}_{name}"))
        return self.sems[-1]

    def clear(self):
        self.nc.clear_and_free_semaphores(self.sems)
        self.nc.all_engine_barrier()


def loop_pairs(eng, n, body, peel=1, step=2):
    for k in range(min(peel, n // step)):
        for u in range(step):
            body(step * k + u, u, k)
    if n // step > peel:
        with eng.Fori(peel, n // step) as k:
            for u in range(step):
                body(k * step + u, u, k)


def loop_blocks(eng, n, body, step=LONG_UNROLL):
    m = (n - 1) // step * step
    loop_pairs(eng, m, body, step=step)
    for b in range(m, n):
        body(b, b % step, b // step)


def is_last(b, nb):
    return isinstance(b, int) and b == nb - 1


def times(u, nb):
    return (nb - u + LONG_UNROLL - 1) // LONG_UNROLL


def bcast(ap, dim, count):
    shape = list(ap.shape)
    return ap.unsqueeze(dim).to_broadcast(shape[:dim] + [count] + shape[dim:])


def idle(C, *engines):
    for engine in engines:
        @engine
        def _(eng):
            settle(eng, C)


def either(eng, flag, yes, no):
    taken = eng.value_load(flag[0:1, 0:1], min_val=0, max_val=1)
    with eng.If(taken != 0):
        yes()
    with eng.Else():
        no()


def settle(eng, C):
    eng.sem_inc(C["settled"], 1)


def constants(nc, C):
    ctx = ExitStack()
    with ctx:
        a = Names(nc, ctx, "const")
        done, filled = a.sem("done"), a.sem("filled")
        block = ctx.enter_context(nc.Block())

        @block.gpsimd
        def _(pool):
            pool.memset(C["ident"][:, :], 0.0).then_inc(filled, 1)
            pool.memset(C["before"][:, :], 1.0).then_inc(filled, 1)
            pool.memset(C["not_before"][:, :], 1.0).then_inc(filled, 1)
            pool.memset(C["ones"][:, :], 1.0).then_inc(done, 1)
            pool.memset(C["ones_f32"][:, :], 1.0).then_inc(done, 1)
            pool.wait_ge(filled, 3)
            pool.affine_select(out=C["ident"][:, :], in_=C["ident"][:, :], compare_op=ALU.not_equal, fill=1.0,
                               base=0, pattern=[[-1, P]], channel_multiplier=1).then_inc(done, 1)
            pool.affine_select(out=C["before"][:, :], in_=C["before"][:, :], compare_op=ALU.is_gt, fill=0.0,
                               base=0, pattern=[[1, P]], channel_multiplier=-1).then_inc(done, 1)
            pool.affine_select(out=C["not_before"][:, :], in_=C["not_before"][:, :], compare_op=ALU.is_ge, fill=0.0,
                               base=0, pattern=[[-1, P]], channel_multiplier=1).then_inc(done, 1)
            nb = C["blocks"]
            pool.iota(C["block_ramp"][:, :], [[1, nb]], base=0, channel_multiplier=0,
                      allow_small_or_imprecise_dtypes=True).then_inc(done, 1)
            pool.iota(C["node_ramp"][:, :], [[1, P]], base=0, channel_multiplier=0,
                      allow_small_or_imprecise_dtypes=True).then_inc(done, 1)
            pool.wait_ge(done, 7)


def make_hot(nc, C, hot, blk, g, nb):
    return nc.vector.tensor_tensor(hot[:, :].rearrange("p (c b) -> p c b", c=RANKED), bcast(C["block_ramp"][:, :], 1, RANKED),
                             bcast(blk[:, bass.ds(g * RANKED, RANKED)], 2, nb), ALU.is_equal)


def examine_destinations(nc, C, dst, cols, nb, n_edges, count, unsorted):
    e_pad, nb1, width = P * cols, nb + 1, 512
    chunks = -(-cols // width)
    ctx = ExitStack()
    with ctx:
        a = Names(nc, ctx, "examine")
        keys, after = a.sb("keys", [P, cols], I32), a.sb("after", [P, cols], I32)
        of_block, after_block = a.sb("of_block", [P, cols], I32), a.sb("after_block", [P, cols], I32)
        blk = a.sb("blk", [P, cols], BF16)
        first = a.sb("first", [P, 1])
        falls, fall = a.sb("falls", [P, cols]), a.sb("fall", [P, 1])
        ramp, own, own_bf = a.sb("ramp", [P, nb1]), a.sb("own", [P, 1]), a.sb("own_bf", [P, 1], BF16)
        starts_below, holder = a.sb("starts_below", [P, nb1], BF16), a.sb("holder", [P, nb1])
        holds = a.sb("holds", [P, nb1], BF16)
        below, inside = a.sb("below", [P, cols]), a.sb("inside", [P, 1])
        lower, diagonal, lower_row = a.sb("lower", [P, 1]), a.sb("diagonal", [P, nb1]), a.sb("lower_row", [P, nb1])
        sums_ps = a.ps("sums")
        FALL, STARTS, HOLDER, ROW = 0, 1, 1 + nb1, 2 + nb1
        rows_ps = [a.ps(f"rows{c}") for c in range(chunks)]
        loaded, ch, last_ready, ramps_ready = (a.sem(s) for s in ("loaded", "chain", "last_ready", "ramps_ready"))
        fall_ready, fall_summed, starts_ready, starts_summed = (
            a.sem(s) for s in ("fall_ready", "fall_summed", "starts_ready", "starts_summed"))
        holds_ready, rows_ready, diagonal_ready, row_ready = (
            a.sem(s) for s in ("holds_ready", "rows_ready", "diagonal_ready", "row_ready"))
        block = ctx.enter_context(nc.Block())

        @block.sync
        def _(sp):
            sp.dma_start(keys[:, :], dst.rearrange("(p c) -> p c", p=P)).then_inc(loaded, 16)
            sp.wait_ge(last_ready, 1)
            sp.dma_start(after[0:P - 1, :], dst[1:1 + (P - 1) * cols].rearrange("(p c) -> p c", p=P - 1)).then_inc(loaded, 16)
            sp.dma_start(after[P - 1:P, 0:cols - 1], dst[1 + (P - 1) * cols:e_pad].rearrange("(p c) -> p c", p=1))\
                .then_inc(loaded, 16)

        @block.gpsimd
        def _(pool):
            pool.iota(ramp[:, :], [[1, nb1]], base=0, channel_multiplier=0,
                      allow_small_or_imprecise_dtypes=True).then_inc(ramps_ready, 1)
            pool.iota(own[:, :], [[1, 1]], base=0, channel_multiplier=1,
                      allow_small_or_imprecise_dtypes=True).then_inc(ramps_ready, 1)

        @block.tensor
        def _(pe):
            pe.wait_ge(starts_ready, 1)
            nc.tensor.matmul(sums_ps[:, STARTS:STARTS + nb1], C["ones"][:, :], starts_below[:, :], start=True, stop=True)\
                .then_inc(starts_summed, 1)
            pe.wait_ge(holds_ready, 1)
            nc.tensor.matmul(sums_ps[0:nb1, HOLDER:HOLDER + 1], holds[:, :], own_bf[:, :], start=True, stop=True)
            for c in range(chunks):
                n = min(width, cols - c * width)
                last_ = nc.tensor.matmul(rows_ps[c][0:nb1, 0:n], holds[:, :], blk[:, c * width:c * width + n],
                                         start=True, stop=True)
            last_.then_inc(rows_ready, 1)
            pe.wait_ge(fall_ready, 1)
            nc.tensor.matmul(sums_ps[:, FALL:FALL + 1], C["ones_f32"][:, :], fall[:, :], start=True, stop=True)\
                .then_inc(fall_summed, 1)
            pe.wait_ge(diagonal_ready, 1)
            nc.tensor.matmul(sums_ps[:, ROW:ROW + nb1], C["ones_f32"][0:nb1, :], diagonal[0:nb1, :], start=True, stop=True)\
                .then_inc(row_ready, 1)

        @block.vector
        def _(dve):
            chain = [0]

            def link(ins):
                chain[0] += 1
                ins.then_inc(ch, 1)
                dve.wait_ge(ch, chain[0])

            nc.vector.memset(after[:, cols - 1:cols], (nb + 1) * P).then_inc(last_ready, 1)
            dve.wait_ge(loaded, 48)
            dve.wait_ge(ramps_ready, 2)
            link(nc.vector.tensor_scalar(of_block[:, :], keys[:, :], 7, None, ALU.logical_shift_right))
            link(nc.vector.tensor_copy(blk[:, :], of_block[:, :]))
            link(nc.vector.tensor_copy(first[:, :], of_block[:, 0:1]))
            link(nc.vector.tensor_copy(own_bf[:, :], own[:, :]))
            nc.vector.tensor_scalar(starts_below[:, :], ramp[:, :], first[:, :], None, ALU.is_gt).then_inc(starts_ready, 1)
            link(nc.vector.tensor_scalar(after_block[:, :], after[:, :], 7, None, ALU.logical_shift_right))
            link(nc.vector.tensor_tensor(falls[:, :], of_block[:, :], after_block[:, :], ALU.is_gt))
            dve.wait_ge(starts_summed, 1)
            link(nc.vector.tensor_scalar(holder[:, :], sums_ps[:, STARTS:STARTS + nb1], -1.0, 0.0, ALU.add, ALU.max))
            nc.vector.tensor_scalar(holds[:, :], holder[:, :], own[:, :], None, ALU.is_equal).then_inc(holds_ready, 1)
            dve.wait_ge(rows_ready, 1)
            for c in range(chunks):
                n = min(width, cols - c * width)
                link(nc.vector.tensor_scalar(below[0:nb1, c * width:c * width + n], rows_ps[c][0:nb1, 0:n], own[0:nb1, :],
                                             None, ALU.is_lt))
            link(nc.vector.tensor_reduce(inside[0:nb1, :], below[0:nb1, :], AXX, ALU.add))
            link(nc.vector.scalar_tensor_tensor(lower[0:nb1, :], sums_ps[0:nb1, HOLDER:HOLDER + 1], float(cols),
                                                inside[0:nb1, :], ALU.mult, ALU.add))
            nc.vector.tensor_reduce(fall[:, :], falls[:, :], AXX, ALU.add).then_inc(fall_ready, 1)
            nc.vector.tensor_scalar(diagonal[0:nb1, :], C["ident"][0:nb1, 0:nb1], lower[0:nb1, :], None, ALU.mult)\
                .then_inc(diagonal_ready, 1)
            dve.wait_ge(fall_summed, 1)
            dve.wait_ge(row_ready, 1)
            link(nc.vector.tensor_scalar(unsorted[:, :], sums_ps[0:1, FALL:FALL + 1], 1.0, None, ALU.min))
            link(nc.vector.tensor_copy(lower_row[:, :], sums_ps[:, ROW:ROW + nb1]))
            link(nc.vector.tensor_tensor(count[:, :], lower_row[:, 1:nb1], lower_row[:, 0:nb], ALU.subtract))


def count_edges(nc, C, stage, key, cols, nb, total, count):
    W = RANKED * nb
    n = cols // RANKED
    ctx = ExitStack()
    with ctx:
        a = Names(nc, ctx, stage)
        keys, of_block = a.sb("keys", [P, cols], I32), a.sb("of_block", [P, cols], I32)
        blk = a.sb("blk", [P, cols], BF16)
        hot = [a.sb(f"hot{i}", [P, W], BF16) for i in range(4)]
        totals_ps = [a.ps(f"totals{i}") for i in range(2)]
        loaded, ch, hot_ready, summed = (a.sem(s) for s in ("loaded", "chain", "hot_ready", "summed"))
        block = ctx.enter_context(nc.Block())
        idle(C, block.scalar, block.gpsimd)

        @block.sync
        def _(sp):
            sp.dma_start(keys[:, :], key.rearrange("(p c) -> p c", p=P)).then_inc(loaded, 16)

        @block.tensor
        def _(pe):
            def count_batch(g, u, k):
                pe.wait_ge(hot_ready, g + 1)
                nc.tensor.matmul(totals_ps[u % 2][:, 0:W], C["ones"][:, :], hot[u][:, :],
                                 start=before(g, 2), stop=isinstance(g, int) and g >= n - 2).then_inc(summed, 1)
            loop_blocks(pe, n, count_batch, UNROLL)

        @block.vector
        def _(dve):
            chain = [0]

            def link(ins):
                chain[0] += 1
                ins.then_inc(ch, 1)
                dve.wait_ge(ch, chain[0])

            dve.wait_ge(loaded, 16)
            link(nc.vector.tensor_scalar(of_block[:, :], keys[:, :], 7, None, ALU.logical_shift_right))
            link(nc.vector.tensor_copy(blk[:, :], of_block[:, :]))

            def count_batch(g, u, k):
                if not before(g, 4):
                    dve.wait_ge(summed, g - 3)
                make_hot(nc, C, hot[u], blk, g, nb).then_inc(hot_ready, 1)
            loop_blocks(dve, n, count_batch, UNROLL)
            dve.wait_ge(summed, n)
            for u in range(2):
                link(nc.vector.tensor_copy(total[:, u * W:(u + 1) * W], totals_ps[u][:, 0:W]))
            link(nc.vector.tensor_reduce(count[:, :], total[:, :].rearrange("p (c b) -> p b c", c=2 * RANKED), AXX, ALU.add))


def rank(nc, C, stage, key, cols, nb, pos_dram, total, count):
    W = RANKED * nb
    n = cols // RANKED
    ctx = ExitStack()
    with ctx:
        a = Names(nc, ctx, stage)
        keys = a.sb("keys", [P, cols], I32)
        of_block = a.sb("of_block", [P, cols], I32)
        blk = a.sb("blk", [P, cols], BF16)
        hot = [a.sb(f"hot{i}", [P, W], BF16) for i in range(4)]
        picked = [a.sb(f"picked{i}", [P, W]) for i in range(4)]
        place = a.sb("place", [P, cols])
        own = a.sb("own", [P, cols])
        padding = a.sb("padding", [P, cols])
        place_i = a.sb("place_i", [P, cols], I32)
        base = a.sb("base", [P, 2 * W])
        end = a.sb("end", [P, nb])
        zeros = a.sb("zeros", [P, nb])
        ranks_ps = [a.ps(f"ranks{i}") for i in range(2)]
        loaded, ch, iota_done = a.sem("loaded"), a.sem("chain"), a.sem("iota")
        base_ready, based = a.sem("base_ready"), a.sem("based")
        hot_ready, ranked, read, advanced = a.sem("hot_ready"), a.sem("ranked"), a.sem("read"), a.sem("advanced")
        reduced, stored = a.sem("reduced"), a.sem("stored")
        block = ctx.enter_context(nc.Block())

        @block.sync
        def _(sp):
            sp.dma_start(keys[:, :], key.rearrange("(p c) -> p c", p=P)).then_inc(loaded, 16)
            sp.wait_ge(stored, 1)
            sp.dma_start(pos_dram.rearrange("(p c) -> p c", p=P), place_i[:, :]).then_inc(loaded, 16)
            sp.wait_ge(loaded, 32)

        @block.gpsimd
        def _(pool):
            pool.iota(own[:, :], [[1, cols]], base=0, channel_multiplier=cols,
                      allow_small_or_imprecise_dtypes=True).then_inc(iota_done, 1)

        @block.tensor
        def _(pe):
            pe.wait_ge(base_ready, 1)
            for v in range(2):
                nc.tensor.matmul(ranks_ps[v][:, 0:W], C["ident"][:, :], base[:, v * W:(v + 1) * W], start=True, stop=True)\
                    .then_inc(based, 1)

            def advance(g, u, k):
                pe.wait_ge(read, g + 1)
                nc.tensor.matmul(ranks_ps[u % 2][:, 0:W], C["not_before"][:, :], hot[u][:, :], start=False, stop=True,
                                 skip_group_check=True).then_inc(advanced, 1)

            def rank_batch(g, u, k):
                if not before(g, 2):
                    advance(*shifted(g, u, k, -2))
                pe.wait_ge(hot_ready, g + 1)
                nc.tensor.matmul(ranks_ps[u % 2][:, 0:W], C["before"][:, :], hot[u][:, :], start=False, stop=True,
                                 skip_group_check=True).then_inc(ranked, 1)
            loop_blocks(pe, n, rank_batch, UNROLL)

        @block.scalar
        def _(act):
            def reduce_batch(g, u, k):
                act.wait_ge(read, g + 1)
                for c in range(RANKED):
                    last_ = nc.scalar.activation(picked[u][:, c * nb:(c + 1) * nb], picked[u][:, c * nb:(c + 1) * nb], ACT.Copy,
                                                 accum_out=place[:, bass.ds(g * RANKED + c, 1)])
                last_.then_inc(reduced, 1)
            loop_blocks(act, n, reduce_batch, UNROLL)

        @block.vector
        def _(dve):
            chain = [0]

            def link(ins):
                chain[0] += 1
                ins.then_inc(ch, 1)
                dve.wait_ge(ch, chain[0])

            dve.wait_ge(loaded, 16)
            link(nc.vector.tensor_scalar(of_block[:, :], keys[:, :], 7, None, ALU.logical_shift_right))
            link(nc.vector.tensor_copy(blk[:, :], of_block[:, :]))
            link(nc.vector.memset(zeros[:, :], 0.0))
            link(nc.vector.tensor_tensor_scan(end[:, :], count[:, :], zeros[:, :], 0.0, ALU.add, ALU.add))
            link(nc.vector.tensor_tensor(base[:, 0:nb], end[:, :], count[:, :], ALU.subtract))
            for c in range(1, 2 * RANKED):
                ins = nc.vector.tensor_tensor(base[:, c * nb:(c + 1) * nb], base[:, (c - 1) * nb:c * nb],
                                              total[:, (c - 1) * nb:c * nb], ALU.add)
                if c < 2 * RANKED - 1:
                    link(ins)
                else:
                    ins.then_inc(base_ready, 1)
            dve.wait_ge(based, 2)

            def hot_batch(g, u, k):
                if not before(g, 4):
                    dve.wait_ge(advanced, g - 3)
                make_hot(nc, C, hot[u], blk, g, nb).then_inc(hot_ready, 1)

            def step(g, u, k):
                dve.wait_ge(ranked, g + 1)
                if not before(g, 4):
                    dve.wait_ge(reduced, g - 3)
                nc.vector.tensor_tensor(picked[u][:, :], ranks_ps[u % 2][:, 0:W], hot[u][:, :], ALU.mult).then_inc(read, 1)
                if not (isinstance(g, int) and g >= n - 2):
                    hot_batch(*shifted(g, u, k, 2))
            hot_batch(0, 0, 0)
            hot_batch(1, 1, 0)
            loop_blocks(dve, n, step, UNROLL)
            dve.wait_ge(iota_done, 1)
            dve.wait_ge(reduced, n)
            link(nc.vector.tensor_scalar(padding[:, :], blk[:, :], float(nb), None, ALU.is_ge))
            link(nc.vector.tensor_tensor(padding[:, :], padding[:, :], own[:, :], ALU.mult))
            nc.vector.tensor_tensor(place_i[:, :], place[:, :], padding[:, :], ALU.add).then_inc(stored, 1)


def group_table(nc, C, stage, count, nb, n_edges, ng, meta_dram, table, last):
    cols = -(-ng // P)
    ctx = ExitStack()
    with ctx:
        a = Names(nc, ctx, stage)
        up = a.sb("up", [P, nb], I32)
        groups_i = a.sb("groups_i", [P, nb], I32)
        groups = a.sb("groups", [P, nb])
        zeros = a.sb("zeros", [P, nb])
        end = a.sb("end", [P, nb])
        start = a.sb("start", [P, nb])
        slack = a.sb("slack", [P, nb])
        g_of = a.sb("g_of", [P, cols])
        junk = a.sb("junk", [P, nb])
        out = a.sb("out", [P, 3, cols])
        ch, iota_done, made, moved = a.sem("chain"), a.sem("iota"), a.sem("made"), a.sem("moved")
        block = ctx.enter_context(nc.Block())

        @block.gpsimd
        def _(pool):
            pool.iota(g_of[:, :], [[P, cols]], base=0, channel_multiplier=1,
                      allow_small_or_imprecise_dtypes=True).then_inc(iota_done, 1)

        @block.vector
        def _(dve):
            chain = [0]

            def link(ins):
                chain[0] += 1
                ins.then_inc(ch, 1)
                dve.wait_ge(ch, chain[0])

            link(nc.vector.tensor_scalar(up[:, :], count[:, :], float(G - 1), None, ALU.add))
            link(nc.vector.tensor_scalar(groups_i[:, :], up[:, :], G.bit_length() - 1, None, ALU.logical_shift_right))
            link(nc.vector.tensor_scalar(groups[:, :], groups_i[:, :], 1.0, None, ALU.max))
            link(nc.vector.memset(zeros[:, :], 0.0))
            link(nc.vector.tensor_tensor_scan(end[:, :], groups[:, :], zeros[:, :], 0.0, ALU.add, ALU.add))
            link(nc.vector.tensor_tensor(start[:, :], end[:, :], groups[:, :], ALU.subtract))
            link(nc.vector.scalar_tensor_tensor(slack[:, :], groups[:, :], float(-G), count[:, :], ALU.mult, ALU.add))
            link(nc.vector.tensor_scalar(last[:, :], end[0:1, :], -1.0, None, ALU.add))
            dve.wait_ge(iota_done, 1)
            for c in range(cols):
                g = g_of[:, c:c + 1]
                link(nc.vector.scalar_tensor_tensor(junk[:, :], end[:, :], g, slack[:, :], ALU.is_le, ALU.mult))
                link(nc.vector.tensor_reduce(out[:, 0, c:c + 1], junk[:, :], AXX, ALU.add))
                link(nc.vector.tensor_scalar(junk[:, :], end[:, :], g, float(P), ALU.is_le, ALU.mult))
                link(nc.vector.tensor_reduce(out[:, 1, c:c + 1], junk[:, :], AXX, ALU.add))
                link(nc.vector.tensor_scalar(junk[:, :], start[:, :], g, None, ALU.is_equal))
                link(nc.vector.tensor_reduce(out[:, 2, c:c + 1], junk[:, :], AXX, ALU.add))
            link(nc.vector.scalar_tensor_tensor(out[:, 0, :], g_of[:, :], float(G), out[:, 0, :], ALU.mult, ALU.add))
            link(nc.vector.tensor_scalar(out[:, 0, :], out[:, 0, :], float(n_edges), None, ALU.min))
            nc.vector.tensor_scalar(out[:, 2, :], out[:, 2, :], -1.0, 1.0, ALU.mult, ALU.add).then_inc(made, 1)

        @block.sync
        def _(sp):
            sp.wait_ge(made, 1)
            with nc.allow_non_contiguous_dma(reason="a table of a few hundred words"):
                for r in range(3):
                    sp.dma_start(meta_dram[r, :].rearrange("(c p) -> p c", p=P), out[:, r, :]).then_inc(moved, 16)
            sp.wait_ge(moved, 48)
            for r in range(3):
                sp.dma_start(table[:, r, :], meta_dram[r:r + 1, 0:ng].to_broadcast([P, ng])).then_inc(moved, 16)
            sp.wait_ge(moved, 96)


def ids_in_order(nc, C, A, posb, ids_a, cols):
    ctx = ExitStack()
    with ctx:
        a = Names(nc, ctx, "ids")
        ids = a.sb("ids", [P, cols, 3], I32)
        one = [a.sb(f"one{i}", [P, cols], I32) for i in range(3)]
        loaded, ids_ready, stored = a.sem("loaded"), a.sem("ids_ready"), a.sem("stored")
        block = ctx.enter_context(nc.Block())
        idle(C, block.scalar, block.tensor, block.gpsimd)

        @block.sync
        def _(sp):
            for i, x in enumerate((A["src"], A["dst"], posb)):
                sp.dma_start(one[i][:, :], x.rearrange("(p c) -> p c", p=P)).then_inc(loaded, 16)
            sp.wait_ge(ids_ready, 3)
            sp.dma_start(ids_a.rearrange("(p c) w -> p c w", p=P), ids[:, :, :]).then_inc(stored, 16)
            sp.wait_ge(stored, 16)

        @block.vector
        def _(dve):
            dve.wait_ge(loaded, 48)
            for i in range(3):
                nc.vector.tensor_copy(ids[:, :, i], one[i][:, :]).then_inc(ids_ready, 1)


def to_destination_order(nc, C, A, posa, posb, attr0_a, attr1_a, ids_a, cols):
    n = cols // RANKED
    ctx = ExitStack()
    with ctx:
        a = Names(nc, ctx, "pack")
        place = a.sb("place", [P, cols], I32)
        ids = a.sb("ids", [P, cols, 3], I32)
        one = [a.sb(f"one{i}", [P, cols], I32) for i in range(3)]
        r0 = [a.sb(f"r0_{i}", [P, RANKED, ATTR0]) for i in range(2)]
        r1 = [a.sb(f"r1_{i}", [P, RANKED, ATTR1]) for i in range(2)]
        r2 = [a.sb(f"r2_{i}", [P, RANKED, 3], I32) for i in range(2)]
        at = [a.sb(f"at{i}", [P, RANKED], I32) for i in range(2)]
        loaded, ids_ready, packed = a.sem("loaded"), a.sem("ids_ready"), a.sem("packed")
        filled = [a.sem(f"filled{i}") for i in range(2)]
        scattered = [a.sem(f"scattered{i}") for i in range(2)]
        block = ctx.enter_context(nc.Block())
        idle(C, block.scalar, block.tensor)

        def columns(ap, g):
            return ap.rearrange("(p c) w -> p c w", p=P)[:, bass.ds(g * RANKED, RANKED), :]

        @block.sync
        def _(sp):
            for i, x in enumerate((A["src"], A["dst"], posb)):
                sp.dma_start(one[i][:, :], x.rearrange("(p c) -> p c", p=P)).then_inc(loaded, 16)
            sp.dma_start(place[:, :], posa.rearrange("(p c) -> p c", p=P)).then_inc(loaded, 16)

            def load(g, u, k):
                if not before(g, 2):
                    sp.wait_ge(scattered[u], k * (48 * RANKED))
                    settle(sp, C)
                sp.dma_start(r0[u][:, :, :], columns(A["attr0"], g)).then_inc(filled[u], 16)
                sp.dma_start(r1[u][:, :, :], columns(A["attr1"], g)).then_inc(filled[u], 16)
            loop_pairs(sp, n, load)

        @block.vector
        def _(dve):
            dve.wait_ge(loaded, 64)
            for i in range(3):
                nc.vector.tensor_copy(ids[:, :, i], one[i][:, :]).then_inc(ids_ready, 1)
            dve.wait_ge(ids_ready, 3)

            def pack(g, u, k):
                if not before(g, 2):
                    dve.wait_ge(scattered[u], k * (48 * RANKED))
                nc.vector.tensor_copy(r2[u][:, :, :], ids[:, bass.ds(g * RANKED, RANKED), :]).then_inc(packed, 1)
                nc.vector.tensor_copy(at[u][:, :], place[:, bass.ds(g * RANKED, RANKED)]).then_inc(packed, 1)
            loop_pairs(dve, n, pack)

        @block.gpsimd
        def _(pool):
            def scatter(g, u, k):
                pool.wait_ge(filled[u], k * 32 + 32)
                pool.wait_ge(packed, g * 2 + 2)
                settle(pool, C)
                for j in range(RANKED):
                    for out, row in ((attr0_a, r0), (attr1_a, r1), (ids_a, r2)):
                        pool.indirect_dma_start(
                            out=out, out_offset=bass.IndirectOffsetOnAxis(ap=at[u][:, j:j + 1], axis=0),
                            in_=row[u][:, j, :], in_offset=None).then_inc(scattered[u], 16)
            loop_pairs(pool, n, scatter)
            for u in range(2):
                pool.wait_ge(scattered[u], 48 * RANKED * (n // 2))


def before_gnn0(nc, C, x, attr, Wn, nb, x1, base):
    U = LONG_UNROLL
    ctx = ExitStack()
    with ctx:
        a = Names(nc, ctx, "node0")
        xin = [a.sb(f"x{i}", [P, D]) for i in range(U)]
        at = [a.sb(f"attr{i}", [P, 3]) for i in range(U)]
        hs = [a.sb(f"h{i}", [P, D]) for i in range(2)]
        hT = [a.sb(f"hT{i}", [P, 2 * P]) for i in range(2)]
        o1 = [a.sb(f"x1_{i}", [P, D]) for i in range(U)]
        ob = [a.sb(f"base{i}", [P, D]) for i in range(U)]
        tmp = [a.sb(f"tmp{i}", [P, 2 * D]) for i in range(2)]
        st, rs = a.sb("st", [P, 6]), a.sb("rs", [P, 1])
        mv = [a.sb(f"mv{i}", [P, 2]) for i in range(2)]
        sd = [a.sb(f"sd{i}", [P, 1]) for i in range(2)]
        eps = a.sb("eps", [P, 1])
        tps = [a.ps(f"t{i}") for i in range(2)]
        sps = [a.ps(f"s{i}") for i in range(2)]
        vps = [a.ps(f"v{i}") for i in range(2)]
        ld = [a.sem(f"loaded{i}") for i in range(U)]
        stx = [a.sem(f"stored{i}") for i in range(U)]
        zero = a.sb("zero", [P, D])
        zero_ready, zero_out, eps_ready = a.sem("zero_ready"), a.sem("zero_out"), a.sem("eps_ready")
        stats_ready, var, root, inverse, h_ready, tr, ev, mm, halves, sums, made = (
            a.sem(s) for s in ("stats_ready", "var", "root", "inverse", "h_ready", "transposed", "evacuated", "mixed",
                               "halves", "sums", "made"))
        block = ctx.enter_context(nc.Block())

        def rows(ap, b):
            return ap[bass.ds(b * P, P), :]

        @block.sync
        def _(sp):
            def step(b, u, k):
                if not before(b, U):
                    sp.wait_ge(made, b - (U - 1))
                settle(sp, C)
                sp.dma_start(xin[u][:, :], rows(x, b)).then_inc(ld[u], 16)
                sp.dma_start(at[u][:, :], rows(attr, b)).then_inc(ld[u], 16)
            loop_blocks(sp, nb, step)

        @block.vector
        def _(dve):
            nc.vector.memset(eps[:, :], LN_EPS).then_inc(eps_ready, 1)
            nc.vector.memset(zero[:, :], 0.0).then_inc(zero_ready, 1)

            def stats(b, u, k):
                dve.wait_ge(ld[u], k * 32 + 32)
                if not before(b, 1):
                    dve.wait_ge(var, b)
                if not before(b, 2):
                    dve.wait_ge(h_ready, b - 1)
                nc.vector.bn_stats(st[:, :], xin[u][:, :]).then_inc(stats_ready, 1)
                dve.wait_ge(stats_ready, b + 1)
                settle(dve, C)
                nc.vector.bn_aggr(mv[u % 2][:, :], st[:, :]).then_inc(var, 1)

            def norm(b, u, k):
                dve.wait_ge(root, b + 1)
                if not before(b, 1):
                    dve.wait_ge(h_ready, b)
                nc.vector.reciprocal(rs[:, :], sd[u % 2][:, :]).then_inc(inverse, 1)
                dve.wait_ge(inverse, b + 1)
                if not before(b, 2):
                    dve.wait_ge(tr, b - 1)
                nc.vector.tensor_scalar(hs[u % 2][:, :], xin[u][:, :], mv[u % 2][:, 0:1], rs[:, :], ALU.subtract, ALU.mult)\
                    .then_inc(h_ready, 1)

            def mix(b, u, k):
                v = u % 2
                dve.wait_ge(mm, b + 1)
                if not before(b, 2):
                    dve.wait_ge(made, b - 1)
                s4 = sps[v][:, 0:4 * MS].rearrange("p (l a f) -> p l a f", l=2, a=2)
                v4 = vps[v][:, 0:4 * 96].rearrange("p (l a f) -> p l a f", l=2, a=2)
                t2 = tmp[v][:, :].rearrange("p (l f) -> p l f", l=2)
                nc.vector.tensor_scalar(t2[:, :, 0:MS], s4[:, :, 0, :], at[u][:, 0:1], None, ALU.mult)
                nc.vector.tensor_scalar(t2[:, :, MS:D], v4[:, :, 0, :], at[u][:, 0:1], None, ALU.mult).then_inc(halves, 1)
                dve.wait_ge(halves, b + 1)
                if not before(b, U):
                    dve.wait_ge(stx[u], k * 32)
                nc.vector.scalar_tensor_tensor(ob[u][:, 0:MS], s4[:, 1, 1, :], at[u][:, 1:2], t2[:, 1, 0:MS], ALU.mult, ALU.add)
                nc.vector.scalar_tensor_tensor(ob[u][:, MS:D], v4[:, 1, 1, :], at[u][:, 1:2], t2[:, 1, MS:D], ALU.mult, ALU.add)\
                    .then_inc(sums, 1)
                nc.vector.scalar_tensor_tensor(o1[u][:, 0:MS], s4[:, 0, 1, :], at[u][:, 1:2], t2[:, 0, 0:MS], ALU.mult, ALU.add)
                nc.vector.scalar_tensor_tensor(o1[u][:, MS:D], v4[:, 0, 1, :], at[u][:, 1:2], t2[:, 0, MS:D], ALU.mult, ALU.add)
                dve.wait_ge(sums, b + 1)
                nc.vector.tensor_tensor(ob[u][:, :], ob[u][:, :], xin[u][:, :], ALU.add).then_inc(made, 1)

            def step(b, u, k):
                if not is_last(b, nb):
                    stats(*shifted(b, u, k, 1, U))
                norm(b, u, k)
                if not before(b, 2):
                    mix(*shifted(b, u, k, -2, U))
            stats(0, 0, 0)
            loop_blocks(dve, nb, step)
            for b in (nb - 2, nb - 1):
                mix(b, b % U, b // U)

        @block.scalar
        def _(act):
            act.wait_ge(eps_ready, 1)

            def deviation(b, u, k):
                act.wait_ge(var, b + 1)
                if not before(b, 2):
                    act.wait_ge(inverse, b - 1)
                nc.scalar.activation(sd[u % 2][:, :], mv[u % 2][:, 1:2], ACT.Sqrt, bias=eps[:, :]).then_inc(root, 1)

            def step(b, u, k):
                if not is_last(b, nb):
                    deviation(*shifted(b, u, k, 1, U))
                act.wait_ge(tr, b + 1)
                if not before(b, 2):
                    act.wait_ge(mm, b - 1)
                nc.scalar.activation(hT[u % 2][0:96, :], tps[u % 2][0:96, 0:2 * P], ACT.Relu).then_inc(ev, 1)
            deviation(0, 0, 0)
            loop_blocks(act, nb, step)

        @block.tensor
        def _(pe):
            def transpose_h(b, u, k):
                v = u % 2
                pe.wait_ge(h_ready, b + 1)
                if not before(b, 2):
                    pe.wait_ge(ev, b - 1)
                settle(pe, C)
                nc.tensor.transpose(tps[v][0:96, 0:P], hs[v][:, 0:96], C["ident"][:, :])
                nc.tensor.transpose(tps[v][0:96, P:2 * P], hs[v][:, MS:D], C["ident"][:, :]).then_inc(tr, 1)

            def mix(b, u, k):
                v = u % 2
                pe.wait_ge(ev, b + 1)
                if not before(b, 2):
                    pe.wait_ge(made, b - 1)
                settle(pe, C)
                nc.tensor.matmul(sps[v][:, 0:4 * MS], hT[v][0:MS, 0:P], Wn["s0"][0:MS, :], start=True, stop=True)
                nc.tensor.matmul(vps[v][:, 0:4 * 96], hT[v][0:96, P:2 * P], Wn["v0"][0:96, :], start=True, stop=True).then_inc(mm, 1)

            def step(b, u, k):
                transpose_h(b, u, k)
                if not before(b, 1):
                    mix(*shifted(b, u, k, -1, U))
            loop_blocks(pe, nb, step)
            mix(nb - 1, (nb - 1) % U, (nb - 1) // U)

        @block.gpsimd
        def _(pool):
            pool.wait_ge(zero_ready, 1)
            pool.dma_start(x1[nb * P:(nb + 1) * P, :], zero[:, :]).then_inc(zero_out, 16)
            pool.wait_ge(zero_out, 16)

            def step(b, u, k):
                pool.wait_ge(made, b + 1)
                settle(pool, C)
                pool.dma_start(rows(x1, b), o1[u][:, :]).then_inc(stx[u], 16)
                pool.dma_start(rows(base, b), ob[u][:, :]).then_inc(stx[u], 16)
            loop_blocks(pool, nb, step)
            for u in range(U):
                pool.wait_ge(stx[u], 32 * times(u, nb))


def prepare_weights(nc, C, Wd, Wn):
    ctx = ExitStack()
    with ctx:
        a = Names(nc, ctx, "weights")
        l2 = {k: a.sb(f"l2{k}", [96, 96]) for k in ("sa", "sc", "va", "vc")}
        l3s, l3v = a.sb("l3s", [96, MS]), a.sb("l3v", [96, MV])
        l2T = a.sb("l2T", [96, 4 * 96])
        tps, mps = a.ps("t"), a.ps("m")
        zeroed, loaded, scaled, tr, ev, mm = (a.sem(s) for s in ("zeroed", "loaded", "scaled", "tr", "ev", "mm"))
        block = ctx.enter_context(nc.Block())
        loads = []
        for i, m in enumerate(("Ws_l1_a", "Ws_l1_c", "Ws_sc_a", "Ws_sc_c")):
            loads.append((Wn["s0"][0:MS, i * MS:(i + 1) * MS], Wd["L0_gnn_" + m][:, :]))
        for i, m in enumerate(("Wv_l1_a", "Wv_l1_c", "Wv_sc_a", "Wv_sc_c")):
            for c in range(3):
                loads.append((Wn["v0"][c * MV:(c + 1) * MV, i * 96 + c * MV:i * 96 + (c + 1) * MV], Wd["L0_gnn_" + m][:, :]))
        for j in range(TILES):
            loads.append((Wn["fc1_0"][j * ATTR0:j * ATTR0 + 10, j * H0:(j + 1) * H0], Wd["L0_gnn_W_fc1"][:, :]))
        for j in range(2):
            loads.append((Wn["fc1_1"][j * 64:(j + 1) * 64, j * 64:(j + 1) * 64], Wd["L1_gnn_W_fc1"][:, :]))
            loads.append((Wn["fc2_1"][j * 64:(j + 1) * 64, j * WN1:(j + 1) * WN1], Wd["L1_gnn_W_fc2"][:, :]))
        for to, of, n in ((0, 0, MS), (MS, 2 * MS, MV), (MS + MV, MS, MS), (2 * MS + MV, 2 * MS + MV, MV)):
            loads.append((Wn["fc2_0"][0:H0, to:to + n], Wd["L0_gnn_W_fc2"][:, of:of + n]))
        for k, m in (("sa", "Ws_l2_a"), ("sc", "Ws_l2_c"), ("va", "Wv_l2_a"), ("vc", "Wv_l2_c")):
            loads.append((l2[k][:, :], Wd["L0_gnn_" + m][:, :]))
        loads.append((l3s[:, :], Wd["L0_gnn_Ws_l3"][:, :]))
        loads.append((l3v[:, :], Wd["L0_gnn_Wv_l3"][:, :]))
        loads.append((Wn["s1"][0:MS, 0:96], Wd["L1_gnn_W_skip0"][:, :]))
        loads.append((Wn["s1"][0:MS, 96:96 + MS], Wd["L1_gnn_W_nl0"][:, :]))
        for i, m in enumerate(("W_nl1", "W_skip1")):
            for c in range(3):
                loads.append((Wn["v1"][c * MV:(c + 1) * MV, i * 96 + c * MV:i * 96 + (c + 1) * MV], Wd["L1_gnn_" + m][:, :]))
        loads.append((Wn["outs"][0:96, :], Wd["L1_gnn_W_out_s"][:, :]))
        loads.append((Wn["outv"][:, :], Wd["L1_gnn_W_out_v"][:, :]))

        @block.sync
        def _(sp):
            sp.wait_ge(zeroed, 5)
            for to, of in loads:
                sp.dma_start(to, of).then_inc(loaded, 16)

        @block.vector
        def _(dve):
            for k in ("v0", "v1", "fc1_0", "fc1_1", "fc2_1"):
                nc.vector.memset(Wn[k][:, :], 0.0).then_inc(zeroed, 1)
            dve.wait_ge(loaded, 16 * len(loads))
            for w, f in ((Wn["s0"][0:MS, 2 * MS:4 * MS], C_S), (Wn["v0"][0:96, 2 * 96:4 * 96], C_S),
                         (Wn["fc2_0"][0:H0, 2 * MS + MV:WN0], 3.0 ** -0.5), (Wn["fc2_1"][:, 160:192], 3.0 ** -0.5),
                         (Wn["fc2_1"][:, 192:224], 2.0 ** -0.5), (Wn["fc2_1"][:, WN1 + 160:WN1 + 192], 3.0 ** -0.5),
                         (Wn["fc2_1"][:, WN1 + 192:WN1 + 224], 2.0 ** -0.5), (Wn["outs"][0:96, :], 1 / 32.0),
                         (Wn["outv"][:, :], 1 / 32.0)):
                nc.vector.tensor_scalar(w, w, f, None, ALU.mult).then_inc(scaled, 1)
            dve.wait_ge(tr, 1)
            nc.vector.tensor_copy(l2T[:, :], tps[0:96, 0:4 * 96]).then_inc(ev, 1)
            dve.wait_ge(mm, 1)
            nc.vector.tensor_scalar(Wn["ps"][0:96, :], mps[0:96, 0:2 * MS], C_X / 4.0, None, ALU.mult).then_inc(scaled, 1)
            nc.vector.tensor_scalar(Wn["pv"][0:96, :], mps[0:96, 2 * MS:2 * MS + 2 * MV], C_X / 4.0, None, ALU.mult).then_inc(scaled, 1)
            dve.wait_ge(scaled, 11)

        @block.tensor
        def _(pe):
            pe.wait_ge(loaded, 16 * len(loads))
            for i, k in enumerate(("sa", "sc", "va", "vc")):
                last = nc.tensor.transpose(tps[0:96, i * 96:(i + 1) * 96], l2[k][:, :], C["ident"][0:96, 0:96])
            last.then_inc(tr, 1)
            pe.wait_ge(ev, 1)
            at = 0
            for i, w, n in ((0, l3s, MS), (1, l3s, MS), (2, l3v, MV), (3, l3v, MV)):
                last = nc.tensor.matmul(mps[0:96, at:at + n], l2T[:, i * 96:(i + 1) * 96], w[:, :], start=True, stop=True)
                at += n
            last.then_inc(mm, 1)


def between(nc, C, agg, last, base, attr, Wn, nb, x2, mixed):
    U = LONG_UNROLL
    ctx = ExitStack()
    with ctx:
        a = Names(nc, ctx, "node1")
        def several(n, name, shape):
            return [a.sb(f"{name}{i}", shape) for i in range(n)]
        ag, bs, at = several(U, "agg", [P, AGG0]), several(U, "base", [P, D]), several(U, "attr", [P, 3])
        mT, hT, hs = several(2, "mT", [P, 4 * P]), several(2, "hT", [P, 2 * P]), several(2, "h", [P, D])
        xo, mo = several(U, "x2", [P, D]), several(U, "mixed", [P, MIXED])
        mv, sd = several(2, "mv", [P, 2]), several(2, "sd", [P, 1])
        am, st, rs, eps = a.sb("am", [P, 2]), a.sb("st", [P, 6]), a.sb("rs", [P, 1]), a.sb("eps", [P, 1])
        mps, ops = [a.ps(f"m{i}") for i in range(2)], [a.ps(f"o{i}") for i in range(2)]
        hps, kps = a.ps("h"), [a.ps(f"k{i}") for i in range(2)]
        ld = [a.sem(f"loaded{i}") for i in range(U)]
        stx = [a.sem(f"stored{i}") for i in range(U)]
        eps_ready, masked, first, x2_ready, stats_ready, inverse = (
            a.sem(s) for s in ("eps_ready", "masked", "first", "x2_ready", "stats_ready", "inverse"))
        mtr, mev, mmm, var, root, h_ready, htr, hev, hmm, made = (
            a.sem(s) for s in ("mtr", "mev", "mmm", "var", "root", "h_ready", "htr", "hev", "hmm", "made"))
        block = ctx.enter_context(nc.Block())
        agg_rows = agg.rearrange("g p f -> (g p) f")

        def rows(ap, b):
            return ap[bass.ds(b * P, P), :]

        @block.sync
        def _(sp):
            def step(b, u, k):
                if not before(b, U):
                    sp.wait_ge(var, b - (U - 1))
                settle(sp, C)
                g = sp.value_load(last[0:1, bass.ds(b, 1)], min_val=0, max_val=agg.shape[0] - 1)
                sp.dma_start(ag[u][:, :], agg_rows[bass.ds(g * P, P), :]).then_inc(ld[u], 16)
                sp.dma_start(bs[u][:, :], rows(base, b)).then_inc(ld[u], 16)
                sp.dma_start(at[u][:, :], rows(attr, b)).then_inc(ld[u], 16)
            loop_blocks(sp, nb, step)

        @block.vector
        def _(dve):
            nc.vector.memset(eps[:, :], LN_EPS).then_inc(eps_ready, 1)

            def norm(b, u, k):
                dve.wait_ge(root, b + 1)
                if not before(b, 1):
                    dve.wait_ge(h_ready, b)
                nc.vector.reciprocal(rs[:, :], sd[u % 2][:, :]).then_inc(inverse, 1)
                dve.wait_ge(inverse, b + 1)
                if not before(b, 2):
                    dve.wait_ge(htr, b - 1)
                nc.vector.tensor_scalar(hs[u % 2][:, :], xo[u][:, :], mv[u % 2][:, 0:1], rs[:, :], ALU.subtract, ALU.mult)\
                    .then_inc(h_ready, 1)

            def combine(b, u, k):
                v = u % 2
                dve.wait_ge(ld[u], k * 48 + 48)
                if not before(b, 1):
                    dve.wait_ge(x2_ready, b)
                nc.vector.tensor_scalar(am[:, :], at[u][:, 0:2], at[u][:, 2:3], None, ALU.mult).then_inc(masked, 1)
                dve.wait_ge(mmm, b + 1)
                dve.wait_ge(masked, b + 1)
                if not before(b, U):
                    dve.wait_ge(stx[u], k * 32)
                s2 = ops[v][:, 0:2 * MS].rearrange("p (a f) -> p a f", a=2)
                v2 = ops[v][:, 2 * MS:2 * MS + 6 * MV].rearrange("p (c a f) -> p a c f", c=3, a=2)
                xv = xo[u][:, MS:D].rearrange("p (c f) -> p c f", c=3)
                bv = bs[u][:, MS:D].rearrange("p (c f) -> p c f", c=3)
                nc.vector.scalar_tensor_tensor(xo[u][:, 0:MS], s2[:, 0, :], am[:, 0:1], bs[u][:, 0:MS], ALU.mult, ALU.add)
                nc.vector.scalar_tensor_tensor(xv, v2[:, 0, :, :], am[:, 0:1], bv, ALU.mult, ALU.add).then_inc(first, 1)
                dve.wait_ge(first, b + 1)
                nc.vector.scalar_tensor_tensor(xo[u][:, 0:MS], s2[:, 1, :], am[:, 1:2], xo[u][:, 0:MS], ALU.mult, ALU.add)
                nc.vector.scalar_tensor_tensor(xv, v2[:, 1, :, :], am[:, 1:2], xv, ALU.mult, ALU.add).then_inc(x2_ready, 1)
                dve.wait_ge(x2_ready, b + 1)
                nc.vector.bn_stats(st[:, :], xo[u][:, :]).then_inc(stats_ready, 1)
                dve.wait_ge(stats_ready, b + 1)
                settle(dve, C)
                nc.vector.bn_aggr(mv[v][:, :], st[:, :]).then_inc(var, 1)

            def step(b, u, k):
                if not before(b, 1):
                    norm(*shifted(b, u, k, -1, U))
                combine(b, u, k)
            loop_blocks(dve, nb, step)
            norm(nb - 1, (nb - 1) % U, (nb - 1) // U)

        @block.scalar
        def _(act):
            act.wait_ge(eps_ready, 1)

            def take_sums(b, u, k):
                act.wait_ge(mtr, b + 1)
                if not before(b, 2):
                    act.wait_ge(mmm, b - 1)
                nc.scalar.copy(mT[u % 2][0:96, :], mps[u % 2][0:96, :]).then_inc(mev, 1)

            def take_h(b, u, k):
                act.wait_ge(htr, b + 1)
                if not before(b, 2):
                    act.wait_ge(hmm, b - 1)
                nc.scalar.activation(hT[u % 2][0:96, :], hps[0:96, 0:2 * P], ACT.Relu).then_inc(hev, 1)

            def outputs(b, u, k):
                act.wait_ge(hmm, b + 1)
                if not before(b, U):
                    act.wait_ge(stx[u], k * 32)
                nc.scalar.copy(mo[u][:, :], kps[u % 2][:, 0:MIXED]).then_inc(made, 1)

            def deviation(b, u, k):
                act.wait_ge(var, b + 1)
                if not before(b, 2):
                    act.wait_ge(inverse, b - 1)
                nc.scalar.activation(sd[u % 2][:, :], mv[u % 2][:, 1:2], ACT.Sqrt, bias=eps[:, :]).then_inc(root, 1)

            def step(b, u, k):
                if not is_last(b, nb):
                    take_sums(*shifted(b, u, k, 1, U))
                if not before(b, 1):
                    take_h(*shifted(b, u, k, -1, U))
                if not before(b, 2):
                    outputs(*shifted(b, u, k, -2, U))
                deviation(b, u, k)
            take_sums(0, 0, 0)
            loop_blocks(act, nb, step)
            take_h(nb - 1, (nb - 1) % U, (nb - 1) // U)
            for b in (nb - 2, nb - 1):
                outputs(b, b % U, b // U)

        @block.tensor
        def _(pe):
            def transpose_sums(b, u, k):
                pe.wait_ge(ld[u], k * 48 + 48)
                if not before(b, 2):
                    pe.wait_ge(mev, b - 1)
                for c in range(4):
                    last_ = nc.tensor.transpose(mps[u % 2][0:96, c * P:(c + 1) * P], ag[u][:, c * 96:(c + 1) * 96], C["ident"][:, :])
                last_.then_inc(mtr, 1)

            def mix_sums(b, u, k):
                v = u % 2
                pe.wait_ge(mev, b + 1)
                if not before(b, 2):
                    pe.wait_ge(x2_ready, b - 1)
                nc.tensor.matmul(ops[v][:, 0:2 * MS], mT[v][0:96, 0:P], Wn["ps"][0:96, :], start=True, stop=True)
                for c in range(3):
                    last_ = nc.tensor.matmul(ops[v][:, 2 * MS + c * 2 * MV:2 * MS + (c + 1) * 2 * MV],
                                             mT[v][0:96, (c + 1) * P:(c + 2) * P], Wn["pv"][0:96, :], start=True, stop=True)
                last_.then_inc(mmm, 1)

            def transpose_h(b, u, k):
                pe.wait_ge(h_ready, b + 1)
                if not before(b, 1):
                    pe.wait_ge(hev, b)
                settle(pe, C)
                nc.tensor.transpose(hps[0:96, 0:P], hs[u % 2][:, 0:96], C["ident"][:, :])
                nc.tensor.transpose(hps[0:96, P:2 * P], hs[u % 2][:, MS:D], C["ident"][:, :]).then_inc(htr, 1)

            def mix_h(b, u, k):
                v = u % 2
                pe.wait_ge(hev, b + 1)
                if not before(b, 2):
                    pe.wait_ge(made, b - 1)
                settle(pe, C)
                nc.tensor.matmul(kps[v][:, 0:96 + MS], hT[v][0:MS, 0:P], Wn["s1"][0:MS, :], start=True, stop=True)
                nc.tensor.matmul(kps[v][:, 96 + MS:MIXED], hT[v][0:96, P:2 * P], Wn["v1"][0:96, :], start=True, stop=True)\
                    .then_inc(hmm, 1)

            def step(b, u, k):
                if not is_last(b, nb):
                    transpose_sums(*shifted(b, u, k, 1, U))
                mix_sums(b, u, k)
                if not before(b, 1):
                    transpose_h(*shifted(b, u, k, -1, U))
                if not before(b, 2):
                    mix_h(*shifted(b, u, k, -2, U))
            transpose_sums(0, 0, 0)
            loop_blocks(pe, nb, step)
            transpose_h(nb - 1, (nb - 1) % U, (nb - 1) // U)
            for b in (nb - 2, nb - 1):
                mix_h(b, b % U, b // U)

        @block.gpsimd
        def _(pool):
            def step(b, u, k):
                pool.wait_ge(made, b + 1)
                settle(pool, C)
                pool.dma_start(rows(x2, b), xo[u][:, :]).then_inc(stx[u], 16)
                pool.dma_start(rows(mixed, b), mo[u][:, :]).then_inc(stx[u], 16)
            loop_blocks(pool, nb, step)
            for u in range(U):
                pool.wait_ge(stx[u], 32 * times(u, nb))


def after_gnn1(nc, C, agg, last, x2, mixed, Wn, nb, out):
    U = LONG_UNROLL
    ctx = ExitStack()
    with ctx:
        a = Names(nc, ctx, "node2")
        def several(n, name, shape):
            return [a.sb(f"{name}{i}", shape) for i in range(n)]
        ag, xs, ks = several(U, "agg", [P, AGG1]), several(U, "x2", [P, D]), several(U, "mixed", [P, 2 * W_STRIDE])
        mT, pre, sg = several(2, "mT", [P, 4 * P]), several(2, "pre", [P, 192]), several(2, "sg", [P, 96])
        tm, ot = several(2, "tm", [P, D]), several(U, "out", [P, D])
        mps, ops = [a.ps(f"m{i}") for i in range(2)], [a.ps(f"o{i}") for i in range(2)]
        ld = [a.sem(f"loaded{i}") for i in range(U)]
        stx = [a.sem(f"stored{i}") for i in range(U)]
        mtr, mev, mmm, pre_ready, sig, gated, made = (
            a.sem(s) for s in ("mtr", "mev", "mmm", "pre_ready", "sig", "gated", "made"))
        block = ctx.enter_context(nc.Block())
        agg_rows = agg.rearrange("g p f -> (g p) f")

        def rows(ap, b):
            return ap[bass.ds(b * P, P), :]

        @block.sync
        def _(sp):
            def step(b, u, k):
                if not before(b, U):
                    sp.wait_ge(made, b - (U - 1))
                settle(sp, C)
                g = sp.value_load(last[0:1, bass.ds(b, 1)], min_val=0, max_val=agg.shape[0] - 1)
                sp.dma_start(ag[u][:, :], agg_rows[bass.ds(g * P, P), :]).then_inc(ld[u], 16)
                sp.dma_start(xs[u][:, :], rows(x2, b)).then_inc(ld[u], 16)
                sp.dma_start(ks[u][:, 0:MIXED], rows(mixed, b)).then_inc(ld[u], 16)
            loop_blocks(sp, nb, step)

        @block.vector
        def _(dve):
            def add_skip(b, u, k):
                dve.wait_ge(mmm, b + 1)
                if not before(b, 2):
                    dve.wait_ge(gated, b - 1)
                nc.vector.tensor_tensor(pre[u % 2][:, :].rearrange("p (a f) -> p a f", a=2),
                                        ops[u % 2][:, 0:192].rearrange("p (a f) -> p a f", a=2),
                                        ks[u][:, :].rearrange("p (a f) -> p a f", a=2)[:, :, 0:96], ALU.add).then_inc(pre_ready, 1)

            def close(b, u, k):
                v = u % 2
                dve.wait_ge(sig, b + 1)
                if not before(b, 2):
                    dve.wait_ge(made, b - 1)
                nc.vector.tensor_tensor(tm[v][:, 0:MS], pre[v][:, 0:MS], sg[v][:, 0:MS], ALU.mult)
                nc.vector.tensor_tensor(tm[v][:, MS:D].rearrange("p (c f) -> p c f", c=3),
                                        pre[v][:, 96:192].rearrange("p (c f) -> p c f", c=3),
                                        bcast(sg[v][:, MS:96], 1, 3), ALU.mult).then_inc(gated, 1)
                dve.wait_ge(gated, b + 1)
                if not before(b, U):
                    dve.wait_ge(stx[u], k * 16)
                nc.vector.tensor_tensor(ot[u][:, :], tm[v][:, :], xs[u][:, :], ALU.add).then_inc(made, 1)

            def step(b, u, k):
                add_skip(b, u, k)
                if not before(b, 1):
                    close(*shifted(b, u, k, -1, U))
            loop_blocks(dve, nb, step)
            close(nb - 1, (nb - 1) % U, (nb - 1) // U)

        @block.scalar
        def _(act):
            def take_sums(b, u, k):
                v = u % 2
                act.wait_ge(mtr, b + 1)
                if not before(b, 2):
                    act.wait_ge(mmm, b - 1)
                nc.scalar.copy(mT[v][0:96, 0:P], mps[v][0:96, 0:P])
                nc.scalar.copy(mT[v][:, P:4 * P], mps[v][:, P:4 * P]).then_inc(mev, 1)

            def step(b, u, k):
                if not is_last(b, nb):
                    take_sums(*shifted(b, u, k, 1, U))
                act.wait_ge(pre_ready, b + 1)
                if not before(b, 2):
                    act.wait_ge(gated, b - 1)
                nc.scalar.activation(sg[u % 2][:, :], pre[u % 2][:, 0:96], ACT.Sigmoid).then_inc(sig, 1)
            take_sums(0, 0, 0)
            loop_blocks(act, nb, step)

        @block.tensor
        def _(pe):
            def transpose_sums(b, u, k):
                v = u % 2
                pe.wait_ge(ld[u], k * 48 + 48)
                if not before(b, 2):
                    pe.wait_ge(mev, b - 1)
                nc.tensor.transpose(mps[v][0:96, 0:P], ag[u][:, 0:96], C["ident"][:, :])
                for c in range(3):
                    last_ = nc.tensor.transpose(mps[v][:, (c + 1) * P:(c + 2) * P], ag[u][:, 96 + c * 128:96 + (c + 1) * 128],
                                                C["ident"][:, :])
                last_.then_inc(mtr, 1)

            def step(b, u, k):
                v = u % 2
                if not is_last(b, nb):
                    transpose_sums(*shifted(b, u, k, 1, U))
                pe.wait_ge(mev, b + 1)
                if not before(b, 2):
                    pe.wait_ge(pre_ready, b - 1)
                nc.tensor.matmul(ops[v][:, 0:96], mT[v][0:96, 0:P], Wn["outs"][0:96, :], start=True, stop=True)
                for c in range(3):
                    last_ = nc.tensor.matmul(ops[v][:, 96 + c * MV:96 + (c + 1) * MV], mT[v][:, (c + 1) * P:(c + 2) * P],
                                             Wn["outv"][:, :], start=True, stop=True)
                last_.then_inc(mmm, 1)
            transpose_sums(0, 0, 0)
            loop_blocks(pe, nb, step)

        @block.gpsimd
        def _(pool):
            def step(b, u, k):
                pool.wait_ge(made, b + 1)
                settle(pool, C)
                pool.dma_start(rows(out, b), ot[u][:, :]).then_inc(stx[u], 16)
            loop_blocks(pool, nb, step)
            for u in range(U):
                pool.wait_ge(stx[u], 16 * times(u, nb))


def before(index, n):
    return isinstance(index, int) and index < n


def group_pair(ap, first):
    return ap[bass.ds(first, G), :].rearrange("(p j) w -> p j w", p=P)


def edges_gnn0(nc, C, unsorted, attr0, attr0_a, ids_a, x1, table, row0, Wn, ng, agg):
    U = UNROLL
    n = ng // 2
    ctx = ExitStack()
    with ctx:
        a = Names(nc, ctx, "edge0")
        attr = [a.sb(f"attr{i}", [P, TILES, ATTR0]) for i in range(U)]
        ids = [a.sb(f"ids{i}", [P, TILES, 3], I32) for i in range(U)]
        src = [a.sb(f"src{i}", [P, TILES], I32) for i in range(U)]
        gath = [a.sb(f"gath{i}", [P, TILES, D]) for i in range(U)]
        eT, hid = a.sb("eT", [TILES * ATTR0, P]), a.sb("hid", [P, TILES * P])
        es = [a.sb(f"es{i}", [P, TILES, 96]) for i in range(2)]
        hot = [a.sb(f"hot{i}", [P, TILES, P]) for i in range(2)]
        msg = [a.sb(f"msg{i}", [P, TILES, AGG0]) for i in range(2)]
        local = a.sb("local", [P, TILES])
        ws = [a.sb(f"ws{i}", [P, TILES, MS]) for i in range(2)]
        dots = a.sb("dots", [P, TILES, 3, MV])
        dot = a.sb("dot", [P, TILES, MV])
        acc = [a.sb(f"acc{i}", [P, 2, AGG0]) for i in range(U)]
        tps, hps = a.ps("t"), a.ps("h")
        wps = [a.ps(f"w{i}", TILES * W_STRIDE) for i in range(2)]
        aps = [a.ps(f"a{i}") for i in range(2)]
        in_ = [a.sem(f"in{i}") for i in range(U)]
        gath_in = [a.sem(f"gath_in{i}") for i in range(U)]
        acc_out = [a.sem(f"acc_out{i}") for i in range(U)]
        tr, ev, fc1, act1, w_ready, es_ready = (a.sem(s) for s in ("tr", "ev", "fc1", "act1", "w_ready", "es_ready"))
        ws_ready, spread_ready = a.sem("ws_ready"), a.sem("spread_ready")
        src_ready, msg_ready, summed, acc_ready, ch, zeroed = (
            a.sem(s) for s in ("src_ready", "msg_ready", "summed", "acc_ready", "chain", "zeroed"))
        block = ctx.enter_context(nc.Block())

        @block.sync
        def _(sp):
            def store(i, u):
                sp.wait_ge(acc_ready, i * 2 + 2)
                settle(sp, C)
                sp.dma_start(agg[bass.ds(i * 2, 2), :, :].rearrange("g p f -> p g f"), acc[u][:, :, :]).then_inc(acc_out[u], 16)

            def run(attributes):
                def step(i, u, k):
                    if not before(i, 5):
                        store(i - 5, (u - 5) % U)
                    if not before(i, U):
                        sp.wait_ge(msg_ready, i - (U - 1))
                        sp.wait_ge(spread_ready, i - (U - 1))
                        settle(sp, C)
                    for h in range(2):
                        r = sp.value_load(row0[0:1, bass.ds(i * 2 + h, 1)], min_val=0, max_val=attributes.shape[0] - G)
                        sp.dma_start(ids[u][:, 2 * h:2 * h + 2, :], group_pair(ids_a, r)).then_inc(in_[u], 16)
                        sp.dma_start(attr[u][:, 2 * h:2 * h + 2, :], group_pair(attributes, r)).then_inc(in_[u], 16)
                loop_pairs(sp, n, step, peel=2, step=U)
            either(sp, unsorted, lambda: run(attr0_a), lambda: run(attr0))
            for i in range(n - 5, n):
                store(i, i % U)
            for u in range(U):
                sp.wait_ge(acc_out[u], 16 * (n // U))

        @block.gpsimd
        def _(pool):
            def step(i, u, k):
                if not before(i, U):
                    pool.wait_ge(msg_ready, i - (U - 1))
                pool.wait_ge(src_ready, i + 1)
                settle(pool, C)
                for j in range(TILES):
                    pool.indirect_dma_start(
                        out=gath[u][:, j, :], out_offset=None, in_=x1,
                        in_offset=bass.IndirectOffsetOnAxis(ap=src[u][:, j:j + 1], axis=0)).then_inc(gath_in[u], 16)
            loop_pairs(pool, n, step, peel=1, step=U)

        @block.scalar
        def _(act):
            def scale(i, u):
                act.wait_ge(w_ready, i + 1)
                if not before(i, 2):
                    act.wait_ge(msg_ready, i - 1)
                for j in range(TILES):
                    last_ = nc.scalar.activation(es[u % 2][:, j, :], wps[u % 2][:, j * W_STRIDE:j * W_STRIDE + 96], ACT.Copy,
                                                 scale=attr[u][:, j, EA4:EA4 + 1])
                last_.then_inc(es_ready, 1)

            def spread(i, u, half):
                act.wait_ge(ws_ready, i + 1)
                if not before(i, 2):
                    act.wait_ge(summed, i * 2 - 2)
                for j in (2 * half, 2 * half + 1):
                    for c in range(SPREAD0):
                        last_ = nc.scalar.activation(msg[u % 2][:, j, 96 * (c + 1):96 * (c + 1) + MS], ws[u % 2][:, j, :], ACT.Copy,
                                                     scale=attr[u][:, j, EA4 + 1 + c:EA4 + 2 + c])
                if half:
                    last_.then_inc(spread_ready, 1)

            def step(i, u, k):
                act.wait_ge(in_[u], k * 64 + 64)
                if not before(i, U):
                    act.wait_ge(gath_in[u], k * (16 * TILES))
                nc.scalar.copy(src[u][:, :], ids[u][:, :, SRC]).then_inc(src_ready, 1)
                act.wait_ge(tr, i + 1)
                if not before(i, 1):
                    act.wait_ge(fc1, i)
                nc.scalar.copy(eT[:, :], tps[0:TILES * ATTR0, 0:P]).then_inc(ev, 1)
                if not before(i, 1):
                    scale(i - 1, (u - 1) % U)
                    spread(i - 1, (u - 1) % U, 0)
                act.wait_ge(fc1, i + 1)
                if not before(i, 1):
                    act.wait_ge(w_ready, i)
                nc.scalar.activation(hid[0:H0, :], hps[0:H0, :], ACT.Silu).then_inc(act1, 1)
                if not before(i, 1):
                    spread(i - 1, (u - 1) % U, 1)
            loop_pairs(act, n, step, peel=1, step=U)
            scale(n - 1, (n - 1) % U)
            for half in range(2):
                spread(n - 1, (n - 1) % U, half)

        @block.vector
        def _(dve):
            nc.vector.memset(acc[U - 1][:, :, :], 0.0).then_inc(zeroed, 1)
            dve.wait_ge(zeroed, 1)

            def add_group(i, u, k, h):
                if h == 0 and not before(i, U):
                    dve.wait_ge(acc_out[u], k * 16)
                dve.wait_ge(summed, i * 2 + h + 1)
                if not (before(i, 1) and h == 0):
                    dve.wait_ge(acc_ready, i * 2 + h)
                prev = acc[u][:, 0, :] if h else acc[(u - 1) % U][:, 1, :]
                nc.vector.scalar_tensor_tensor(acc[u][:, h, :], prev, table[:, 2, bass.ds(i * 2 + h, 1)],
                                               aps[h][:, 0:AGG0], ALU.mult, ALU.add).then_inc(acc_ready, 1)

            def step(i, u, k):
                v = u % 2
                CH = 4
                dve.wait_ge(in_[u], k * 64 + 64)
                if not before(i, 1):
                    dve.wait_ge(ch, i * CH)
                nc.vector.tensor_tensor(local[:, :].rearrange("p (h j) -> p h j", h=2),
                                        ids[u][:, :, DST].rearrange("p (h j) -> p h j", h=2),
                                        bcast(table[:, 1, bass.ds(i * 2, 2)], 2, 2), ALU.subtract).then_inc(ch, 1)
                if not before(i, 2):
                    add_group(*shifted(i, u, k, -2), 0)
                dve.wait_ge(ch, i * CH + 1)
                if not before(i, 2):
                    dve.wait_ge(summed, i * 2 - 2)
                nc.vector.tensor_tensor(hot[v][:, :, :], bcast(C["node_ramp"][:, :], 1, TILES), bcast(local[:, :], 2, P),
                                        ALU.is_equal)
                if not before(i, 2):
                    add_group(*shifted(i, u, k, -2), 1)
                dve.wait_ge(gath_in[u], (k + 1) * (16 * TILES))
                gs = gath[u][:, :, 0:MS]
                gv = gath[u][:, :, MS:D].rearrange("p j (c f) -> p j c f", c=3)
                ev_ = attr[u][:, :, EA4 + 1:EA4 + 4]
                w = wps[v][:, :].rearrange("p (j f) -> p j f", j=TILES)
                m = msg[v]
                mv_ = m[:, :, 96:AGG0].rearrange("p j (c f) -> p j c f", c=3)
                nc.vector.tensor_tensor(dots[:, :, :, :], gv, bcast(ev_, 3, MV), ALU.mult).then_inc(ch, 1)
                dve.wait_ge(es_ready, i + 1)
                if not before(i, 2):
                    dve.wait_ge(spread_ready, i - 1)
                nc.vector.tensor_tensor(ws[v][:, :, :], w[:, :, 96:160], gs, ALU.mult).then_inc(ws_ready, 1)
                dve.wait_ge(ch, i * CH + 2)
                nc.vector.tensor_tensor(dot[:, :, :], dots[:, :, 0, :], dots[:, :, 1, :], ALU.add).then_inc(ch, 1)
                nc.vector.tensor_tensor(m[:, :, 0:MS], es[v][:, :, 0:MS], gs, ALU.mult)
                dve.wait_ge(ch, i * CH + 3)
                nc.vector.tensor_tensor(dot[:, :, :], dot[:, :, :], dots[:, :, 2, :], ALU.add).then_inc(ch, 1)
                dve.wait_ge(ws_ready, i + 1)
                nc.vector.tensor_tensor(mv_[:, :, SPREAD0:3, 0:MS], bcast(ws[v][:, :, :], 2, 3 - SPREAD0),
                                        bcast(ev_[:, :, SPREAD0:3], 3, MS), ALU.mult)
                dve.wait_ge(ch, i * CH + 4)
                nc.vector.tensor_tensor(m[:, :, MS:96], w[:, :, 160:192], dot[:, :, :], ALU.mult)
                nc.vector.tensor_tensor(mv_[:, :, :, MS:96], bcast(es[v][:, :, MS:96], 2, 3), gv, ALU.mult).then_inc(msg_ready, 1)
            loop_pairs(dve, n, step, peel=1, step=U)
            for i in (n - 2, n - 1):
                for h in range(2):
                    add_group(i, i % U, n // U - 1, h)

        @block.tensor
        def _(pe):
            def group_sum(i, v, h):
                if h == 0:
                    pe.wait_ge(msg_ready, i + 1)
                    pe.wait_ge(spread_ready, i + 1)
                if not before(i, 1):
                    pe.wait_ge(acc_ready, i * 2 + (h - 1))
                for j in range(2):
                    last_ = nc.tensor.matmul(aps[h][:, 0:AGG0], hot[v][:, 2 * h + j, :], msg[v][:, 2 * h + j, :],
                                             start=j == 0, stop=j == 1)
                last_.then_inc(summed, 1)

            def step(i, u, k):
                v = u % 2
                pe.wait_ge(in_[u], k * 64 + 64)
                if not before(i, 1):
                    pe.wait_ge(ev, i)
                pe.sem_inc(C["settled"], 1)
                nc.tensor.transpose(tps[0:TILES * ATTR0, 0:P], attr[u][:, :, :].rearrange("p j w -> p (j w)"),
                                    C["ident"][:, :]).then_inc(tr, 1)
                if not before(i, 2):
                    group_sum(i - 2, v, 0)
                pe.wait_ge(ev, i + 1)
                if not before(i, 1):
                    pe.wait_ge(act1, i)
                settle(pe, C)
                for j in range(TILES):
                    last_ = nc.tensor.matmul(hps[0:H0, j * P:(j + 1) * P], Wn["fc1_0"][0:TILES * ATTR0, j * H0:(j + 1) * H0],
                                             eT[:, :], start=True, stop=True)
                last_.then_inc(fc1, 1)
                if not before(i, 2):
                    group_sum(i - 2, v, 1)
                pe.wait_ge(act1, i + 1)
                for j in range(TILES):
                    last_ = nc.tensor.matmul(wps[v][:, j * W_STRIDE:j * W_STRIDE + WN0], hid[0:H0, j * P:(j + 1) * P],
                                             Wn["fc2_0"][0:H0, :], start=True, stop=True)
                last_.then_inc(w_ready, 1)
            loop_pairs(pe, n, step, peel=1, step=U)
            for i in (n - 2, n - 1):
                for h in range(2):
                    group_sum(i, i % 2, h)


def to_source_order(nc, C, unsorted, attr1, attr1_a, ids_a, mixed, table, row0, node0, Wn, ng, n_edges, rows_b):
    U = LONG_UNROLL
    n = ng // 2
    ctx = ExitStack()
    with ctx:
        a = Names(nc, ctx, "route")
        row = [a.sb(f"row{i}", [P, TILES, ROW_B]) for i in range(U)]
        attr = [a.sb(f"attr{i}", [P, TILES, ATTR1]) for i in range(U)]
        ids = [a.sb(f"ids{i}", [P, TILES, 3], I32) for i in range(U)]
        node = [a.sb(f"node{i}", [P, 2, D]) for i in range(U)]
        at = [a.sb(f"at{i}", [P, TILES], I32) for i in range(U)]
        hot = [a.sb(f"hot{i}", [P, TILES, P]) for i in range(2)]
        hotT = [a.sb(f"hotT{i}", [P, TILES * P]) for i in range(2)]
        feat = [a.sb(f"feat{i}", [P, TILES * 64]) for i in range(2)]
        fT = a.sb("fT", [P, 2 * P])
        local, low, high = a.sb("local", [P, TILES]), a.sb("low", [P, TILES]), a.sb("high", [P, TILES])
        squares, n2, rn = a.sb("squares", [P, TILES, 3]), a.sb("n2", [P, TILES]), a.sb("rn", [P, TILES])
        n1 = [a.sb(f"n1_{i}", [P, TILES]) for i in range(2)]
        pad = a.sb("pad", [G // 8, 8 * ROW_B])
        tps = [a.ps(f"t{i}") for i in range(2)]
        nps = [a.ps(f"n{i}", TILES * W_STRIDE) for i in range(2)]
        fps = [a.ps(f"f{i}") for i in range(2)]
        in_ = [a.sem(f"in{i}") for i in range(U)]
        out_done = [a.sem(f"out_done{i}") for i in range(U)]
        hot_ready, tr, ev, picked, filled, at_ready, ch, padded, pad_out = (
            a.sem(s) for s in ("hot_ready", "tr", "ev", "picked", "filled", "at_ready", "chain", "padded", "pad_out"))
        feat_ready, ftr, fev, fc1, hid_ready = (a.sem(s) for s in ("feat_ready", "ftr", "fev", "fc1", "hid_ready"))
        squared, n2_ready, root, inverse, scaled, sh_ready = (
            a.sem(s) for s in ("squared", "n2_ready", "root", "inverse", "scaled", "sh_ready"))
        block = ctx.enter_context(nc.Block())

        def load(eng, attributes, h, i, u, k):
            if not before(i, U):
                eng.wait_ge(out_done[u], k * (16 * TILES))
                settle(eng, C)
            r = eng.value_load(row0[0:1, bass.ds(i * 2 + h, 1)], min_val=0, max_val=attributes.shape[0] - G)
            eng.dma_start(ids[u][:, 2 * h:2 * h + 2, :], group_pair(ids_a, r)).then_inc(in_[u], 16)
            eng.dma_start(attr[u][:, 2 * h:2 * h + 2, :], group_pair(attributes, r)).then_inc(in_[u], 16)
            b = eng.value_load(node0[0:1, bass.ds(i * 2 + h, 1)], min_val=0, max_val=mixed.shape[0] - P)
            eng.dma_start(node[u][:, h, :], mixed[bass.ds(b, P), 96:96 + D]).then_inc(in_[u], 16)

        @block.sync
        def _(sp):
            sp.wait_ge(padded, 2)
            sp.dma_start(rows_b[n_edges:n_edges + G, :].rearrange("(p j) w -> p (j w)", j=8), pad[:, :]).then_inc(pad_out, 16)

            def run(attributes):
                loop_pairs(sp, n, lambda i, u, k: load(sp, attributes, 0, i, u, k), peel=1, step=U)
            either(sp, unsorted, lambda: run(attr1_a), lambda: run(attr1))
            sp.wait_ge(pad_out, 16)

        @block.vector
        def _(dve):
            nc.vector.memset(pad[:, :], 1.0).then_inc(padded, 1)
            dve.wait_ge(padded, 1)
            nc.vector.memset(pad[:, :].rearrange("p (j w) -> p j w", j=8)[:, :, B_SRC].bitcast(I32), C["blocks"] * P + P)\
                .then_inc(padded, 1)

            def inverse_length(i, u, k):
                dve.wait_ge(root, i + 1)
                if not before(i, 1):
                    dve.wait_ge(scaled, i)
                nc.vector.reciprocal(rn[:, :], n1[u % 2][:, :]).then_inc(inverse, 1)

            def direction(i, u, k):
                dve.wait_ge(inverse, i + 1)
                nc.vector.tensor_tensor(row[u][:, :, B_SH:B_SH + 3], attr[u][:, :, EA3:EA3 + 3], bcast(rn[:, :], 2, 3), ALU.mult)\
                    .then_inc(scaled, 1)

            def wrap(i, u, k):
                dve.wait_ge(scaled, i + 1)
                nc.vector.tensor_copy(row[u][:, :, B_SH + 3:B_SH + 5], row[u][:, :, B_SH:B_SH + 2]).then_inc(sh_ready, 1)

            def fill(i, u, k):
                dve.wait_ge(picked, i + 1)
                nc.vector.tensor_copy(row[u][:, :, B_NODE:ROW_B],
                                      nps[u % 2][:, :].rearrange("p (j f) -> p j f", j=TILES)[:, :, 0:D]).then_inc(filled, 1)

            def take_transposed(i, u, k):
                v = u % 2
                dve.wait_ge(tr, i + 1)
                if not before(i, 2):
                    dve.wait_ge(picked, i - 1)
                nc.vector.tensor_copy(hotT[v][:, :], tps[v][:, :]).then_inc(ev, 1)
                dve.wait_ge(ftr, i + 1)
                if not before(i, 1):
                    dve.wait_ge(fc1, i)
                nc.vector.tensor_copy(fT[:, :], fps[v][:, 0:2 * P]).then_inc(fev, 1)

            def step(i, u, k):
                CH = 4
                dve.wait_ge(in_[u], k * 96 + 96)
                if not before(i, 1):
                    dve.wait_ge(ch, i * CH)
                    dve.wait_ge(at_ready, i)
                nc.vector.tensor_tensor(local[:, :].rearrange("p (h j) -> p h j", h=2),
                                        ids[u][:, :, DST].rearrange("p (h j) -> p h j", h=2),
                                        bcast(table[:, 1, bass.ds(i * 2, 2)], 2, 2), ALU.subtract).then_inc(ch, 1)
                if not before(i, 1):
                    dve.wait_ge(n2_ready, i)
                    dve.wait_ge(root, i)
                nc.vector.tensor_tensor(squares[:, :, :], attr[u][:, :, EA3:EA3 + 3], attr[u][:, :, EA3:EA3 + 3], ALU.mult)\
                    .then_inc(squared, 1)
                dve.wait_ge(ch, i * CH + 1)
                if not before(i, 2):
                    dve.wait_ge(tr, i - 1)
                nc.vector.tensor_tensor(hot[u % 2][:, :, :], bcast(C["node_ramp"][:, :], 1, TILES), bcast(local[:, :], 2, P),
                                        ALU.is_equal).then_inc(hot_ready, 1)
                dve.wait_ge(squared, i + 1)
                nc.vector.tensor_reduce(n2[:, :], squares[:, :, :], AXX, ALU.add).then_inc(n2_ready, 1)
                nc.vector.tensor_scalar(low[:, :], local[:, :], 0.0, float(OUT_OF_BOUNDS), ALU.is_lt, ALU.mult).then_inc(ch, 1)
                nc.vector.tensor_scalar(high[:, :], local[:, :], float(P), float(OUT_OF_BOUNDS), ALU.is_ge, ALU.mult).then_inc(ch, 1)
                if not before(i, 1):
                    inverse_length(*shifted(i, u, k, -1, U))
                dve.wait_ge(ch, i * CH + 3)
                nc.vector.tensor_tensor(high[:, :], high[:, :], low[:, :], ALU.add).then_inc(ch, 1)
                if not before(i, 1):
                    direction(*shifted(i, u, k, -1, U))
                    fill(*shifted(i, u, k, -1, U))
                    wrap(*shifted(i, u, k, -1, U))
                dve.wait_ge(ch, i * CH + 4)
                if not before(i, U):
                    dve.wait_ge(out_done[u], k * (16 * TILES))
                nc.vector.tensor_tensor(at[u][:, :], high[:, :], ids[u][:, :, PLACE], ALU.add).then_inc(at_ready, 1)
                take_transposed(i, u, k)
            loop_pairs(dve, n, step, peel=1, step=U)
            for finish in (inverse_length, direction, fill, wrap):
                finish(n - 1, U - 1, n // U - 1)

        @block.scalar
        def _(act):
            def prepare(i, u, k):
                act.wait_ge(in_[u], k * 96 + 96)
                if not before(i, 2):
                    act.wait_ge(ftr, i - 1)
                nc.scalar.copy(feat[u % 2][:, :].rearrange("p (j f) -> p j f", j=TILES), attr[u][:, :, EA64:EA64 + 64])\
                    .then_inc(feat_ready, 1)
                nc.scalar.copy(row[u][:, :, B_SRC].bitcast(I32), ids[u][:, :, SRC])

            def hidden(i, u, k):
                act.wait_ge(fc1, i + 1)
                nc.scalar.activation(row[u][:, :, B_HID:B_HID + 64],
                                     fps[u % 2][:, 2 * P:4 * P].rearrange("p (j f) -> p j f", j=TILES), ACT.Relu)\
                    .then_inc(hid_ready, 1)

            def run(attributes):
                def step(i, u, k):
                    if not (isinstance(i, int) and i >= n - 3):
                        load(act, attributes, 1, *shifted(i, u, k, 3, U))
                    if not before(i, 1):
                        hidden(*shifted(i, u, k, -1, U))
                    if not (isinstance(i, int) and i == n - 1):
                        prepare(*shifted(i, u, k, 1, U))
                    act.wait_ge(n2_ready, i + 1)
                    if not before(i, 2):
                        act.wait_ge(inverse, i - 1)
                    nc.scalar.activation(n1[u % 2][:, :], n2[:, :], ACT.Sqrt, scale=1 / 3.0).then_inc(root, 1)
                for i in range(3):
                    load(act, attributes, 1, i, i, 0)
                prepare(0, 0, 0)
                loop_pairs(act, n - U, step, peel=1, step=U)
                for u in range(U):
                    step(n - U + u, u, n // U - 1)
                hidden(n - 1, U - 1, n // U - 1)
            either(act, unsorted, lambda: run(attr1_a), lambda: run(attr1))

        @block.tensor
        def _(pe):
            def step(i, u, k):
                v = u % 2
                pe.wait_ge(hot_ready, i + 1)
                if not before(i, 2):
                    pe.wait_ge(ev, i - 1)
                for j in range(TILES):
                    last_ = nc.tensor.transpose(tps[v][:, j * P:(j + 1) * P], hot[v][:, j, :], C["ident"][:, :])
                last_.then_inc(tr, 1)
                pe.wait_ge(feat_ready, i + 1)
                if not before(i, 2):
                    pe.wait_ge(hid_ready, i - 1)
                settle(pe, C)
                for j in range(2):
                    last_ = nc.tensor.transpose(fps[v][:, j * P:(j + 1) * P], feat[v][:, j * P:(j + 1) * P], C["ident"][:, :])
                last_.then_inc(ftr, 1)
                pe.wait_ge(ev, i + 1)
                if not before(i, 2):
                    pe.wait_ge(filled, i - 1)
                pe.wait_ge(in_[u], k * 96 + 96)
                for j in range(TILES):
                    last_ = nc.tensor.matmul(nps[v][:, j * W_STRIDE:j * W_STRIDE + D], hotT[v][:, j * P:(j + 1) * P],
                                             node[u][:, j // 2, :], start=True, stop=True)
                last_.then_inc(picked, 1)
                pe.wait_ge(fev, i + 1)
                for j in range(2):
                    last_ = nc.tensor.matmul(fps[v][:, (2 + j) * P:(3 + j) * P], fT[:, j * P:(j + 1) * P], Wn["fc1_1"][:, :],
                                             start=True, stop=True)
                last_.then_inc(fc1, 1)
            loop_pairs(pe, n, step, peel=1, step=U)

        @block.gpsimd
        def _(pool):
            bound = rows_b.shape[0] - 1

            def step(i, u, k):
                pool.wait_ge(filled, i + 1)
                pool.wait_ge(sh_ready, i + 1)
                pool.wait_ge(hid_ready, i + 1)
                pool.wait_ge(at_ready, i + 1)
                settle(pool, C)
                for j in range(TILES):
                    pool.indirect_dma_start(
                        out=rows_b, out_offset=bass.IndirectOffsetOnAxis(ap=at[u][:, j:j + 1], axis=0),
                        in_=row[u][:, j, :], in_offset=None, bounds_check=bound, oob_is_err=False).then_inc(out_done[u], 16)
            loop_pairs(pool, n, step, peel=1, step=U)
            for u in range(U):
                pool.wait_ge(out_done[u], 16 * TILES * (n // U))


def edges_gnn1(nc, C, rows_b, table, row0, Wn, ng, agg):
    U = UNROLL
    n = ng // 2
    ctx = ExitStack()
    with ctx:
        a = Names(nc, ctx, "edge1")
        row = [a.sb(f"row{i}", [P, TILES, ROW_B]) for i in range(U)]
        feat = [a.sb(f"feat{i}", [P, TILES * 64]) for i in range(2)]
        hid = a.sb("hid", [P, 2 * P])
        hot = [a.sb(f"hot{i}", [P, TILES, P]) for i in range(2)]
        msg = [a.sb(f"msg{i}", [P, TILES, AGG1]) for i in range(2)]
        local = [a.sb(f"local{i}", [P, TILES]) for i in range(2)]
        ws = [a.sb(f"ws{i}", [P, TILES, MS]) for i in range(2)]
        dots, part = a.sb("dots", [P, TILES, 3, MV]), a.sb("part", [P, TILES, MV])
        dot = [a.sb(f"dot{i}", [P, TILES, MV]) for i in range(2)]
        wv = [a.sb(f"wv{i}", [P, TILES, 5, MV]) for i in range(2)]
        left, right = a.sb("left", [P, TILES, 3, MV]), a.sb("right", [P, TILES, 3, MV])
        acc = [a.sb(f"acc{i}", [P, 2, AGG1]) for i in range(U)]
        tps = a.ps("t")
        wps = [a.ps(f"w{i}", TILES * W_STRIDE) for i in range(2)]
        aps = [a.ps(f"a{i}") for i in range(2)]
        in_ = [a.sem(f"in{i}") for i in range(U)]
        acc_out = [a.sem(f"acc_out{i}") for i in range(U)]
        feat_ready, tr, hid_ready, w_ready, local_ready = (
            a.sem(s) for s in ("feat_ready", "tr", "hid_ready", "w_ready", "local_ready"))
        dots_ready, part_ready, dot_ready, wv_ready, both_ready, crossed = (
            a.sem(s) for s in ("dots_ready", "part_ready", "dot_ready", "wv_ready", "both_ready", "crossed"))
        ws_ready, spread_ready, msg_ready, summed, acc_ready, zeroed = (
            a.sem(s) for s in ("ws_ready", "spread_ready", "msg_ready", "summed", "acc_ready", "zeroed"))
        block = ctx.enter_context(nc.Block())

        def direction(u, lo, hi):
            return row[u][:, :, B_SH + lo:B_SH + hi]

        def vectors(u):
            return row[u][:, :, B_NODE + MS:ROW_B].rearrange("p j (c f) -> p j c f", c=3)

        def vector_message(v):
            return msg[v][:, :, 96:AGG1].rearrange("p j (c f) -> p j c f", c=3)

        @block.sync
        def _(sp):
            def store(i, u):
                sp.wait_ge(acc_ready, i * 2 + 2)
                settle(sp, C)
                sp.dma_start(agg[bass.ds(i * 2, 2), :, :].rearrange("g p f -> p g f"), acc[u][:, :, :]).then_inc(acc_out[u], 16)

            def step(i, u, k):
                if not before(i, 5):
                    store(i - 5, (u - 5) % U)
                if not before(i, U):
                    sp.wait_ge(msg_ready, i - (U - 1))
                    sp.wait_ge(crossed, i - (U - 1))
                    sp.wait_ge(spread_ready, i - (U - 1))
                    settle(sp, C)
                for h in range(2):
                    r = sp.value_load(row0[0:1, bass.ds(i * 2 + h, 1)], min_val=0, max_val=rows_b.shape[0] - G)
                    sp.dma_start(row[u][:, 2 * h:2 * h + 2, :], group_pair(rows_b, r)).then_inc(in_[u], 16)
            loop_pairs(sp, n, step, peel=2, step=U)
            for i in range(n - 5, n):
                store(i, i % U)
            for u in range(U):
                sp.wait_ge(acc_out[u], 16 * (n // U))

        @block.scalar
        def _(act):
            def features(i, u, k):
                act.wait_ge(in_[u], k * 32 + 32)
                if not before(i, 2):
                    act.wait_ge(tr, i - 1)
                nc.scalar.copy(feat[u % 2][:, :].rearrange("p (j f) -> p j f", j=TILES), row[u][:, :, B_HID:B_HID + 64])\
                    .then_inc(feat_ready, 1)

            def spread(i, u, k):
                act.wait_ge(ws_ready, i + 1)
                if not before(i, 2):
                    act.wait_ge(summed, i * 2 - 2)
                for j in range(TILES):
                    for c in range(SPREAD1):
                        last_ = nc.scalar.activation(vector_message(u % 2)[:, j, c, 0:MS], ws[u % 2][:, j, :], ACT.Copy,
                                                     scale=direction(u, c, c + 1)[:, j, :])
                last_.then_inc(spread_ready, 1)

            def step(i, u, k):
                act.wait_ge(tr, i + 1)
                if not before(i, 1):
                    act.wait_ge(w_ready, i)
                nc.scalar.copy(hid[:, :], tps[:, 0:2 * P]).then_inc(hid_ready, 1)
                if not (isinstance(i, int) and i == n - 1):
                    features(*shifted(i, u, k, 1))
                if not before(i, 1):
                    spread(*shifted(i, u, k, -1))
            features(0, 0, 0)
            loop_pairs(act, n - U, step, peel=1, step=U)
            for u in range(U):
                step(n - U + u, u, n // U - 1)
            spread(n - 1, U - 1, n // U - 1)

        @block.gpsimd
        def _(pool):
            def step(i, u, k):
                v = u % 2
                pool.wait_ge(in_[u], k * 32 + 32)
                if not before(i, 1):
                    pool.wait_ge(dot_ready, i)
                settle(pool, C)
                nc.gpsimd.tensor_tensor(dots[:, :, :, :], vectors(u), bcast(direction(u, 0, 3), 3, MV), ALU.mult).then_inc(dots_ready, 1)
                pool.wait_ge(dots_ready, i + 1)
                settle(pool, C)
                nc.gpsimd.tensor_tensor(part[:, :, :], dots[:, :, 0, :], dots[:, :, 1, :], ALU.add).then_inc(part_ready, 1)
                if not before(i, 2):
                    pool.wait_ge(msg_ready, i - 1)
                pool.wait_ge(part_ready, i + 1)
                settle(pool, C)
                nc.gpsimd.tensor_tensor(dot[v][:, :, :], part[:, :, :], dots[:, :, 2, :], ALU.add).then_inc(dot_ready, 1)
                pool.wait_ge(wv_ready, i + 1)
                if not before(i, 1):
                    pool.wait_ge(crossed, i)
                settle(pool, C)
                nc.gpsimd.tensor_tensor(left[:, :, :, :], wv[v][:, :, 1:4, :], bcast(direction(u, 2, 5), 3, MV), ALU.mult)
                nc.gpsimd.tensor_tensor(right[:, :, :, :], wv[v][:, :, 2:5, :], bcast(direction(u, 1, 4), 3, MV), ALU.mult)\
                    .then_inc(both_ready, 1)
                if not before(i, 2):
                    pool.wait_ge(summed, i * 2 - 2)
                pool.wait_ge(both_ready, i + 1)
                nc.gpsimd.tensor_tensor(vector_message(v)[:, :, :, 96:128], left[:, :, :, :], right[:, :, :, :], ALU.subtract)\
                    .then_inc(crossed, 1)
            loop_pairs(pool, n, step, peel=1, step=U)

        @block.vector
        def _(dve):
            nc.vector.memset(acc[U - 1][:, :, :], 0.0).then_inc(zeroed, 1)
            dve.wait_ge(zeroed, 1)

            def add_group(i, u, k, h):
                if h == 0 and not before(i, U):
                    dve.wait_ge(acc_out[u], k * 16)
                dve.wait_ge(summed, i * 2 + h + 1)
                if not (before(i, 1) and h == 0):
                    dve.wait_ge(acc_ready, i * 2 + h)
                prev = acc[u][:, 0, :] if h else acc[(u - 1) % U][:, 1, :]
                nc.vector.scalar_tensor_tensor(acc[u][:, h, :], prev, table[:, 2, bass.ds(i * 2 + h, 1)],
                                               aps[h][:, 0:AGG1], ALU.mult, ALU.add).then_inc(acc_ready, 1)

            def find_local(i, u, k):
                dve.wait_ge(in_[u], k * 32 + 32)
                nc.vector.tensor_tensor(local[u % 2][:, :].rearrange("p (h j) -> p h j", h=2),
                                        row[u][:, :, B_SRC].bitcast(I32).rearrange("p (h j) -> p h j", h=2),
                                        bcast(table[:, 1, bass.ds(i * 2, 2)], 2, 2), ALU.subtract).then_inc(local_ready, 1)

            def step(i, u, k):
                v = u % 2
                xs = row[u][:, :, B_NODE:B_NODE + MS]
                xv = vectors(u)
                m, mv_ = msg[v], vector_message(v)

                def w(lo, width):
                    return wps[v][:, :].rearrange("p (j f) -> p j f", j=TILES)[:, :, lo:lo + width]
                if not before(i, 2):
                    add_group(*shifted(i, u, k, -2), 0)
                dve.wait_ge(local_ready, i + 1)
                if not before(i, 2):
                    dve.wait_ge(summed, i * 2 - 2)
                nc.vector.tensor_tensor(hot[v][:, :, :], bcast(C["node_ramp"][:, :], 1, TILES), bcast(local[v][:, :], 2, P),
                                        ALU.is_equal)
                if not before(i, 2):
                    add_group(*shifted(i, u, k, -2), 1)
                dve.wait_ge(w_ready, i + 1)
                if not before(i, 2):
                    dve.wait_ge(crossed, i - 1)
                nc.vector.tensor_tensor(wv[v][:, :, 0:3, :], bcast(w(192, MV), 2, 3), xv, ALU.mult)
                nc.vector.tensor_tensor(wv[v][:, :, 3:5, :], bcast(w(192, MV), 2, 2), xv[:, :, 0:2, :], ALU.mult).then_inc(wv_ready, 1)
                if not before(i, 2):
                    dve.wait_ge(spread_ready, i - 1)
                nc.vector.tensor_tensor(ws[v][:, :, :], w(MS, MS), xs, ALU.mult).then_inc(ws_ready, 1)
                nc.vector.tensor_tensor(m[:, :, 0:MS], w(0, MS), xs, ALU.mult)
                dve.wait_ge(ws_ready, i + 1)
                nc.vector.tensor_tensor(mv_[:, :, SPREAD1:3, 0:MS], bcast(ws[v][:, :, :], 2, 3 - SPREAD1),
                                        bcast(direction(u, SPREAD1, 3), 3, MS), ALU.mult)
                nc.vector.tensor_tensor(mv_[:, :, :, MS:96], bcast(w(128, MV), 2, 3), xv, ALU.mult)
                dve.wait_ge(dot_ready, i + 1)
                nc.vector.tensor_tensor(m[:, :, MS:96], w(160, MV), dot[v][:, :, :], ALU.mult).then_inc(msg_ready, 1)
                if not (isinstance(i, int) and i == n - 1):
                    find_local(*shifted(i, u, k, 1))
            find_local(0, 0, 0)
            loop_pairs(dve, n - U, step, peel=1, step=U)
            for u in range(U):
                step(n - U + u, u, n // U - 1)
            for i in (n - 2, n - 1):
                for h in range(2):
                    add_group(i, i % U, n // U - 1, h)

        @block.tensor
        def _(pe):
            def group_sum(i, v, h):
                if h == 0:
                    pe.wait_ge(msg_ready, i + 1)
                    pe.wait_ge(crossed, i + 1)
                    pe.wait_ge(spread_ready, i + 1)
                if not before(i, 1):
                    pe.wait_ge(acc_ready, i * 2 + (h - 1))
                for j in range(2):
                    last_ = nc.tensor.matmul(aps[h][:, 0:AGG1], hot[v][:, 2 * h + j, :], msg[v][:, 2 * h + j, :],
                                             start=j == 0, stop=j == 1)
                last_.then_inc(summed, 1)

            def step(i, u, k):
                v = u % 2
                pe.wait_ge(feat_ready, i + 1)
                if not before(i, 1):
                    pe.wait_ge(hid_ready, i)
                settle(pe, C)
                for j in range(2):
                    last_ = nc.tensor.transpose(tps[:, j * P:(j + 1) * P], feat[v][:, j * P:(j + 1) * P],
                                                C["ident"][:, :])
                last_.then_inc(tr, 1)
                if not before(i, 2):
                    for h in range(2):
                        group_sum(i - 2, v, h)
                pe.wait_ge(hid_ready, i + 1)
                for j in range(TILES):
                    last_ = nc.tensor.matmul(wps[v][:, j * W_STRIDE:j * W_STRIDE + WN1], hid[:, (j // 2) * P:(j // 2 + 1) * P],
                                             Wn["fc2_1"][:, (j % 2) * WN1:(j % 2 + 1) * WN1], start=True, stop=True)
                last_.then_inc(w_ready, 1)
            loop_pairs(pe, n, step, peel=1, step=U)
            for i in (n - 2, n - 1):
                for h in range(2):
                    group_sum(i, i % 2, h)


def table_ints(nc, stage, nb, table, row0, node0):
    ctx = ExitStack()
    with ctx:
        done = Names(nc, ctx, stage).sem("ints")
        block = ctx.enter_context(nc.Block())

        @block.vector
        def _(dve):
            nc.vector.tensor_copy(row0[:, :], table[0:1, 0, :]).then_inc(done, 1)
            nc.vector.tensor_scalar(node0[:, :], table[0:1, 1, :], float((nb - 1) * P), None, ALU.min).then_inc(done, 1)
            dve.wait_ge(done, 2)


def program(nc, n_nodes, n_edges, A, Wd, out):
    nb, cols = blocks_of(n_nodes), columns_of(n_edges)
    ng = groups_of(n_edges, nb)
    e_pad = P * cols

    def dram(name, shape, dt=F32):
        return nc.dram_tensor(name, shape, dt, kind="Internal").ap()
    pos_a, pos_b = dram("place_by_destination", [e_pad], I32), dram("place_by_source", [e_pad], I32)
    attr0_a, attr1_a = dram("attr0_by_destination", [e_pad, ATTR0]), dram("attr1_by_destination", [e_pad, ATTR1])
    ids_a, rows_b = dram("ids_by_destination", [e_pad, 3], I32), dram("rows_by_source", [e_pad, ROW_B])
    x1 = dram("x1", [(nb + 1) * P, D])
    base, x2, mixed = dram("base", [nb * P, D]), dram("x2", [nb * P, D]), dram("mixed", [nb * P, MIXED])
    agg0, agg1 = dram("agg0", [ng, P, AGG0]), dram("agg1", [ng, P, AGG1])
    meta = dram("meta", [2, 3, P * (-(-ng // P))])
    ctx = ExitStack()
    with ctx:
        a = Names(nc, ctx, "all")
        C = {"blocks": nb, "ident": a.sb("ident", [P, P]), "before": a.sb("before", [P, P], BF16),
             "not_before": a.sb("not_before", [P, P], BF16), "ones": a.sb("ones", [P, P], BF16), "ones_f32": a.sb("ones_f32", [P, P]),
             "block_ramp": a.sb("block_ramp", [P, nb], BF16), "node_ramp": a.sb("node_ramp", [P, P])}
        Wn = {k: a.sb(k, [P, n]) for k, n in (("s0", 4 * MS), ("v0", 4 * 96), ("fc1_0", TILES * H0), ("fc2_0", WN0), ("ps", 2 * MS),
                                             ("pv", 2 * MV), ("s1", MS + 96), ("v1", 192), ("fc1_1", P), ("fc2_1", 2 * WN1),
                                             ("outs", 96), ("outv", MV))}
        counts = [a.sb(f"count{i}", [P, nb]) for i in range(2)]
        total = a.sb("total", [P, 2 * RANKED * nb])
        unsorted = a.sb("unsorted", [1, 1], I32)
        tables = [a.sb(f"table{i}", [P, 3, ng]) for i in range(2)]
        row0 = [a.sb(f"row0_{i}", [1, ng], I32) for i in range(2)]
        node0 = [a.sb(f"node0_{i}", [1, ng], I32) for i in range(2)]
        last = [a.sb(f"last{i}", [1, nb], I32) for i in range(2)]
        C["settled"] = a.sem("settled")
        constants(nc, C)
        prepare_weights(nc, C, Wd, Wn)
        examine_destinations(nc, C, A["dst"], cols, nb, n_edges, counts[1], unsorted)
        count_edges(nc, C, "count_src", A["src"], cols, nb, total, counts[0])
        rank(nc, C, "rank_src", A["src"], cols, nb, pos_b, total, counts[0])
        taken = nc.values_load(unsorted[0:1, 0:1], min_val=0, max_val=1)
        with nc.If(taken != 0):
            count_edges(nc, C, "count_dst", A["dst"], cols, nb, total, counts[1])
            rank(nc, C, "rank_dst", A["dst"], cols, nb, pos_a, total, counts[1])
            to_destination_order(nc, C, A, pos_a, pos_b, attr0_a, attr1_a, ids_a, cols)
        with nc.Else():
            ids_in_order(nc, C, A, pos_b, ids_a, cols)
        for i, name in ((0, "dst"), (1, "src")):
            group_table(nc, C, f"groups_{name}", counts[1 - i], nb, n_edges, ng, meta[i], tables[i], last[i])
            table_ints(nc, name, nb, tables[i], row0[i], node0[i])
        before_gnn0(nc, C, A["x"], A["attr"], Wn, nb, x1, base)
        edges_gnn0(nc, C, unsorted, A["attr0"], attr0_a, ids_a, x1, tables[0], row0[0], Wn, ng, agg0)
        between(nc, C, agg0, last[0], base, A["attr"], Wn, nb, x2, mixed)
        to_source_order(nc, C, unsorted, A["attr1"], attr1_a, ids_a, mixed, tables[0], row0[0], node0[0], Wn, ng, n_edges,
                        rows_b)
        edges_gnn1(nc, C, rows_b, tables[1], row0[1], Wn, ng, agg1)
        after_gnn1(nc, C, agg1, last[1], x2, mixed, Wn, nb, out)


WEIGHTS = ["L0_gnn_" + s for s in ("Ws_sc_a", "Wv_sc_a", "Ws_sc_c", "Wv_sc_c", "Ws_l1_a", "Wv_l1_a", "Ws_l1_c", "Wv_l1_c",
                                   "W_fc1", "W_fc2", "Ws_l2_a", "Wv_l2_a", "Ws_l2_c", "Wv_l2_c", "Ws_l3", "Wv_l3")] \
    + ["L1_gnn_" + s for s in ("W_skip0", "W_skip1", "W_nl0", "W_nl1", "W_fc1", "W_fc2", "W_out_s", "W_out_v")]


def kernel(**inputs):
    import numpy as np
    import concourse.bacc as bacc
    from concourse.bass_utils import run_bass_kernel_spmd

    n, e = inputs["x"].shape[0], inputs["src"].shape[0]
    nb, e_pad = blocks_of(n), P * columns_of(e)

    def padded(a, rows, value):
        return np.concatenate([a, np.full((rows - a.shape[0],) + a.shape[1:], value, a.dtype)])

    x = np.asarray(inputs["x"])
    x = np.concatenate([x[:, :MS], x[:, MS:].reshape(n, MV, 3).transpose(0, 2, 1).reshape(n, 3 * MV)], axis=1)
    attr0 = np.concatenate([np.asarray(inputs[s]) for s in ("edge_attr_10", "edge_attr_4")], axis=1)
    attr1 = np.concatenate([np.asarray(inputs[s]) for s in ("edge_attr_3", "edge_attr_64")], axis=1)
    attr = np.concatenate([np.asarray(inputs[s]) for s in ("node_vec1", "node_vec1_n2", "node_vec1_n3")], axis=1)
    arrays = {"x": padded(x, nb * P, 0), "attr": padded(attr, nb * P, 0),
              "attr0": padded(attr0, e_pad, 1), "attr1": padded(attr1, e_pad, 1),
              "src": padded(np.asarray(inputs["src"]), e_pad, nb * P),
              "dst": padded(np.asarray(inputs["dst"]), e_pad, (nb + 1) * P)}
    for s in WEIGHTS:
        arrays[s] = np.asarray(inputs[s])
    nc = bacc.Bacc("TRN2", target_bir_lowering=False, num_devices=1)
    aps = {s: nc.dram_tensor("in_" + s, v.shape, mybir.dt.from_np(v.dtype), kind="ExternalInput").ap() for s, v in arrays.items()}
    out = nc.dram_tensor("out", (nb * P, D), F32, kind="ExternalOutput").ap()
    program(nc, n, e, aps, aps, out)
    r = run_bass_kernel_spmd(nc, [{"in_" + s: np.ascontiguousarray(v) for s, v in arrays.items()}], core_ids=[0])
    y = r.results[0]["out"][:n]
    return np.concatenate([y[:, :MS], y[:, MS:].reshape(n, 3, MV).transpose(0, 2, 1).reshape(n, 3 * MV)], axis=1)
```
